# Optimizing a Trainium2 kernel written in Bass

```python
import numpy as np
import jax
import jax.numpy as jnp

def _softmax(x, axis=-1):
    return jax.nn.softmax(x, axis=axis)

def _gelu(x):
    return jax.nn.gelu(x, approximate=True)

def _silu(x):
    return jax.nn.silu(x)

def _sigmoid(x):
    return jax.nn.sigmoid(x)

def _layernorm(x, axis=-1, eps=1e-05):
    m = jnp.mean(x, axis=axis, keepdims=True)
    v = jnp.var(x, axis=axis, keepdims=True)
    return (x - m) / jnp.sqrt(v + eps)

def _scatter_add(tgt, idx, src, axis=0):
    return tgt.at[idx].add(src)

def _segment_sum(src, seg, n):
    return jax.ops.segment_sum(src, seg, n)
kernel_name = 'mk_seq_preln_d2_jaxref_r8_d9a99d'

def setup_inputs(seed: int=0):
    np.random.seed(seed)
    _w = jnp.asarray

    def _L0_attn_setup():
        import jax, jax.numpy as jnp
        import numpy as np
        EMBED_DIM = 128
        NUM_HEADS = 16
        HEAD_DIM = EMBED_DIM // NUM_HEADS
        WINDOW = 64
        SEQ = 256
        BATCH = 2
        key = jax.random.key(seed)
        ks = jax.random.split(key, 5)
        s = 0.02
        x = jax.random.normal(ks[0], (BATCH, SEQ, EMBED_DIM), dtype=jnp.float32)
        Wq = jax.random.normal(ks[1], (EMBED_DIM, EMBED_DIM), dtype=jnp.float32) * s
        Wk = jax.random.normal(ks[2], (EMBED_DIM, EMBED_DIM), dtype=jnp.float32) * s
        Wv = jax.random.normal(ks[3], (EMBED_DIM, EMBED_DIM), dtype=jnp.float32) * s
        Wo = jax.random.normal(ks[4], (EMBED_DIM, EMBED_DIM), dtype=jnp.float32) * s
        return {'x': x, 'Wq': Wq, 'Wk': Wk, 'Wv': Wv, 'Wo': Wo}
    _L0_attn_in = _L0_attn_setup()

    def _L0_ffn_setup():
        import jax, jax.numpy as jnp
        import numpy as np
        from jax import lax
        H, DK, DV, N_EXP, CHUNK = (8, 64, 64, 4, 64)
        LORA, GATE_LR = (64, 16)
        NORMALIZER = 16.0
        EPS = 1e-05

        def chunk_gla(q, k, v, gk, C=CHUNK):
            L, h, dk = q.shape
            dv = v.shape[-1]
            nc = L // C
            qc, kc, vc, gc = (t.reshape(nc, C, h, -1) for t in (q, k, v, gk))
            g = jnp.cumsum(gc, axis=1)
            g_last = g[:, -1]
            qg = qc * jnp.exp(g)
            kg = kc * jnp.exp(-g)
            A = jnp.einsum('cthd,cshd->chts', qg, kg)
            A = A * jnp.tril(jnp.ones((C, C), q.dtype))
            o_intra = jnp.einsum('chts,cshe->cthe', A, vc)
            k_out = kc * jnp.exp(g_last[:, None] - g)
            chunk_kv = jnp.einsum('cthd,cthe->chde', k_out, vc)
            decay = jnp.exp(g_last)

            def step(S, inp):
                kv, dec, qg_c = inp
                o_inter = jnp.einsum('thd,hde->the', qg_c, S)
                return (S * dec[..., None] + kv, o_inter)
            S0 = jnp.zeros((h, dk, dv), q.dtype)
            _, o_inter = lax.scan(step, S0, (chunk_kv, decay, qg))
            return (o_intra + o_inter).reshape(L, h, dv)
        key = jax.random.key(seed)
        ks = jax.random.split(key, 20)
        B, L, Dh = (1, 512, 128)
        KD, VD = (H * DK, H * DV)
        w = lambda i, shape: jax.random.normal(ks[i], shape, jnp.float32) * 0.02
        return {'x': jax.random.normal(ks[0], (B, L, Dh), jnp.float32), 'Wq': w(1, (Dh, KD)), 'Wk': w(2, (Dh, KD)), 'Wv': w(3, (Dh, VD)), 'Wqa': w(4, (Dh, LORA)), 'Wqb': w(5, (LORA, KD)), 'Wka': w(6, (Dh, LORA)), 'Wkb': w(7, (LORA, KD)), 'Wg1a': w(8, (Dh, GATE_LR)), 'Wg1b': w(9, (GATE_LR, KD)), 'bg1': jnp.zeros((KD,), jnp.float32), 'Wg2a': w(10, (Dh, GATE_LR)), 'Wg2b': w(11, (GATE_LR, KD)), 'bg2': jnp.zeros((KD,), jnp.float32), 'We': w(12, (Dh, N_EXP)), 'Wga': w(13, (Dh, LORA)), 'Wgb': w(14, (LORA, VD)), 'norm_w': jnp.ones((DV,), jnp.float32), 'Wo': w(15, (VD, Dh))}
    _L0_ffn_in = _L0_ffn_setup()

    def _L1_attn_setup():
        import jax, jax.numpy as jnp
        import numpy as np
        B, L, D, H = (1, 256, 128, 16)
        d = D // H

        def _forward(x, Wqkv_w, Wqkv_b, out_w, out_b, W_static, Lambda_raw, Gamma, gate_w1, gate_b1, gate_w2, gate_b2):
            Bb, Ll, Dm = x.shape
            Hh = Gamma.shape[0]
            dd = Dm // Hh
            scale = 1.0 / np.sqrt(dd)
            qkv = (x @ Wqkv_w + Wqkv_b).reshape(Bb, Ll, 3, Hh, dd)
            q = jnp.transpose(qkv[:, :, 0], (0, 2, 1, 3))
            k = jnp.transpose(qkv[:, :, 1], (0, 2, 1, 3))
            v = jnp.transpose(qkv[:, :, 2], (0, 2, 1, 3))
            scores = jnp.einsum('bhid,bhjd->bhij', q, k) * scale
            causal_mask = jnp.triu(jnp.full((Ll, Ll), -10000.0, dtype=scores.dtype), 1)
            attn = jax.nn.softmax(scores + causal_mask, axis=-1)
            y_softmax = jnp.einsum('bhij,bhjd->bhid', attn, v)
            retention = 1.0 - jax.nn.sigmoid(Lambda_raw)
            k_stp = k * scale

            def step(state, inp):
                q_t, k_t, v_t = inp
                hebbian = v_t[..., :, None] * k_t[..., None, :]
                state = retention * state + Gamma * hebbian
                y_t = jnp.einsum('bhij,bhj->bhi', W_static + state, q_t)
                return (state, y_t)
            state0 = jnp.zeros((Bb, Hh, dd, dd), x.dtype)
            qT = jnp.moveaxis(q, 2, 0)
            kT = jnp.moveaxis(k_stp, 2, 0)
            vT = jnp.moveaxis(v, 2, 0)
            _, ys = jax.lax.scan(step, state0, (qT, kT, vT))
            y_stp = jnp.moveaxis(ys, 0, 2)
            g = jax.nn.gelu(x @ gate_w1 + gate_b1, approximate=False)
            alpha = jax.nn.sigmoid(g @ gate_w2 + gate_b2)
            alpha = jnp.transpose(alpha, (0, 2, 1))[..., None]
            y = alpha * y_softmax + (1.0 - alpha) * y_stp
            y = jnp.transpose(y, (0, 2, 1, 3)).reshape(Bb, Ll, Dm)
            return y @ out_w + out_b
        key = jax.random.key(seed)
        ks = jax.random.split(key, 8)
        s = 1.0 / np.sqrt(D)
        return {'x': jax.random.normal(ks[0], (B, L, D), jnp.float32), 'Wqkv_w': jax.random.normal(ks[1], (D, 3 * D), jnp.float32) * s, 'Wqkv_b': jnp.zeros((3 * D,), jnp.float32), 'out_w': jax.random.normal(ks[2], (D, D), jnp.float32) * s, 'out_b': jnp.zeros((D,), jnp.float32), 'W_static': jnp.zeros((H, d, d), jnp.float32), 'Lambda_raw': jax.random.uniform(ks[3], (H, d, d), jnp.float32, -3.0, 3.0), 'Gamma': jax.random.uniform(ks[4], (H, d, d), jnp.float32, -0.5 / np.sqrt(d), 0.5 / np.sqrt(d)), 'gate_w1': jax.random.normal(ks[5], (D, D // 2), jnp.float32) * s, 'gate_b1': jnp.zeros((D // 2,), jnp.float32), 'gate_w2': jax.random.normal(ks[6], (D // 2, H), jnp.float32) * (1.0 / np.sqrt(D // 2)), 'gate_b2': jnp.zeros((H,), jnp.float32)}
    _L1_attn_in = _L1_attn_setup()

    def _L1_ffn_setup():
        import jax, jax.numpy as jnp
        import numpy as np
        DIM = 128
        MOE_HID = 64
        SHARED_HID = 256
        N_EXPERTS = 16
        TOP_K = 2
        NORM_TOPK_PROB = True
        key = jax.random.key(seed)
        ks = jax.random.split(key, 9)
        s = 0.02
        x = jax.random.normal(ks[0], (2, 128, DIM), dtype=jnp.float32)
        Wg = jax.random.normal(ks[1], (N_EXPERTS, DIM), dtype=jnp.float32) * s
        We_gate = jax.random.normal(ks[2], (N_EXPERTS, MOE_HID, DIM), dtype=jnp.float32) * s
        We_up = jax.random.normal(ks[3], (N_EXPERTS, MOE_HID, DIM), dtype=jnp.float32) * s
        We_down = jax.random.normal(ks[4], (N_EXPERTS, DIM, MOE_HID), dtype=jnp.float32) * s
        Ws_gate = jax.random.normal(ks[5], (SHARED_HID, DIM), dtype=jnp.float32) * s
        Ws_up = jax.random.normal(ks[6], (SHARED_HID, DIM), dtype=jnp.float32) * s
        Ws_down = jax.random.normal(ks[7], (DIM, SHARED_HID), dtype=jnp.float32) * s
        Wsg = jax.random.normal(ks[8], (1, DIM), dtype=jnp.float32) * s
        return {'x': x, 'Wg': Wg, 'We_gate': We_gate, 'We_up': We_up, 'We_down': We_down, 'Ws_gate': Ws_gate, 'Ws_up': Ws_up, 'Ws_down': Ws_down, 'Wsg': Wsg}
    _L1_ffn_in = _L1_ffn_setup()
    _d = {'L0_attn_x': _L0_attn_in['x'], 'L0_attn_Wq': _L0_attn_in['Wq'], 'L0_attn_Wk': _L0_attn_in['Wk'], 'L0_attn_Wv': _L0_attn_in['Wv'], 'L0_attn_Wo': _L0_attn_in['Wo'], 'L0_ffn_Wq': _L0_ffn_in['Wq'], 'L0_ffn_Wk': _L0_ffn_in['Wk'], 'L0_ffn_Wv': _L0_ffn_in['Wv'], 'L0_ffn_Wqa': _L0_ffn_in['Wqa'], 'L0_ffn_Wqb': _L0_ffn_in['Wqb'], 'L0_ffn_Wka': _L0_ffn_in['Wka'], 'L0_ffn_Wkb': _L0_ffn_in['Wkb'], 'L0_ffn_Wg1a': _L0_ffn_in['Wg1a'], 'L0_ffn_Wg1b': _L0_ffn_in['Wg1b'], 'L0_ffn_bg1': _L0_ffn_in['bg1'], 'L0_ffn_Wg2a': _L0_ffn_in['Wg2a'], 'L0_ffn_Wg2b': _L0_ffn_in['Wg2b'], 'L0_ffn_bg2': _L0_ffn_in['bg2'], 'L0_ffn_We': _L0_ffn_in['We'], 'L0_ffn_Wga': _L0_ffn_in['Wga'], 'L0_ffn_Wgb': _L0_ffn_in['Wgb'], 'L0_ffn_norm_w': _L0_ffn_in['norm_w'], 'L0_ffn_Wo': _L0_ffn_in['Wo'], 'L1_attn_Wqkv_w': _L1_attn_in['Wqkv_w'], 'L1_attn_Wqkv_b': _L1_attn_in['Wqkv_b'], 'L1_attn_out_w': _L1_attn_in['out_w'], 'L1_attn_out_b': _L1_attn_in['out_b'], 'L1_attn_W_static': _L1_attn_in['W_static'], 'L1_attn_Lambda_raw': _L1_attn_in['Lambda_raw'], 'L1_attn_Gamma': _L1_attn_in['Gamma'], 'L1_attn_gate_w1': _L1_attn_in['gate_w1'], 'L1_attn_gate_b1': _L1_attn_in['gate_b1'], 'L1_attn_gate_w2': _L1_attn_in['gate_w2'], 'L1_attn_gate_b2': _L1_attn_in['gate_b2'], 'L1_ffn_Wg': _L1_ffn_in['Wg'], 'L1_ffn_We_gate': _L1_ffn_in['We_gate'], 'L1_ffn_We_up': _L1_ffn_in['We_up'], 'L1_ffn_We_down': _L1_ffn_in['We_down'], 'L1_ffn_Ws_gate': _L1_ffn_in['Ws_gate'], 'L1_ffn_Ws_up': _L1_ffn_in['Ws_up'], 'L1_ffn_Ws_down': _L1_ffn_in['Ws_down'], 'L1_ffn_Wsg': _L1_ffn_in['Wsg']}
    _x0 = _d['L0_attn_x']
    _d['L0_attn_x'] = jax.random.normal(jax.random.fold_in(jax.random.key(seed), 1), (4, 1024, 128), dtype=_x0.dtype)
    del _x0
    return _d

def reference(L0_attn_x, L0_attn_Wq, L0_attn_Wk, L0_attn_Wv, L0_attn_Wo, L0_ffn_Wq, L0_ffn_Wk, L0_ffn_Wv, L0_ffn_Wqa, L0_ffn_Wqb, L0_ffn_Wka, L0_ffn_Wkb, L0_ffn_Wg1a, L0_ffn_Wg1b, L0_ffn_bg1, L0_ffn_Wg2a, L0_ffn_Wg2b, L0_ffn_bg2, L0_ffn_We, L0_ffn_Wga, L0_ffn_Wgb, L0_ffn_norm_w, L0_ffn_Wo, L1_attn_Wqkv_w, L1_attn_Wqkv_b, L1_attn_out_w, L1_attn_out_b, L1_attn_W_static, L1_attn_Lambda_raw, L1_attn_Gamma, L1_attn_gate_w1, L1_attn_gate_b1, L1_attn_gate_w2, L1_attn_gate_b2, L1_ffn_Wg, L1_ffn_We_gate, L1_ffn_We_up, L1_ffn_We_down, L1_ffn_Ws_gate, L1_ffn_Ws_up, L1_ffn_Ws_down, L1_ffn_Wsg):

    def _L0_attn_ref(x, Wq, Wk, Wv, Wo):
        import jax, jax.numpy as jnp
        import numpy as np
        EMBED_DIM = 128
        NUM_HEADS = 16
        HEAD_DIM = EMBED_DIM // NUM_HEADS
        WINDOW = 64
        SEQ = 256
        BATCH = 2
        b, s, _ = x.shape
        scale = 1.0 / np.sqrt(HEAD_DIM)
        q = (x @ Wq.T).reshape(b, s, NUM_HEADS, HEAD_DIM)
        k = (x @ Wk.T).reshape(b, s, NUM_HEADS, HEAD_DIM)
        v = (x @ Wv.T).reshape(b, s, NUM_HEADS, HEAD_DIM)
        attn = jnp.einsum('bqhd,bkhd->bhqk', q, k) * scale
        i = jnp.arange(s)[:, None]
        j = jnp.arange(s)[None, :]
        allowed = (j <= i) & (j > i - WINDOW)
        attn = jnp.where(allowed, attn, -jnp.inf)
        attn = jax.nn.softmax(attn.astype(jnp.float32), axis=-1).astype(q.dtype)
        out = jnp.einsum('bhqk,bkhd->bqhd', attn, v).reshape(b, s, EMBED_DIM)
        return out @ Wo.T

    def _L0_ffn_ref(x, Wq, Wk, Wv, Wqa, Wqb, Wka, Wkb, Wg1a, Wg1b, bg1, Wg2a, Wg2b, bg2, We, Wga, Wgb, norm_w, Wo):
        import jax, jax.numpy as jnp
        import numpy as np
        from jax import lax
        H, DK, DV, N_EXP, CHUNK = (8, 64, 64, 4, 64)
        LORA, GATE_LR = (64, 16)
        NORMALIZER = 16.0
        EPS = 1e-05

        def chunk_gla(q, k, v, gk, C=CHUNK):
            L, h, dk = q.shape
            dv = v.shape[-1]
            nc = L // C
            qc, kc, vc, gc = (t.reshape(nc, C, h, -1) for t in (q, k, v, gk))
            g = jnp.cumsum(gc, axis=1)
            g_last = g[:, -1]
            qg = qc * jnp.exp(g)
            kg = kc * jnp.exp(-g)
            A = jnp.einsum('cthd,cshd->chts', qg, kg)
            A = A * jnp.tril(jnp.ones((C, C), q.dtype))
            o_intra = jnp.einsum('chts,cshe->cthe', A, vc)
            k_out = kc * jnp.exp(g_last[:, None] - g)
            chunk_kv = jnp.einsum('cthd,cthe->chde', k_out, vc)
            decay = jnp.exp(g_last)

            def step(S, inp):
                kv, dec, qg_c = inp
                o_inter = jnp.einsum('thd,hde->the', qg_c, S)
                return (S * dec[..., None] + kv, o_inter)
            S0 = jnp.zeros((h, dk, dv), q.dtype)
            _, o_inter = lax.scan(step, S0, (chunk_kv, decay, qg))
            return (o_intra + o_inter).reshape(L, h, dv)
        B, L, Dh = x.shape
        scale = DK ** (-0.5)
        q1 = (x @ Wq).reshape(B, L, H, DK) * scale
        k1 = (x @ Wk).reshape(B, L, H, DK)
        v = (x @ Wv).reshape(B, L, H, DV)
        q2 = (x @ Wqa @ Wqb).reshape(B, L, H, DK) * scale
        k2 = jax.nn.softmax((x @ Wka @ Wkb).reshape(B, L, H, DK), axis=-1)
        gk1 = (jax.nn.log_sigmoid(x @ Wg1a @ Wg1b + bg1) / NORMALIZER).reshape(B, L, H, DK)
        gk2 = (jax.nn.log_sigmoid(x @ Wg2a @ Wg2b + bg2) / NORMALIZER).reshape(B, L, H, DK)
        e = jax.nn.softmax(x @ We, axis=-1)
        _, idx = lax.top_k(e, 1)
        mask = jax.nn.one_hot(idx, N_EXP, dtype=x.dtype).sum(-2)
        rw = e * mask
        fac = jnp.swapaxes(rw, 1, 2)[:, :, :, None, None]
        mfac = jnp.swapaxes(mask, 1, 2)[:, :, :, None, None]
        q_e = q2[:, None] * fac
        k_e = k2[:, None] * fac
        gk_e = gk2[:, None] * mfac
        gla_b = jax.vmap(chunk_gla)
        o_dense = gla_b(q1, k1, v, gk1)
        gla_be = jax.vmap(jax.vmap(chunk_gla, in_axes=(0, 0, None, 0)))
        o_sparse = gla_be(q_e, k_e, v, gk_e).sum(axis=1)
        o = o_dense + o_sparse
        g = (x @ Wga @ Wgb).reshape(B, L, H, DV)
        o = o * lax.rsqrt(jnp.mean(o * o, axis=-1, keepdims=True) + EPS) * norm_w
        o = o * (g * jax.nn.sigmoid(g))
        return o.reshape(B, L, H * DV) @ Wo

    def _L1_attn_ref(x, Wqkv_w, Wqkv_b, out_w, out_b, W_static, Lambda_raw, Gamma, gate_w1, gate_b1, gate_w2, gate_b2):
        import jax, jax.numpy as jnp
        import numpy as np
        B, L, D, H = (1, 256, 128, 16)
        d = D // H

        def _forward(x, Wqkv_w, Wqkv_b, out_w, out_b, W_static, Lambda_raw, Gamma, gate_w1, gate_b1, gate_w2, gate_b2):
            Bb, Ll, Dm = x.shape
            Hh = Gamma.shape[0]
            dd = Dm // Hh
            scale = 1.0 / np.sqrt(dd)
            qkv = (x @ Wqkv_w + Wqkv_b).reshape(Bb, Ll, 3, Hh, dd)
            q = jnp.transpose(qkv[:, :, 0], (0, 2, 1, 3))
            k = jnp.transpose(qkv[:, :, 1], (0, 2, 1, 3))
            v = jnp.transpose(qkv[:, :, 2], (0, 2, 1, 3))
            scores = jnp.einsum('bhid,bhjd->bhij', q, k) * scale
            causal_mask = jnp.triu(jnp.full((Ll, Ll), -10000.0, dtype=scores.dtype), 1)
            attn = jax.nn.softmax(scores + causal_mask, axis=-1)
            y_softmax = jnp.einsum('bhij,bhjd->bhid', attn, v)
            retention = 1.0 - jax.nn.sigmoid(Lambda_raw)
            k_stp = k * scale

            def step(state, inp):
                q_t, k_t, v_t = inp
                hebbian = v_t[..., :, None] * k_t[..., None, :]
                state = retention * state + Gamma * hebbian
                y_t = jnp.einsum('bhij,bhj->bhi', W_static + state, q_t)
                return (state, y_t)
            state0 = jnp.zeros((Bb, Hh, dd, dd), x.dtype)
            qT = jnp.moveaxis(q, 2, 0)
            kT = jnp.moveaxis(k_stp, 2, 0)
            vT = jnp.moveaxis(v, 2, 0)
            _, ys = jax.lax.scan(step, state0, (qT, kT, vT))
            y_stp = jnp.moveaxis(ys, 0, 2)
            g = jax.nn.gelu(x @ gate_w1 + gate_b1, approximate=False)
            alpha = jax.nn.sigmoid(g @ gate_w2 + gate_b2)
            alpha = jnp.transpose(alpha, (0, 2, 1))[..., None]
            y = alpha * y_softmax + (1.0 - alpha) * y_stp
            y = jnp.transpose(y, (0, 2, 1, 3)).reshape(Bb, Ll, Dm)
            return y @ out_w + out_b
        return _forward(x, Wqkv_w, Wqkv_b, out_w, out_b, W_static, Lambda_raw, Gamma, gate_w1, gate_b1, gate_w2, gate_b2)

    def _L1_ffn_ref(x, Wg, We_gate, We_up, We_down, Ws_gate, Ws_up, Ws_down, Wsg):
        import jax, jax.numpy as jnp
        import numpy as np
        DIM = 128
        MOE_HID = 64
        SHARED_HID = 256
        N_EXPERTS = 16
        TOP_K = 2
        NORM_TOPK_PROB = True
        B, S, D = x.shape
        xt = x.reshape(-1, D)
        gates = jax.nn.softmax(xt @ Wg.T, axis=-1)
        scores, inds = jax.lax.top_k(gates, TOP_K)
        if NORM_TOPK_PROB:
            scores = scores / jnp.sum(scores, axis=-1, keepdims=True)
        g = jnp.einsum('td,ehd->teh', xt, We_gate)
        u = jnp.einsum('td,ehd->teh', xt, We_up)
        h = jax.nn.silu(g) * u
        y_all = jnp.einsum('teh,edh->ted', h, We_down)
        y_sel = jnp.take_along_axis(y_all, inds[:, :, None], axis=1)
        y = jnp.sum(y_sel * scores[:, :, None], axis=1)
        shared = jax.nn.silu(xt @ Ws_gate.T) * (xt @ Ws_up.T) @ Ws_down.T
        y = y + jax.nn.sigmoid(xt @ Wsg.T) * shared
        return y.reshape(B, S, D)
    x = L0_attn_x
    x = x + _L0_attn_ref(_layernorm(x, axis=-1), L0_attn_Wq, L0_attn_Wk, L0_attn_Wv, L0_attn_Wo)
    x = x + _L0_ffn_ref(_layernorm(x, axis=-1), L0_ffn_Wq, L0_ffn_Wk, L0_ffn_Wv, L0_ffn_Wqa, L0_ffn_Wqb, L0_ffn_Wka, L0_ffn_Wkb, L0_ffn_Wg1a, L0_ffn_Wg1b, L0_ffn_bg1, L0_ffn_Wg2a, L0_ffn_Wg2b, L0_ffn_bg2, L0_ffn_We, L0_ffn_Wga, L0_ffn_Wgb, L0_ffn_norm_w, L0_ffn_Wo)
    x = x + _L1_attn_ref(_layernorm(x, axis=-1), L1_attn_Wqkv_w, L1_attn_Wqkv_b, L1_attn_out_w, L1_attn_out_b, L1_attn_W_static, L1_attn_Lambda_raw, L1_attn_Gamma, L1_attn_gate_w1, L1_attn_gate_b1, L1_attn_gate_w2, L1_attn_gate_b2)
    x = x + _L1_ffn_ref(_layernorm(x, axis=-1), L1_ffn_Wg, L1_ffn_We_gate, L1_ffn_We_up, L1_ffn_We_down, L1_ffn_Ws_gate, L1_ffn_Ws_up, L1_ffn_Ws_down, L1_ffn_Wsg)
    return x

_drawn_inputs = setup_inputs


def setup_inputs(seed=0):
    import zlib

    import numpy as np

    out = dict(_drawn_inputs(seed))
    spreads = {'L0_ffn_bg1': (0.0, 0.8),
     'L0_ffn_bg2': (0.0, 0.8),
     'L0_ffn_norm_w': (1.0, 0.6),
     'L1_attn_Wqkv_b': (0.0, 0.1),
     'L1_attn_out_b': (0.0, 0.1),
     'L1_attn_W_static': (0.0, 0.1),
     'L1_attn_gate_b1': (0.0, 0.8),
     'L1_attn_gate_b2': (0.0, 0.8)}
    factors = {'L0_attn_Wq': 8.0,
     'L0_attn_Wk': 8.0,
     'L0_attn_Wv': 7.525,
     'L0_attn_Wo': 7.413,
     'L0_ffn_Wq': 6.615,
     'L0_ffn_Wk': 6.63,
     'L0_ffn_Wv': 6.605,
     'L0_ffn_Wqa': 8.0,
     'L0_ffn_Wqb': 8.0,
     'L0_ffn_Wka': 8.0,
     'L0_ffn_Wkb': 8.0,
     'L0_ffn_Wg1a': 8.0,
     'L0_ffn_Wg1b': 8.0,
     'L0_ffn_Wg2a': 8.0,
     'L0_ffn_Wg2b': 8.0,
     'L0_ffn_We': 8.0,
     'L0_ffn_Wga': 6.644,
     'L0_ffn_Wgb': 6.567,
     'L0_ffn_Wo': 6.622,
     'L1_ffn_Wg': 8.0,
     'L1_ffn_We_gate': 8.0,
     'L1_ffn_We_up': 8.0,
     'L1_ffn_We_down': 8.0,
     'L1_ffn_Ws_gate': 8.0,
     'L1_ffn_Ws_up': 8.0,
     'L1_ffn_Ws_down': 8.0,
     'L1_ffn_Wsg': 8.0}
    for name, (base, spread) in spreads.items():
        noise = np.random.default_rng([zlib.crc32(name.encode()), seed]).standard_normal(out[name].shape)
        drawn = base * np.exp(spread * noise) if base else spread * noise
        out[name] = jnp.asarray(drawn.astype(out[name].dtype))
    for name, factor in factors.items():
        out[name] = (out[name] * factor).astype(out[name].dtype)
    return out
```

```python
from contextlib import ExitStack

import numpy as np

import concourse.bass as bass
from concourse import mybir

ALU = mybir.AluOpType
ACT = mybir.ActivationFunctionType
AX = mybir.AxisListType
F32 = mybir.dt.float32
BF16 = mybir.dt.bfloat16

P = 128
BANK = 512
EPS = 1e-5
HEADS, HD = 16, 8
GROUP = 4
WINDOW = 64
GLA_HEADS, GLA_D = 8, 64
PAIRS = GLA_HEADS // 2
GLA_CHUNK = 64
ROUTES = 4
EXPERTS, EXPERT_HID, SHARED_HID = 16, 64, 256
MOE_TILES = (EXPERTS * EXPERT_HID + SHARED_HID) // P
NORMALIZER = 16.0
SPLIT = 3
NEG_ROW = 96
ATT_SCALE = float(1.0 / np.sqrt(HD))


def flat(tokens):
    for t in tokens:
        if isinstance(t, list):
            yield from flat(t)
        elif t is not None:
            yield t


class Lane:

    def __init__(self, eng, sem, one_by_one=False):
        self.eng, self.sem, self.count, self.seen, self.held = eng, sem, 0, {}, []
        self.one_by_one = one_by_one

    def wait(self, after):
        need = {}
        held, self.held = self.held, []
        for lane, value in flat([list(after), held]):
            if value > self.seen.get(lane, 0):
                need[lane] = max(need.get(lane, 0), value)
        self.seen.update(need)
        for lane, value in need.items():
            self.eng.wait_ge(lane.sem, value)

    def do(self, op, after=()):
        if self.one_by_one:
            after = [list(after), [(self, self.count)]]
        self.wait(after)
        op(self.eng).then_inc(self.sem, 1)
        self.count += 1
        return (self, self.count)


class Channel:

    def __init__(self, sem):
        self.sem, self.count = sem, 0


class Slot:

    def __init__(self, ring, ap, after):
        self.ring, self.ap, self.after = ring, ap, after

    def done(self, *tokens):
        self.ring.free.append((self.ap, list(tokens)))


class Ring:
    def __init__(self, buffers):
        self.free = [(b, []) for b in buffers]

    def take(self):
        ap, after = self.free.pop(0)
        return Slot(self, ap, after)


def constant_columns():
    r = np.arange(P)[:, None]
    c = np.arange(P)[None, :]
    w = np.arange(P + WINDOW)[None, :]
    mid = (r < GLA_CHUNK) * np.ones((1, 1))
    out = {
        "ident": r == c,
        "eps": np.full((P, 1), EPS),
        "win_row": ~((w > r) & (w <= r + WINDOW)) * -(2.0 ** 60),
        "win_col": ~((w >= r) & (w < r + WINDOW)) * -(2.0 ** 60),
        "causal_row": (c > r) * -100.0,
        "causal_col": (r > c) * -100.0,
        "tril": (r <= c) * 1.0,
        "gate_sum": np.concatenate([(r <= c) * 1.0 - mid, 1 - mid, mid], 1) / NORMALIZER,
        "half": np.concatenate([1 - mid, mid], 1) / NORMALIZER,
        "head_mean": (r // GLA_D == c // GLA_D) / GLA_D,
        "route_first": (r < ROUTES) * 1.0,
        "ones": np.ones((P, 1)),
    }
    part_rows = SPLIT * ROUTES
    sel = [((r % ROUTES == e) & (r < part_rows)) * np.ones((1, P)) for e in range(ROUTES)]
    out["route_bcast"] = np.concatenate(sel, 1)
    n = EXPERTS + 1
    sel = [((r % n == np.minimum(2 * f + c // EXPERT_HID, EXPERTS)) & (r < SPLIT * n)) * 1.0
           for f in range(EXPERTS // 2 + 1)]
    sel[-1] = ((r % n == EXPERTS) & (r < SPLIT * n)) * np.ones((1, P))
    out["moe_bcast"] = np.concatenate(sel, 1)
    return {k: np.asarray(v, np.float32) for k, v in out.items()}


REGION_OF = {"k": "constants", "a": "small", "b": "large", "c": "small", "d": "large"}
ARENA = 40500

BF_CONSTANTS = ("win_row", "win_col", "causal_row", "causal_col", "route_bcast", "moe_bcast")


def build(nc, x_in, packed, x_out, place, batches, T):
    sizes = {k: a.shape[1] for k, a in packed.items()}
    region_of = REGION_OF
    NT = T // P
    HALF = min(BANK, T)
    ctx = ExitStack()
    with ctx:
        def sb(name, shape, dt=F32):
            return ctx.enter_context(nc.sbuf_tensor(name, shape, dt))

        def sem(name):
            return ctx.enter_context(nc.semaphore(name))

        pe, dv, ac = (Lane(eng, sem(f"count_{n}")) for n, eng in
                      (("tensor", nc.tensor), ("vector", nc.vector), ("scalar", nc.scalar)))
        gp = Lane(nc.gpsimd, sem("count_gpsimd"), one_by_one=True)
        sp = Lane(nc.sync, None)
        channels = [Channel(sem(f"dma_{i}")) for i in range(24)]
        turn = [0]

        def dma(out, in_, after=()):
            ch = channels[turn[0] % len(channels)]
            turn[0] += 1
            sp.wait([list(after), [(ch, ch.count)]])
            nc.sync.dma_start(out, in_).then_inc(ch.sem, 16)
            ch.count += 16
            return (ch, ch.count)

        def end_of_layer():
            every = [(lane, lane.count) for lane in (pe, dv, ac, gp)] + [(ch, ch.count) for ch in channels]
            for lane in (pe, dv, ac, gp, sp):
                lane.held = every

        regions = {r: sb(f"weights_{r}", [P, max(n for k, n in sizes.items() if region_of.get(k) == r)])
                   for r in sorted(set(region_of.values()))}

        def w(name, a=0, b=None):
            layer, first, rows, cols = place[name]
            t = low_rank if layer == "l" else regions[region_of[layer]]
            return t[0:rows, first + a:first + (cols if b is None else b)]

        arena = sb("arena", [P, ARENA])
        used = [0]

        def carve(shape, dt=F32):
            n = int(np.prod(shape[1:]))
            words = n if dt == F32 else (n + 1) // 2
            ap = arena[0:shape[0], used[0]:used[0] + words]
            used[0] += words
            assert used[0] <= ARENA, used[0]
            if dt != F32:
                ap = ap.bitcast(dt)
            if len(shape) > 2:
                names = "abcdef"[:len(shape) - 1]
                ap = ap.rearrange(f"p ({' '.join(names)}) -> p {' '.join(names)}", **dict(zip(names, shape[1:])))
            return ap

        x = sb("x", [P, batches * NT, P])
        x_ready = [None] * (batches * NT)
        psum = Ring([ctx.enter_context(nc.psum_tensor(f"psum{i}", [P, 2 * BANK], F32)) for i in range(4)])

        stats = sb("stats", [P, NT, 6])
        moments = sb("moments", [P, NT, 2])
        rstd = sb("rstd", [P, 4, NT])
        xn = Ring([sb(f"xn{i}", [P, P]) for i in range(4)])
        xnT = Ring([sb("xnT0", [P, T])])

        w3 = {n: sb(f"bf_{n}", [P, place[n][3]], BF16) for n in BF_CONSTANTS}
        ident = w("ident")
        ident_bf = {v: sb(f"ident_{i}", [P, P], BF16) for i, v in enumerate((100.0, 2.0 ** 60))}

        q_stack = carve([P, HEADS, T], BF16)
        k_stack = carve([P, HEADS, T], BF16)
        full = {s: carve([P, T]) for s in "qkv"}
        rest = carve([P, T])
        parts = Ring([carve([P, SPLIT, T], BF16) for i in range(1)])
        v_nat = carve([P, NT, HEADS, 32])
        neg_max = carve([P, NT, 2, HEADS])
        neg_parts = carve([P, NT, SPLIT, HEADS])
        neg_rest = carve([P, NT, HEADS])
        neg_bf = carve([P, NT, HEADS], BF16)
        neg_T = carve([SPLIT * HEADS, T], BF16)
        probs = Ring([carve([P, 2 * BANK]) for i in range(2)])
        o_T = carve([P, HEADS // GROUP, T])
        att = Ring([carve([P, P]) for i in range(2)])
        attT = Ring([carve([P, P]) for i in range(2)])
        inv_den = Ring([carve([P, HEADS]) for i in range(2)])

        def load(layer, after=()):
            n = sizes[layer]
            return [dma(regions[REGION_OF[layer]][:, a:min(n, a + 2048)], packed[layer][:, a:min(n, a + 2048)], after)
                    for a in range(0, n, 2048)]

        staged = arena[:, 0:sizes["s"]]
        loaded = load("k") + [dma(staged, packed["s"])] + load("a")
        x_dram = x_in.rearrange("b (n p) d -> p (b n) d", p=P)
        out_dram = x_out.rearrange("b (n p) d -> p (b n) d", p=P)
        for b in range(batches):
            t = dma(x[:, b * NT:(b + 1) * NT, :], x_dram[:, b * NT:(b + 1) * NT, :])
            for n in range(NT):
                x_ready[b * NT + n] = t

        load_b = load("b")

        ready = []
        for n in BF_CONSTANTS:
            ready.append(ac.do(lambda e, n=n: e.activation(w3[n][:, :], staged[:, place[n][1]:place[n][1] + place[n][3]], ACT.Copy), loaded))
        for v, t in ident_bf.items():
            ready.append(ac.do(lambda e, v=v, t=t: e.activation(t[:, :], ident, ACT.Copy, scale=v), loaded))
        ready += loaded
        end_of_layer()

        last_norm = [[]]

        def layer_norm(b):
            got = []
            for n in range(NT):
                t = dv.do(lambda e, n=n: e.bn_stats(stats[:, n, :], x[:, b * NT + n, :]),
                          [x_ready[b * NT + n], last_norm[0]])
                got.append(dv.do(lambda e, n=n: e.bn_aggr(moments[:, n, :], stats[:, n, :]), [t, last_norm[0]]))
            t = ac.do(lambda e: e.activation(rstd[:, 0, :], moments[:, :, 1], ACT.Ln, bias=w("eps")),
                      got + last_norm[0] + ready)
            t = ac.do(lambda e: e.activation(rstd[:, 1, :], rstd[:, 0, :], ACT.Exp, scale=-0.5), [t])
            t = dv.do(lambda e: e.tensor_tensor(rstd[:, 2, :], rstd[:, 1, :], rstd[:, 1, :], ALU.mult), [t])
            t = dv.do(lambda e: e.scalar_tensor_tensor(rstd[:, 0, :], moments[:, :, 1], EPS, rstd[:, 2, :],
                                                       ALU.add, ALU.mult), [t])
            t = dv.do(lambda e: e.tensor_scalar(rstd[:, 2, :], rstd[:, 0, :], -0.5, 1.5, ALU.mult, ALU.add), [t])
            t_r = dv.do(lambda e: e.tensor_tensor(rstd[:, 3, :], rstd[:, 1, :], rstd[:, 2, :], ALU.mult), [t])
            out = xnT.take()
            ends, norms = [], []
            for n0 in range(0, NT, 4):
                ps = psum.take()
                k = min(4, NT - n0)
                turned = []
                for n in range(n0, n0 + k):
                    s = xn.take()
                    t = dv.do(lambda e, n=n, s=s: e.tensor_scalar(
                        s.ap[:, :], x[:, b * NT + n, :], moments[:, n, 0:1], rstd[:, 3, n:n + 1],
                        ALU.subtract, ALU.mult), [t_r, s.after])
                    norms.append(t)
                    t = pe.do(lambda e, n=n, s=s, ps=ps, n0=n0: e.transpose(
                        ps.ap[:, (n - n0) * P:(n - n0 + 1) * P], s.ap[:, :], ident), [t, ps.after, ready])
                    s.done(t)
                    turned.append(t)
                t = ac.do(lambda e, ps=ps, n0=n0, k=k: e.activation(
                    out.ap[:, n0 * P:(n0 + k) * P], ps.ap[:, 0:k * P], ACT.Copy), [turned, out.after])
                ps.done(t)
                ends.append(t)
            last_norm[0] = norms
            return out, ends

        def blocks(n):
            return [(a, min(a + BANK, n)) for a in range(0, n, BANK)]

        scratch = {s: nc.dram_tensor(f"scratch_{s}", (SPLIT, P, T), BF16, kind="Internal").ap() for s in "qk"}
        whole = {s: nc.dram_tensor(f"whole_{s}", (P, T), F32, kind="Internal").ap() for s in "qk"}
        whole_free = [[]]
        ones_bf = rest[0:SPLIT, 0:T // 2].bitcast(BF16)

        def clear_attention():
            got = [gp.do(lambda e, s=s: e.memset(s[64:P, :, :], 0.0)) for s in (q_stack, k_stack)]
            t = gp.do(lambda e: e.memset(ones_bf[:, :], 1.0))
            for h in range(HEADS):
                got.append(dma(k_stack[NEG_ROW:NEG_ROW + SPLIT, h, :], ones_bf[:, :], [t] + got[0:2]))
            t = gp.do(lambda e: e.memset(v_nat[:, :, :, :], 0.0))
            got.append(gp.do(lambda e: e.memset(v_nat[:, :, :, HD:HD + 1], 1.0), [t]))
            return got

        stack_free = [[]]
        full_free = {s: [] for s in "qkv"}
        scratch_free = {s: [] for s in "qk"}
        rest_free, o_free, nat_free, neg_free = [[]], [[]], [[]], [[]]

        def project_split(W, src, src_ready, side, bias):
            ps = psum.take()
            mm = [pe.do(lambda e, a=a, c=c: e.matmul(ps.ap[:, a:c], W, src.ap[:, a:c], start=True, stop=True),
                        [src_ready, ps.after, ready]) for a, c in blocks(T)]
            scale = ATT_SCALE if side == "k" else 1.0
            dst = full[side]
            if bias is None:
                t = ac.do(lambda e: e.activation(dst[:, :], ps.ap[:, 0:T], ACT.Copy, scale=scale),
                          [mm, full_free[side]])
            else:
                t = dv.do(lambda e: e.tensor_scalar(dst[:, :], ps.ap[:, 0:T], bias, scale, ALU.add, ALU.mult),
                          [mm, full_free[side]])
            ps.done(t)
            t_full = t
            pt = parts.take()
            hi = ac.do(lambda e: e.activation(pt.ap[:, 0, :], dst[:, :], ACT.Copy), [t, pt.after])
            r = dv.do(lambda e: e.tensor_tensor(rest[:, :], dst[:, :], pt.ap[:, 0, :], ALU.subtract),
                      [hi, rest_free[0]])
            mid = ac.do(lambda e: e.activation(pt.ap[:, 1, :], rest[:, :], ACT.Copy), [r, pt.after])
            lo = dv.do(lambda e: e.tensor_tensor(pt.ap[:, 2, :], rest[:, :], pt.ap[:, 1, :], ALU.subtract),
                       [mid, pt.after])
            rest_free[0] = [lo]
            stack = q_stack if side == "q" else k_stack
            out = scratch[side]
            there = dma(out.rearrange("a (h d) t -> (h d) a t", d=HD), pt.ap[:, :, :], [hi, mid, lo, scratch_free[side]])
            pt.done(there)
            rows = SPLIT * HD
            sent = []
            for i in range(SPLIT):
                if side == "q":
                    for copy in range(SPLIT):
                        r0 = i * rows + copy * HD
                        sent.append(dma(stack[r0:r0 + HD, :, :], out[i, :, :].rearrange("(h d) t -> d h t", d=HD),
                                        [there, stack_free[0], ready]))
                else:
                    for b in range(SPLIT):
                        r0 = i * rows + b * HD
                        sent.append(dma(stack[r0:r0 + HD, :, :], out[b, :, :].rearrange("(h d) t -> d h t", d=HD),
                                        [there, stack_free[0], ready]))
            scratch_free[side] = sent
            return t_full, sent

        def values(W, src, src_ready, bias_row):
            got = []
            for n0 in range(0, NT, 4):
                ps = psum.take()
                k = min(4, NT - n0)
                mm = [pe.do(lambda e, n=n, ps=ps, n0=n0: e.matmul(
                    ps.ap[:, (n - n0) * P:(n - n0 + 1) * P], src.ap[:, n * P:(n + 1) * P], W,
                    start=True, stop=True), [src_ready, ps.after, ready]) for n in range(n0, n0 + k)]
                cols = []
                for n in range(n0, n0 + k):
                    o = v_nat[:, n, :, 0:HD]
                    i = ps.ap[:, (n - n0) * P:(n - n0 + 1) * P].rearrange("p (h d) -> p h d", d=HD)
                    if bias_row is None:
                        t = ac.do(lambda e, o=o, i=i: e.activation(o, i, ACT.Copy), [mm, nat_free[0], ready])
                    else:
                        t = dv.do(lambda e, o=o, i=i: e.tensor_tensor(
                            o, i, bias_row.rearrange("p (h d) -> p h d", d=HD), ALU.add),
                            [mm, nat_free[0], ready])
                    cols.append(t)
                ps.done(*cols)
                got += cols
            return got

        def spread_maxima(maxima):
            view = neg_max[:, :, 0, :]
            t = ac.do(lambda e: e.activation(neg_bf[:, :, :], view, ACT.Copy), [maxima, neg_free[0]])
            t = dv.do(lambda e: e.tensor_copy(neg_parts[:, :, 0, :], neg_bf[:, :, :]), [t, neg_free[0]])
            t = dv.do(lambda e: e.tensor_tensor(neg_rest[:, :, :], view, neg_parts[:, :, 0, :], ALU.subtract), [t])
            t = ac.do(lambda e: e.activation(neg_bf[:, :, :], neg_rest[:, :, :], ACT.Copy), [t])
            t = dv.do(lambda e: e.tensor_copy(neg_parts[:, :, 1, :], neg_bf[:, :, :]), [t])
            t = dv.do(lambda e: e.tensor_tensor(neg_parts[:, :, 2, :], neg_rest[:, :, :], neg_parts[:, :, 1, :],
                                                ALU.subtract), [t])
            rows = SPLIT * HEADS
            ps = psum.take()
            tt = [pe.do(lambda e, n=n: e.transpose(
                ps.ap[0:rows, n * P:(n + 1) * P], neg_parts[:, n, :, :].rearrange("p a h -> p (a h)"), ident),
                [t, ps.after]) for n in range(NT)]
            t = ac.do(lambda e: e.activation(neg_T[:, :], ps.ap[0:rows, 0:T], ACT.Copy), [tt, neg_free[0]])
            ps.done(t)
            sent = [dma(q_stack[NEG_ROW + a:NEG_ROW + a + 1, :, :], neg_T[a * HEADS:(a + 1) * HEADS, :],
                        [t, stack_free[0]]) for a in range(SPLIT)]
            neg_free[0] = sent + [t]
            return sent

        def row_maxima_window(spread):
            got = []
            for n in range(NT):
                lo = max(0, n * P - WINDOW)
                cut = lo - (n * P - WINDOW)
                cols = P + WINDOW - cut
                for h0 in range(0, HEADS, GROUP):
                    ps = psum.take()
                    mm = []
                    for i in range(GROUP):
                        o = ps.ap[:, i * 256:i * 256 + cols]
                        h = h0 + i
                        pe.do(lambda e, o=o, h=h, n=n, lo=lo: e.matmul(
                            o, q_stack[0:NEG_ROW, h, n * P:(n + 1) * P], k_stack[0:NEG_ROW, h, lo:(n + 1) * P],
                            start=True, stop=False), [spread, ps.after])
                        mm.append(pe.do(lambda e, o=o, cut=cut: e.matmul(
                            o, ident_bf[2.0 ** 60][:, :], w3["win_row"][:, cut:P + WINDOW],
                            start=False, stop=True), [ready]))
                    t = dv.do(lambda e, ps=ps, n=n, h0=h0, cols=cols: e.tensor_reduce(
                        neg_max[:, n, 0, h0:h0 + GROUP],
                        ps.ap[:, :].rearrange("p (i c) -> p i c", i=GROUP)[:, :, 0:cols], AX.X, ALU.max,
                        negate=True), [mm, neg_free[0]])
                    ps.done(t)
                    got.append(t)
            return got

        def row_maxima_causal(spread):
            got = []
            for n in range(NT):
                pieces = []
                for half, (a, c) in enumerate(blocks((n + 1) * P)):
                    width = c - a
                    per = max(1, BANK // width)
                    for h0 in range(0, HEADS, 2 * per):
                        ps = psum.take()
                        mm = []
                        for i in range(2 * per):
                            o = ps.ap[:, (i // per) * BANK + (i % per) * width:][:, 0:width]
                            h = h0 + i
                            diag = c == (n + 1) * P
                            t = pe.do(lambda e, o=o, h=h, n=n, a=a, c=c, diag=diag: e.matmul(
                                o, q_stack[0:NEG_ROW, h, n * P:(n + 1) * P], k_stack[0:NEG_ROW, h, a:c],
                                start=True, stop=not diag), [spread, ps.after])
                            if diag:
                                o2 = ps.ap[:, (i // per) * BANK + (i % per) * width:][:, width - P:width]
                                t = pe.do(lambda e, o2=o2: e.matmul(
                                    o2, ident_bf[100.0][:, :], w3["causal_row"][:, :], start=False, stop=True),
                                    [ready])
                            mm.append(t)
                        src = ps.ap[:, :].rearrange("p (k c) -> p k c", k=2)[:, :, 0:per * width]
                        if per > 1:
                            src = src.rearrange("p k (i c) -> p k i c", i=per)
                            dst = neg_max[:, n, half, h0:h0 + 2 * per].rearrange("p (k i) -> p k i", k=2)
                        else:
                            dst = neg_max[:, n, half, h0:h0 + 2]
                        t = dv.do(lambda e, src=src, dst=dst: e.tensor_reduce(dst, src, AX.X, ALU.max, negate=True),
                                  [mm, neg_free[0]])
                        ps.done(t)
                        pieces.append(t)
                if (n + 1) * P > BANK:
                    t = dv.do(lambda e, n=n: e.tensor_tensor(neg_max[:, n, 0, :], neg_max[:, n, 0, :],
                                                             neg_max[:, n, 1, :], ALU.min), [pieces])
                    pieces = [t]
                got += pieces
            return got

        def weigh_window(spread, vals):
            ends = []
            for g in range(HEADS // GROUP):
                acc = psum.take()
                last = None
                for j in range(NT):
                    q0 = j * P
                    cols = min(P + WINDOW, T - q0)
                    ps = psum.take()
                    mm = []
                    for i in range(GROUP):
                        h = g * GROUP + i
                        o = ps.ap[:, i * 256:i * 256 + cols]
                        pe.do(lambda e, o=o, h=h, q0=q0, cols=cols: e.matmul(
                            o, k_stack[:, h, q0:q0 + P], q_stack[:, h, q0:q0 + cols], start=True, stop=False),
                            [spread, ps.after])
                        mm.append(pe.do(lambda e, o=o, cols=cols: e.matmul(
                            o, ident_bf[2.0 ** 60][:, :], w3["win_col"][:, 0:cols], start=False, stop=True),
                            [ready]))
                    pr = probs.take()
                    view = lambda ap, cols=cols: ap[:, :].rearrange("p (i c) -> p i c", i=GROUP)[:, :, 0:cols]
                    t = ac.do(lambda e, ps=ps, pr=pr, view=view: e.activation(view(pr.ap), view(ps.ap), ACT.Exp),
                              [mm, pr.after])
                    ps.done(t)
                    cuts = [(q0, min(q0 + cols, T))]
                    if q0 < BANK < q0 + cols:
                        cuts = [(q0, BANK), (BANK, q0 + cols)]
                    reads = []
                    for a, c in cuts:
                        for i in range(GROUP):
                            h = g * GROUP + i
                            start = (j == 0) or (a == BANK and q0 < BANK) or (q0 == BANK and a == BANK and not crossed)
                            last = pe.do(lambda e, i=i, h=h, a=a, c=c, pr=pr, acc=acc, start=start, j=j, q0=q0: e.matmul(
                                acc.ap[32 * i:32 * i + 32, a:c], v_nat[:, j, h, :],
                                pr.ap[:, i * 256 + a - q0:i * 256 + c - q0], start=start, stop=(j == NT - 1),
                                skip_group_check=True), [t, vals, acc.after])
                            reads.append(last)
                    crossed = len(cuts) == 2
                    pr.done(reads[-1])
                t = ac.do(lambda e, g=g, acc=acc: e.activation(o_T[:, g, :], acc.ap[:, 0:T], ACT.Copy),
                          [last, o_free[0]])
                acc.done(t)
                ends.append(t)
            return ends, [last]

        def weigh_causal(spread, vals):
            ends = []
            for g in range(HEADS // GROUP):
                for a0, c0 in blocks(T):
                    acc = psum.take()
                    keys = c0 // P
                    for j in range(keys):
                        a = max(a0, j * P)
                        n = c0 - a
                        for i0 in range(0, GROUP, 2):
                            ps = psum.take()
                            mm = []
                            for i in range(2):
                                h = g * GROUP + i0 + i
                                diag = a == j * P
                                t = pe.do(lambda e, i=i, h=h, a=a, c0=c0, j=j, n=n, ps=ps, diag=diag: e.matmul(
                                    ps.ap[:, i * BANK:i * BANK + n], k_stack[:, h, j * P:(j + 1) * P],
                                    q_stack[:, h, a:c0], start=True, stop=not diag), [spread, ps.after])
                                if diag:
                                    t = pe.do(lambda e, i=i, ps=ps: e.matmul(
                                        ps.ap[:, i * BANK:i * BANK + P], ident_bf[100.0][:, :],
                                        w3["causal_col"][:, :], start=False, stop=True),
                                        [ready])
                                mm.append(t)
                            pr = probs.take()
                            view = lambda ap, n=n: ap[:, :].rearrange("p (i c) -> p i c", i=2)[:, :, 0:n]
                            t = ac.do(lambda e, ps=ps, pr=pr, view=view: e.activation(
                                view(pr.ap), view(ps.ap), ACT.Exp), [mm, pr.after])
                            ps.done(t)
                            for i in range(2):
                                h = g * GROUP + i0 + i
                                last = pe.do(lambda e, i=i, i0=i0, h=h, a=a, a0=a0, n=n, pr=pr, acc=acc, j=j, keys=keys: e.matmul(
                                    acc.ap[32 * (i0 + i):32 * (i0 + i) + 32, a - a0:a - a0 + n], v_nat[:, j, h, :],
                                    pr.ap[:, i * BANK:i * BANK + n], start=(j == 0), stop=(j == keys - 1),
                                    skip_group_check=True), [t, vals, acc.after])
                            pr.done(last)
                    t = ac.do(lambda e, g=g, acc=acc, a0=a0, c0=c0: e.activation(
                        o_T[:, g, a0:c0], acc.ap[:, 0:c0 - a0], ACT.Copy), [last, o_free[0]])
                    acc.done(t)
                    ends.append(t)
            return ends, [last]

        def attended(n, turned_after):
            ps = psum.take()
            tt = [pe.do(lambda e, g=g, ps=ps: e.transpose(ps.ap[:, g * P:(g + 1) * P], o_T[:, g, n * P:(n + 1) * P],
                                                          ident), [turned_after, ps.after])
                  for g in range(HEADS // GROUP)]
            view = ps.ap[:, 0:4 * P].rearrange("p (h c) -> p h c", c=32)
            iv = inv_den.take()
            t = dv.do(lambda e: e.reciprocal(iv.ap[:, :], view[:, :, HD]), [tt, iv.after])
            at = att.take()
            t = dv.do(lambda e: e.tensor_tensor(
                at.ap[:, :].rearrange("p (h d) -> p h d", d=HD), view[:, :, 0:HD],
                iv.ap[:, :].unsqueeze(2).to_broadcast([P, HEADS, HD]), ALU.mult), [t, at.after])
            iv.done(t)
            ps.done(t)
            return at, t, tt

        def project_out(at, t, Wo, b, n, bias_row):
            ps = psum.take()
            t = pe.do(lambda e: e.transpose(ps.ap[:, 0:P], at.ap[:, :], ident), [t, ps.after])
            at.done(t)
            aT = attT.take()
            t = ac.do(lambda e: e.activation(aT.ap[:, :], ps.ap[:, 0:P], ACT.Copy), [t, aT.after])
            t = pe.do(lambda e: e.matmul(ps.ap[:, BANK:BANK + P], aT.ap[:, :], Wo, start=True, stop=True), [t, ready])
            aT.done(t)
            tile = x[:, b * NT + n, :]
            if bias_row is not None:
                x_ready[b * NT + n] = gp.do(lambda e: e.tensor_tensor(tile, tile, bias_row, ALU.add),
                                            [x_ready[b * NT + n], last_norm[0]])
            t = dv.do(lambda e: e.tensor_tensor(tile, tile, ps.ap[:, BANK:BANK + P], ALU.add),
                      [t, x_ready[b * NT + n], last_norm[0]])
            ps.done(t)
            x_ready[b * NT + n] = t

        def window_attention(b):
            src, src_ready = layer_norm(b)
            f1, s1 = project_split(w("a_wq"), src, src_ready, "q", None)
            f2, s2 = project_split(w("a_wk"), src, src_ready, "k", None)
            vals = values(w("a_wv"), src, src_ready, None)
            src.done(*vals, (pe, pe.count))
            spread = s1 + s2
            full_free["q"], full_free["k"] = list(rest_free[0]), list(rest_free[0])
            neg = spread_maxima(row_maxima_window(spread))
            o, last = weigh_window(spread + neg, vals)
            stack_free[0], nat_free[0] = list(last), list(last)
            turned = []
            for n in range(NT):
                at, t, tt = attended(n, o)
                turned += tt
                project_out(at, t, w("a_wo"), b, n, None)
            o_free[0] = turned

        spread_k = Ring([carve([P, T]) for i in range(2)])
        spread_q = Ring([carve([P, T]) for i in range(1)])
        hebb = Ring([carve([P, T]) for i in range(2)])
        retain = carve([P, HD])
        alpha_T = carve([P // 2 + 1, T])
        alpha = carve([P, NT, HEADS])
        alpha_free = [[]]

        def clear_recurrence():
            t = ac.do(lambda e: e.activation(retain[:, :], w("c_lambda"), ACT.Exp), ready)
            t = dv.do(lambda e: e.tensor_scalar(retain[:, :], retain[:, :], 1.0, None, ALU.add), [t])
            return [dv.do(lambda e: e.reciprocal(retain[:, :], retain[:, :]), [t]),
                    gp.do(lambda e: e.memset(alpha_T[P // 2:P // 2 + 1, :], 1.0))]

        def recurrence(full_ready):
            acc = psum.take()
            there = [dma(whole[s], full[s][:, :], [full_ready, whole_free[0]]) for s in "qk"]
            whole_free[0] = []
            for j in range(HD):
                sk, sq = spread_k.take(), spread_q.take()
                loads = []
                for s, side in ((sk, "k"), (sq, "q")):
                    row = whole[side].rearrange("(h j) t -> h j t", j=HD)[:, j, :]
                    loads.append(dma(s.ap[:, :], row.unsqueeze(1).to_broadcast([HEADS, HD, T]), [there, s.after]))
                hb = hebb.take()
                t = dv.do(lambda e, j=j, sk=sk, hb=hb: e.scalar_tensor_tensor(
                    hb.ap[:, :], sk.ap[:, :], w("c_gamma", j, j + 1), full["v"][:, :], ALU.mult, ALU.mult),
                    [loads, hb.after, full_ready, ready])
                t = dv.do(lambda e, j=j, sk=sk, hb=hb: e.tensor_tensor_scan(
                    sk.ap[:, :], retain[:, j:j + 1].to_broadcast([P, T]), hb.ap[:, :], 0.0, ALU.mult, ALU.add),
                    [t, ready])
                t = dv.do(lambda e, j=j, sk=sk, sq=sq, hb=hb: e.scalar_tensor_tensor(
                    hb.ap[:, :], sk.ap[:, :], w("c_static", j, j + 1), sq.ap[:, :], ALU.add, ALU.mult), [t, loads])
                sk.done(t)
                sq.done(t)
                whole_free[0] += loads
                for n in range(NT):
                    m = pe.do(lambda e, n=n, hb=hb, j=j: e.matmul(
                        acc.ap[:, n * P:(n + 1) * P], hb.ap[:, n * P:(n + 1) * P], ident,
                        start=(j == 0 and n % 4 == 0), stop=(j == HD - 1), skip_group_check=True),
                        [t, acc.after])
                hb.done(m)
            full_free["q"] = full_free["k"] = full_free["v"] = [t] + there
            return acc, m

        y_stp = full["v"]
        y_free = [[]]

        def causal_mixed(b):
            src, src_ready = layer_norm(b)
            ps = psum.take()
            mm = [pe.do(lambda e, a=a, c=c: e.matmul(ps.ap[0:P // 2, a:c], w("c_gw1"), src.ap[:, a:c], start=True,
                                                     stop=True), [src_ready, ps.after, ready])
                  for a, c in blocks(T)]
            t = ac.do(lambda e: e.activation(alpha_T[0:P // 2, :], ps.ap[0:P // 2, 0:T], ACT.Gelu,
                                             bias=w("c_gb1")), [mm, alpha_free[0]])
            ps.done(t)
            ps = psum.take()
            mm = [pe.do(lambda e, n=n: e.matmul(ps.ap[:, n * HEADS:(n + 1) * HEADS],
                                                alpha_T[:, n * P:(n + 1) * P], w("c_gw2"), start=True, stop=True),
                        [t, ps.after, ready]) for n in range(NT)]
            av = alpha[:, :, :].rearrange("p n h -> p (n h)")
            t = ac.do(lambda e: e.activation(av, ps.ap[:, 0:NT * HEADS], ACT.Exp, scale=-1.0), [mm, alpha_free[0]])
            ps.done(t)
            t = dv.do(lambda e: e.tensor_scalar(av, av, 1.0, None, ALU.add), [t])
            t_alpha = dv.do(lambda e: e.reciprocal(av, av), [t])

            f1, s1 = project_split(w("c_wq"), src, src_ready, "q", w("c_bq"))
            f2, s2 = project_split(w("c_wk"), src, src_ready, "k", w("c_bk"))
            ps = psum.take()
            mm = [pe.do(lambda e, a=a, c=c: e.matmul(ps.ap[:, a:c], w("c_wv"), src.ap[:, a:c], start=True, stop=True),
                        [src_ready, ps.after]) for a, c in blocks(T)]
            f3 = dv.do(lambda e: e.tensor_scalar(full["v"][:, :], ps.ap[:, 0:T], w("c_bv"), None, ALU.add),
                       [mm, full_free["v"]])
            ps.done(f3)
            vals = values(w("c_wv"), src, src_ready, w("c_bv_row"))
            src.done(*vals, (pe, pe.count))
            spread = s1 + s2
            acc, m = recurrence([f1, f2, f3] + rest_free[0])
            t_y = ac.do(lambda e: e.activation(y_stp[:, :], acc.ap[:, 0:T], ACT.Copy), [m, y_free[0], full_free["v"]])
            acc.done(t_y)
            neg = spread_maxima(row_maxima_causal(spread))
            o, last = weigh_causal(spread + neg, vals)
            stack_free[0], nat_free[0] = list(last), list(last)
            turned, y_read = [], []
            for n in range(NT):
                at, t, tt = attended(n, o)
                turned += tt
                y = y_stp[:, n * P:(n + 1) * P]
                t = dv.do(lambda e, at=at, y=y: e.tensor_tensor(at.ap[:, :], at.ap[:, :], y, ALU.subtract), [t, t_y])
                t = dv.do(lambda e, at=at, n=n: e.tensor_tensor(
                    at.ap[:, :].rearrange("p (h d) -> p h d", d=HD), at.ap[:, :].rearrange("p (h d) -> p h d", d=HD),
                    alpha[:, n, :].unsqueeze(2).to_broadcast([P, HEADS, HD]), ALU.mult), [t, t_alpha])
                t = dv.do(lambda e, at=at, y=y: e.tensor_tensor(at.ap[:, :], at.ap[:, :], y, ALU.add), [t])
                y_read.append(t)
                project_out(at, t, w("c_wo"), b, n, w("c_bo_row"))
            alpha_free[0], o_free[0] = [t], turned
            full_free["v"] = full_free["v"] + y_read

        def first_largest(scores, eq, run, out, top, keep, after):
            n = scores.shape[2]
            f = lambda ap: ap.rearrange("p a b -> p (a b)")
            t = dv.do(lambda e: e.tensor_tensor(eq, scores, top.unsqueeze(2).to_broadcast([P, NT, n]),
                                                ALU.is_equal), after)
            t = dv.do(lambda e: e.tensor_tensor_scan(f(run), keep, f(eq), 0.0, ALU.mult, ALU.add), [t])
            return dv.do(lambda e: e.scalar_tensor_tensor(out, run, 1.0, eq, ALU.is_equal, ALU.mult), [t])

        def softmax_small(src, dst, small, n, after):
            bc = lambda ap: ap.unsqueeze(2).to_broadcast([P, NT, n])
            t = dv.do(lambda e: e.tensor_reduce(small[:, 0, :], src, AX.X, ALU.max), after)
            t = dv.do(lambda e: e.tensor_tensor(dst, src, bc(small[:, 0, :]), ALU.subtract), [t])
            done_src = t
            t = ac.do(lambda e: e.activation(dst, dst, ACT.Exp), [t])
            t = dv.do(lambda e: e.tensor_reduce(small[:, 1, :], dst, AX.X, ALU.add), [t])
            t = dv.do(lambda e: e.reciprocal(small[:, 1, :], small[:, 1, :]), [t])
            t = dv.do(lambda e: e.tensor_tensor(dst, dst, bc(small[:, 1, :]), ALU.mult), [t])
            return t, done_src

        def split_small(src, dst, n, tmp, tmp_bf, after):
            t = list(after)
            left = src
            for a in range(SPLIT):
                o = dst[:, :, a * n:(a + 1) * n]
                t = [dv.do(lambda e, left=left: e.tensor_copy(tmp_bf, left), t)]
                t = [dv.do(lambda e, o=o: e.tensor_copy(o, tmp_bf), t)]
                if a < SPLIT - 1:
                    t = [dv.do(lambda e, o=o, left=left: e.tensor_tensor(tmp, left, o, ALU.subtract), t)]
                    left = tmp
            return t

        def turn_rows(src, outs, after, free):
            ps = psum.take()
            tt = [pe.do(lambda e, n=n: e.transpose(ps.ap[:, n * P:(n + 1) * P], src[:, n, :], ident),
                        [after, ps.after, ready]) for n in range(NT)]
            got = [ac.do(lambda e, o=o, s=s: e.activation(o[:, :], ps.ap[:, 0:T], ACT.Copy, scale=s), [tt, free])
                   for o, s in outs]
            ps.done(*got)
            return got, tt

        DENSE = 1 + ROUTES
        used[0] = 0
        combined = {n: carve([P, GLA_HEADS * GLA_D]) for n in ("q2", "k2", "g1", "g2", "g")}
        route_p = carve([P, NT, ROUTES])
        route_s = carve([P, 2, NT])
        route_eq = carve([P, NT, ROUTES])
        route_run = carve([P, NT, ROUTES])
        route_hot = carve([P, NT, ROUTES])
        route_bf = carve([P, NT, ROUTES], BF16)
        route_top = carve([P, NT])
        rows_w = carve([P, NT, P])
        rows_h = rows_w
        w_T = carve([P, T], BF16)
        hot_T = carve([P, T], BF16)
        hot1_T = carve([P, T], BF16)
        gate_T = carve([P, PAIRS, T])
        gla = {n: Ring([carve([P, BANK]) for i in range(k)]) for n, k in
               (("z", 1), ("gk", 2), ("e", 1), ("up", 2), ("dn", 2), ("q1", 1), ("q2", 1), ("k1", 1), ("k2", 1),
                ("k2n", 1), ("k1nat", 1), ("k2nat", 1), ("sq", 1), ("rs", 1), ("f", 1))}
        q2m = Ring([carve([P, ROUTES, PAIRS * P])])
        hot_b = Ring([carve([P, ROUTES * P])])
        v5 = Ring([carve([P, DENSE, BANK])])
        masked1 = Ring([carve([P, GLA_HEADS * P])])
        masked2 = Ring([carve([P, GLA_HEADS * P])])
        mix = Ring([carve([P, P + 2 * ROUTES]) for i in range(2)])
        mix_tril = Ring([carve([P, P]) for i in range(2)])
        kmax = Ring([carve([P, 2, GLA_HEADS]) for i in range(2)])
        decay = Ring([carve([P, PAIRS, 2, DENSE]) for i in range(3)])
        factor = carve([P, PAIRS, DENSE])
        state = carve([P, PAIRS, DENSE, GLA_D])
        state_mid = carve([P, PAIRS, DENSE, GLA_D])
        state_dg = carve([P, PAIRS, DENSE, 2, GLA_D])
        low_rank = carve([P, sizes["l"]])
        keep4 = carve([P, NT, ROUTES])
        gla_free = {"route": [], "rows": [], "gate": [], "mid": [], "dg": []}

        def clear_gla():
            got = [gp.do(lambda e: e.memset(state_dg[:, :, :, :, :], 0.0)),
                   gp.do(lambda e: e.memset(rows_w[:, :, :], 0.0))]
            t = gp.do(lambda e: e.memset(keep4[:, :, :], 1.0))
            got.append(gp.do(lambda e: e.memset(keep4[:, :, 0:1], 0.0), [t]))
            low = dma(low_rank, packed["l"])
            for n in combined:
                ps = psum.take()
                t = pe.do(lambda e, n=n, ps=ps: e.matmul(ps.ap[:, 0:BANK], w(f"b_{n}a"), w(f"b_{n}b"), start=True,
                                                         stop=True), [ready, low, ps.after])
                t = ac.do(lambda e, n=n, ps=ps: e.activation(combined[n][:, :], ps.ap[:, 0:BANK], ACT.Copy,
                                                             scale=GLA_D ** -0.5 if n == "q2" else 1.0), [t])
                ps.done(t)
                got.append(t)
            return got

        def at_head(h):
            return (h % 2) * BANK + (h // 2) * P

        def gla_layer(b):
            src, src_ready = layer_norm(b)
            base = [src_ready, ready]
            for p in range(PAIRS):
                ps = psum.take()
                mm = [pe.do(lambda e, p=p, a=a, c=c, ps=ps: e.matmul(
                    ps.ap[:, a:c], combined["g"][:, p * P:(p + 1) * P], src.ap[:, a:c], start=True, stop=True),
                    [base, ps.after]) for a, c in blocks(T)]
                gated = ac.do(lambda e, p=p, ps=ps: e.activation(gate_T[:, p, :], ps.ap[:, 0:T], ACT.Silu),
                              [mm, gla_free["gate"]])
                ps.done(gated)
            ps = psum.take()
            mm = [pe.do(lambda e, n=n: e.matmul(ps.ap[:, n * ROUTES:(n + 1) * ROUTES], src.ap[:, n * P:(n + 1) * P],
                                                w("b_we"), start=True, stop=True), [base, ps.after])
                  for n in range(NT)]
            t, used = softmax_small(ps.ap[:, 0:NT * ROUTES].rearrange("p (n e) -> p n e", e=ROUTES),
                                    route_p[:, :, :], route_s, ROUTES, [mm, gla_free["route"]])
            ps.done(used)
            t_top = dv.do(lambda e: e.tensor_reduce(route_top[:, :], route_p[:, :, :], AX.X, ALU.max), [t])
            hot = first_largest(route_p[:, :, :], route_eq[:, :, :], route_run[:, :, :], route_hot[:, :, :],
                                route_top[:, :], keep4[:, :, :].rearrange("p a b -> p (a b)"),
                                [t_top, ready, gla_free["rows"]])
            t = [dv.do(lambda e, a=a: e.tensor_copy(rows_h[:, :, a * ROUTES:(a + 1) * ROUTES], route_hot[:, :, :]),
                       [hot, gla_free["rows"]]) for a in range(SPLIT)]
            g1, tt = turn_rows(rows_h, [(hot_T, 1.0), (hot1_T, w("route_first"))], t, gla_free["rows"])
            t = dv.do(lambda e: e.tensor_tensor(route_eq[:, :, :], route_p[:, :, :], route_hot[:, :, :], ALU.mult), [hot])
            t = split_small(route_eq[:, :, :], rows_w, ROUTES, route_run[:, :, :], route_bf[:, :, :], [t, tt])
            g2, tt = turn_rows(rows_w, [(w_T, 1.0)], t, gla_free["rows"])
            routed = g1 + g2

            last_state = None
            prev = None
            for n in range(NT):
                tok = slice(n * P, (n + 1) * P)
                xt = src.ap[:, tok]
                gk, gk_ready = [], []
                ps = psum.take()
                mm = [pe.do(lambda e, i=i, ps=ps, xt=xt: e.matmul(ps.ap[:, i * BANK:(i + 1) * BANK], xt,
                                                           combined[f"g{i + 1}"][:, :], start=True, stop=True),
                            [base, ps.after]) for i in range(2)]
                for i in range(2):
                    z, el, g = gla["z"].take(), gla["e"].take(), gla["gk"].take()
                    tz = dv.do(lambda e, i=i, z=z, ps=ps: e.tensor_tensor(
                        z.ap[:, :], ps.ap[:, i * BANK:(i + 1) * BANK], w(f"b_bg{i + 1}"), ALU.add), [mm, z.after])
                    t = dv.do(lambda e, z=z, el=el: e.scalar_tensor_tensor(
                        el.ap[:, :], z.ap[:, :], -1.0, z.ap[:, :], ALU.mult, ALU.min), [tz, el.after])
                    t = ac.do(lambda e, el=el: e.activation(el.ap[:, :], el.ap[:, :], ACT.Exp), [t])
                    t = ac.do(lambda e, el=el: e.activation(el.ap[:, :], el.ap[:, :], ACT.Ln, bias=w("ones")), [t])
                    t = dv.do(lambda e, z=z, el=el, g=g: e.scalar_tensor_tensor(
                        g.ap[:, :], z.ap[:, :], 0.0, el.ap[:, :], ALU.min, ALU.subtract), [t, g.after])
                    z.done(t)
                    el.done(t)
                    gk.append(g)
                    gk_ready.append(t)
                ps.done(tz)
                ps = psum.take()
                m1 = pe.do(lambda e, ps=ps, tok=tok: e.matmul(ps.ap[:, 0:P], hot_T[:, tok], hot1_T[:, tok], start=True,
                                                     stop=True), [routed, ps.after])
                m2 = pe.do(lambda e, ps=ps, tok=tok: e.matmul(ps.ap[:, P:2 * P], hot_T[:, tok], w_T[:, tok], start=True,
                                                     stop=True), [routed])
                m3 = [pe.do(lambda e, ps=ps, r=r, tok=tok: e.matmul(
                    ps.ap[:, BANK + r * P:BANK + (r + 1) * P], w3["route_bcast"][:, r * P:(r + 1) * P], w_T[:, tok],
                    start=True, stop=True), [routed]) for r in range(ROUTES)]
                mx, mt, hb = mix.take(), mix_tril.take(), hot_b.take()
                u1 = dv.do(lambda e, ps=ps, mx=mx: e.tensor_tensor(mx.ap[:, 0:P], ps.ap[:, 0:P], w("gate_sum", 0, P),
                                                                   ALU.mult), [m1, m2, mx.after])
                u2 = dv.do(lambda e, mx=mx, n=n: e.tensor_tensor(
                    mx.ap[:, P:P + 2 * ROUTES].rearrange("p (k r) -> p k r", k=2),
                    route_hot[:, n, :].unsqueeze(1).to_broadcast([P, 2, ROUTES]),
                    w("half").unsqueeze(2).to_broadcast([P, 2, ROUTES]), ALU.mult), [hot, mx.after])
                u3 = dv.do(lambda e, ps=ps, mt=mt: e.tensor_tensor(mt.ap[:, :], ps.ap[:, P:2 * P], w("tril"),
                                                                   ALU.mult), [m2, mt.after])
                u4 = ac.do(lambda e, ps=ps, hb=hb: e.activation(hb.ap[:, :], ps.ap[:, BANK:2 * BANK], ACT.Copy),
                           [m3, hb.after])
                ps.done(u1, u3, u4)
                up, dn, dc = [], [], decay.take()
                sums_ready, dcs = [], []
                for i in range(2):
                    cols = P + (2 if i == 0 else 2 * ROUTES)
                    rhs = w("gate_sum") if i == 0 else mx.ap[:, 0:cols]
                    ps = psum.take()
                    mm = [pe.do(lambda e, p=p, i=i, ps=ps, rhs=rhs, cols=cols: e.matmul(
                        ps.ap[:, p * 256:p * 256 + cols], gk[i].ap[:, p * P:(p + 1) * P], rhs, start=True, stop=True),
                        [gk_ready[i], u1, u2, ps.after]) for p in range(PAIRS)]
                    gk[i].done(mm[-1])
                    v4 = ps.ap[:, :].rearrange("p (a c) -> p a c", a=PAIRS)
                    for lst, name, sc in ((up, "up", 1.0), (dn, "dn", -1.0)):
                        s = gla[name].take()
                        t1 = ac.do(lambda e, s=s, v4=v4, sc=sc: e.activation(
                            s.ap[:, :].rearrange("p (a c) -> p a c", a=PAIRS), v4[:, :, 0:P], ACT.Exp, scale=sc),
                            [mm, s.after])
                        lst.append(s)
                        sums_ready.append(t1)
                    d = 1 if i == 0 else ROUTES
                    first = 0 if i == 0 else 1
                    for k in range(2):
                        t1 = ac.do(lambda e, v4=v4, d=d, first=first, dc=dc, k=k: e.activation(
                            dc.ap[:, :, k, first:first + d], v4[:, :, P + k * d:P + (k + 1) * d], ACT.Exp),
                            [mm, dc.after])
                        dcs.append(t1)
                    ps.done(t1)
                mx.done(mm[-1])
                ps = psum.take()
                mq = [pe.do(lambda e, p=p, ps=ps, xt=xt: e.matmul(ps.ap[:, p * P:(p + 1) * P], w("b_wq", p * P, (p + 1) * P),
                                                           xt, start=True, stop=True), [base, ps.after])
                      for p in range(PAIRS)]
                mk = [pe.do(lambda e, p=p, ps=ps, xt=xt: e.matmul(ps.ap[:, BANK + p * P:BANK + (p + 1) * P],
                                                           w("b_wk", p * P, (p + 1) * P), xt, start=True, stop=True),
                            [base]) for p in range(PAIRS)]
                q1, k1, q2, k2 = (gla[s].take() for s in ("q1", "k1", "q2", "k2"))
                tq1 = dv.do(lambda e, ps=ps, q1=q1, up=up: e.scalar_tensor_tensor(
                    q1.ap[:, :], ps.ap[:, 0:BANK], GLA_D ** -0.5, up[0].ap[:, :], ALU.mult, ALU.mult),
                    [mq, sums_ready, q1.after])
                tk1 = dv.do(lambda e, ps=ps, k1=k1, dn=dn: e.tensor_tensor(
                    k1.ap[:, :], ps.ap[:, BANK:2 * BANK], dn[0].ap[:, :], ALU.mult), [mk, sums_ready, k1.after])
                ps.done(tq1, tk1)
                up[0].done(tq1)
                dn[0].done(tk1)
                ps = psum.take()
                mq = [pe.do(lambda e, p=p, ps=ps, xt=xt: e.matmul(ps.ap[:, p * P:(p + 1) * P],
                                                           combined["q2"][:, p * P:(p + 1) * P], xt, start=True,
                                                           stop=True), [base, ps.after]) for p in range(PAIRS)]
                mk = pe.do(lambda e, ps=ps, xt=xt: e.matmul(ps.ap[:, BANK:2 * BANK], xt, combined["k2"][:, :], start=True,
                                                     stop=True), [base])
                tq2 = dv.do(lambda e, ps=ps, q2=q2, up=up: e.tensor_tensor(q2.ap[:, :], ps.ap[:, 0:BANK],
                                                                    up[1].ap[:, :], ALU.mult),
                            [mq, sums_ready, q2.after])
                up[1].done(tq2)
                km, kn = kmax.take(), gla["k2n"].take()
                heads = lambda ap: ap.rearrange("p (h d) -> p h d", d=GLA_D)
                over = lambda ap: ap.unsqueeze(2).to_broadcast([P, GLA_HEADS, GLA_D])
                t = dv.do(lambda e, ps=ps, km=km, heads=heads: e.tensor_reduce(km.ap[:, 0, :], heads(ps.ap[:, BANK:2 * BANK]),
                                                                  AX.X, ALU.max), [mk, km.after])
                t = dv.do(lambda e, ps=ps, km=km, kn=kn, heads=heads, over=over: e.tensor_tensor(
                    heads(kn.ap[:, :]), heads(ps.ap[:, BANK:2 * BANK]), over(km.ap[:, 0, :]), ALU.subtract),
                    [t, kn.after])
                ps.done(tq2, t)
                t = ac.do(lambda e, kn=kn: e.activation(kn.ap[:, :], kn.ap[:, :], ACT.Exp), [t])
                t = dv.do(lambda e, km=km, kn=kn, heads=heads: e.tensor_reduce(km.ap[:, 0, :], heads(kn.ap[:, :]), AX.X, ALU.add),
                          [t])
                t = dv.do(lambda e, km=km: e.reciprocal(km.ap[:, 1, :], km.ap[:, 0, :]), [t])
                t = dv.do(lambda e, km=km, n=n: e.tensor_scalar(km.ap[:, 0, :], km.ap[:, 1, :], route_top[:, n:n + 1],
                                                                None, ALU.mult), [t, t_top])
                t = dv.do(lambda e, km=km, kn=kn, heads=heads, over=over: e.tensor_tensor(
                    heads(kn.ap[:, :]), heads(kn.ap[:, :]), over(km.ap[:, 0, :]), ALU.mult), [t])
                km.done(t)
                ps = psum.take()
                tt = [pe.do(lambda e, p=p, ps=ps, kn=kn: e.transpose(ps.ap[:, p * P:(p + 1) * P],
                                                                     kn.ap[:, p * P:(p + 1) * P], ident),
                            [t, ps.after]) for p in range(PAIRS)]
                kn.done(tt[-1])
                tk2 = dv.do(lambda e, ps=ps, k2=k2, dn=dn: e.tensor_tensor(k2.ap[:, :], ps.ap[:, 0:BANK],
                                                                    dn[1].ap[:, :], ALU.mult), [tt, k2.after])
                dn[1].done(tk2)
                ps.done(tk2)
                qm = q2m.take()
                tm = [gp.do(lambda e, r=r, qm=qm, q2=q2, hb=hb: e.tensor_tensor(
                    qm.ap[:, r, :].rearrange("p (a c) -> p a c", a=PAIRS),
                    q2.ap[:, :].rearrange("p (a c) -> p a c", a=PAIRS),
                    hb.ap[:, r * P:(r + 1) * P].unsqueeze(1).to_broadcast([P, PAIRS, P]), ALU.mult),
                    [tq2, u4, qm.after]) for r in range(ROUTES)]
                hb.done(tm[-1])
                ps = psum.take()
                t = pe.do(lambda e, ps=ps, xt=xt: e.matmul(ps.ap[:, 0:BANK], xt, w("b_wv"), start=True, stop=True),
                          [base, ps.after])
                vv = v5.take()
                tv = [ac.do(lambda e, ps=ps, vv=vv: e.activation(vv.ap[:, 0, :], ps.ap[:, 0:BANK], ACT.Copy),
                            [t, vv.after])]
                for r in range(ROUTES):
                    if r % 2:
                        tv.append(ac.do(lambda e, r=r, ps=ps, vv=vv, n=n: e.activation(
                            vv.ap[:, 1 + r, :], ps.ap[:, 0:BANK], ACT.Copy, scale=route_hot[:, n, r:r + 1]),
                            [t, vv.after, hot]))
                    else:
                        tv.append(dv.do(lambda e, r=r, vv=vv, n=n: e.tensor_scalar(
                            vv.ap[:, 1 + r, :], vv.ap[:, 0, :], route_hot[:, n, r:r + 1], None, ALU.mult),
                            [tv[0], vv.after, hot]))
                ps.done(*tv)
                masked = []
                for q_, k_, tq, tk, ring, mask in ((q1, k1, tq1, tk1, masked1, w("tril")),
                                                   (q2, k2, tq2, tk2, masked2, mt.ap[:, :])):
                    ps = psum.take()
                    mm = []
                    for h in range(GLA_HEADS):
                        r0, c0 = (h % 2) * GLA_D, (h // 2) * P
                        mm.append(pe.do(lambda e, h=h, r0=r0, c0=c0, q_=q_, k_=k_, ps=ps: e.matmul(
                            ps.ap[:, at_head(h):at_head(h) + P], k_.ap[r0:r0 + GLA_D, c0:c0 + P],
                            q_.ap[r0:r0 + GLA_D, c0:c0 + P], start=True, stop=True), [tq, tk, ps.after]))
                    mk_ = ring.take()
                    t = dv.do(lambda e, ps=ps, mk_=mk_, mask=mask: e.tensor_tensor(
                        mk_.ap[:, :].rearrange("p (h c) -> p h c", c=P), ps.ap[:, :].rearrange("p (h c) -> p h c", c=P),
                        mask.unsqueeze(1).to_broadcast([P, GLA_HEADS, P]), ALU.mult), [mm, mk_.after, u3])
                    ps.done(t)
                    masked.append((mk_, t, mm[-1]))
                mt.done(masked[1][1])
                if n:
                    tf = dv.do(lambda e, prev=prev, dc=dc: e.tensor_tensor(
                        factor[:, :, :], prev.ap[:, :, 0, :], dc.ap[:, :, 1, :], ALU.mult), [dcs, gla_free["mid"]])
                    prev.done(tf)
                    t_mid = [gp.do(lambda e, p=p: e.tensor_tensor(
                        state_mid[:, p, :, :], state[:, p, :, :],
                        factor[:, p, :].unsqueeze(2).to_broadcast([P, DENSE, GLA_D]), ALU.mult),
                        [tf, last_state, gla_free["mid"]]) for p in range(PAIRS)]
                    t_dg = [ac.do(lambda e, r=r, p=p: e.activation(
                        state_dg[r * GLA_D:(r + 1) * GLA_D, p, :, r, :],
                        state_mid[r * GLA_D:(r + 1) * GLA_D, p, :, :], ACT.Copy), [t_mid, gla_free["dg"]])
                        for r in range(2) for p in range(PAIRS)]
                acc = psum.take()
                for (mk_, t, _) in masked:
                    for h in range(GLA_HEADS):
                        r0 = (h % 2) * GLA_D
                        last = pe.do(lambda e, h=h, r0=r0, mk_=mk_, acc=acc, vv=vv, first=mk_ is masked[0][0]: e.matmul(
                            acc.ap[r0:r0 + GLA_D, (h // 2) * P:(h // 2 + 1) * P],
                            vv.ap[:, 0, h * GLA_D:(h + 1) * GLA_D], mk_.ap[:, at_head(h):at_head(h) + P],
                            start=first and h < 2, stop=not first and n == 0, skip_group_check=True), [t, tv, acc.after])
                    mk_.done(last)
                if n:
                    for p in range(PAIRS):
                        for r in range(DENSE):
                            rhs = q1.ap[:, p * P:(p + 1) * P] if r == 0 else qm.ap[:, r - 1, p * P:(p + 1) * P]
                            last = pe.do(lambda e, p=p, r=r, rhs=rhs, acc=acc: e.matmul(
                                acc.ap[:, p * P:(p + 1) * P], state_dg[:, p, r, :, :].rearrange("p a b -> p (a b)"),
                                rhs, start=False, stop=(r == DENSE - 1), skip_group_check=True), [t_dg, tm])
                    gla_free["dg"] = [last]
                t_out = last
                q1.done(t_out)
                q2.done(tm[-1], masked[1][2])
                qm.done(t_out)
                nats = []
                for k_, tk, name, mm_last in ((k1, tk1, "k1nat", masked[0][2]), (k2, tk2, "k2nat", masked[1][2])):
                    ps = psum.take()
                    tt = [pe.do(lambda e, p=p, ps=ps, k_=k_: e.transpose(ps.ap[:, p * P:(p + 1) * P],
                                                                         k_.ap[:, p * P:(p + 1) * P], ident),
                                [tk, ps.after]) for p in range(PAIRS)]
                    k_.done(tt[-1], mm_last)
                    kn = gla[name].take()
                    t = ac.do(lambda e, ps=ps, kn=kn: e.activation(kn.ap[:, :], ps.ap[:, 0:BANK], ACT.Copy),
                              [tt, kn.after])
                    ps.done(t)
                    nats.append((kn, t))
                ups = []
                for p0 in range(0, PAIRS, 2):
                    ps = psum.take()
                    for p in (p0, p0 + 1):
                        o = (p - p0) * BANK
                        for r in range(2):
                            h = 2 * p + r
                            pe.do(lambda e, h=h, r=r, o=o, ps=ps, vv=vv, nats=nats: e.matmul(
                                ps.ap[r * GLA_D:(r + 1) * GLA_D, o:o + GLA_D],
                                nats[0][0].ap[:, h * GLA_D:(h + 1) * GLA_D],
                                vv.ap[:, 0, h * GLA_D:(h + 1) * GLA_D], start=True, stop=True,
                                skip_group_check=True), [nats[0][1], tv, ps.after])
                            last = pe.do(lambda e, h=h, r=r, o=o, ps=ps, vv=vv, nats=nats: e.matmul(
                                ps.ap[r * GLA_D:(r + 1) * GLA_D, o + GLA_D:o + DENSE * GLA_D],
                                nats[1][0].ap[:, h * GLA_D:(h + 1) * GLA_D],
                                vv.ap[:, 1:DENSE, h * GLA_D:(h + 1) * GLA_D], start=True, stop=True,
                                skip_group_check=True), [nats[1][1], tv])
                    src_ps = ps.ap[:, :].rearrange("p (a c) -> p a c", a=2)[:, :, 0:DENSE * GLA_D]
                    dst = state[:, p0:p0 + 2, :, :].rearrange("p a r d -> p a (r d)")
                    if n:
                        mid = state_mid[:, p0:p0 + 2, :, :].rearrange("p a r d -> p a (r d)")
                        t = dv.do(lambda e, dst=dst, mid=mid, src_ps=src_ps: e.tensor_tensor(dst, src_ps, mid, ALU.add),
                                  [last, t_mid])
                    else:
                        t = dv.do(lambda e, dst=dst, src_ps=src_ps: e.tensor_copy(dst, src_ps),
                                  [last, gla_free["mid"]])
                    ps.done(t)
                    ups.append(t)
                for kn, _ in nats:
                    kn.done(last)
                vv.done(last, t_out, (ac, ac.count), (dv, dv.count))
                last_state = ups
                gla_free["mid"] = ups + ([t_dg] if n else [])
                prev = dc
                sq, rs, f = gla["sq"].take(), gla["rs"].take(), gla["f"].take()
                t = ac.do(lambda e, acc=acc, sq=sq: e.activation(sq.ap[:, :], acc.ap[:, 0:BANK], ACT.Square),
                          [t_out, sq.after])
                t = pe.do(lambda e, acc=acc, sq=sq: e.matmul(acc.ap[:, BANK:2 * BANK], w("head_mean"), sq.ap[:, :],
                                                             start=True, stop=True), [t])
                sq.done(t)
                t = ac.do(lambda e, acc=acc, rs=rs: e.activation(rs.ap[:, :], acc.ap[:, BANK:2 * BANK], ACT.Ln,
                                                                 bias=w("eps")), [t, rs.after])
                t = ac.do(lambda e, rs=rs: e.activation(rs.ap[:, :], rs.ap[:, :], ACT.Exp, scale=-0.5), [t])
                t = dv.do(lambda e, acc=acc, rs=rs: e.scalar_tensor_tensor(
                    rs.ap[:, :], acc.ap[:, 0:BANK], w("b_norm"), rs.ap[:, :], ALU.mult, ALU.mult), [t])
                acc.done(t)
                t = dv.do(lambda e, rs=rs, f=f, tok=tok: e.tensor_tensor(
                    f.ap[:, :].rearrange("p (a c) -> p a c", a=PAIRS), rs.ap[:, :].rearrange("p (a c) -> p a c", a=PAIRS),
                    gate_T[:, :, tok], ALU.mult), [t, f.after, gated])
                rs.done(t)
                t_gate = t
                ps = psum.take()
                for p in range(PAIRS):
                    t = pe.do(lambda e, p=p, f=f, ps=ps: e.matmul(ps.ap[:, 0:P], f.ap[:, p * P:(p + 1) * P],
                                                                  w("b_wo", p * P, (p + 1) * P), start=(p == 0),
                                                                  stop=(p == PAIRS - 1)), [t_gate, ps.after])
                f.done(t)
                tile = x[:, b * NT + n, :]
                t = dv.do(lambda e, tile=tile, ps=ps: e.tensor_tensor(tile, tile, ps.ap[:, 0:P], ALU.add),
                          [t, x_ready[b * NT + n], last_norm[0]])
                ps.done(t)
                x_ready[b * NT + n] = t
            prev.done((dv, dv.count), (ac, ac.count))
            src.done((pe, pe.count))
            gla_free["gate"] = [t_gate]
            gla_free["route"] = gla_free["rows"] = [(pe, pe.count), (dv, dv.count), (ac, ac.count)]

        NG = EXPERTS + 1
        used[0] = 0
        moe_p = carve([P, NT, EXPERTS])
        moe_s = carve([P, 2, NT])
        moe_eq = carve([P, NT, EXPERTS])
        moe_run = carve([P, NT, EXPERTS])
        moe_hot = carve([P, 2, NT, EXPERTS])
        moe_w = carve([P, NT, NG])
        moe_tmp = carve([P, NT, NG])
        moe_bf = carve([P, NT, NG], BF16)
        keep16 = carve([P, NT, EXPERTS])
        moe_T = carve([P, T], BF16)
        moe_rows = carve([P, NT, P])
        act = Ring([carve([P, BANK]) for i in range(2)])
        hid = Ring([carve([P, BANK]) for i in range(2)])
        moe_free = [[]]

        def clear_moe():
            t = gp.do(lambda e: e.memset(keep16[:, :, :], 1.0))
            return [gp.do(lambda e: e.memset(keep16[:, :, 0:1], 0.0), [t]),
                    gp.do(lambda e: e.memset(moe_rows[:, :, :], 0.0))]

        def moe_layer(b):
            src, src_ready = layer_norm(b)
            ps = psum.take()
            free = moe_free[0]
            mm = [pe.do(lambda e, n=n: e.matmul(ps.ap[:, n * 32:n * 32 + NG], src.ap[:, n * P:(n + 1) * P], w("d_wg"),
                                                start=True, stop=True), [src_ready, ready, ps.after])
                  for n in range(NT)]
            lg = ps.ap[:, 0:NT * 32].rearrange("p (n e) -> p n e", e=32)
            t, used = softmax_small(lg[:, :, 0:EXPERTS], moe_p[:, :, :], moe_s, EXPERTS, [mm, free])
            s0 = ac.do(lambda e: e.activation(moe_w[:, :, EXPERTS], lg[:, :, EXPERTS], ACT.Exp, scale=-1.0), [mm, free])
            ps.done(used, s0)
            s1 = dv.do(lambda e: e.tensor_scalar(moe_w[:, :, EXPERTS], moe_w[:, :, EXPERTS], 1.0, None, ALU.add), [s0])
            s1 = dv.do(lambda e: e.reciprocal(moe_w[:, :, EXPERTS], moe_w[:, :, EXPERTS]), [s1])
            keep = keep16[:, :, :].rearrange("p a b -> p (a b)")
            t = dv.do(lambda e: e.tensor_reduce(moe_s[:, 0, :], moe_p[:, :, :], AX.X, ALU.max), [t])
            t = first_largest(moe_p[:, :, :], moe_eq[:, :, :], moe_run[:, :, :], moe_hot[:, 0, :, :], moe_s[:, 0, :],
                              keep, [t, ready])
            t = dv.do(lambda e: e.scalar_tensor_tensor(moe_tmp[:, :, 0:EXPERTS], moe_hot[:, 0, :, :], -2.0,
                                                       moe_p[:, :, :], ALU.mult, ALU.add), [t])
            t = dv.do(lambda e: e.tensor_reduce(moe_s[:, 1, :], moe_tmp[:, :, 0:EXPERTS], AX.X, ALU.max), [t])
            t = first_largest(moe_tmp[:, :, 0:EXPERTS], moe_eq[:, :, :], moe_run[:, :, :], moe_hot[:, 1, :, :],
                              moe_s[:, 1, :], keep, [t])
            t = dv.do(lambda e: e.tensor_tensor(moe_hot[:, 0, :, :], moe_hot[:, 0, :, :], moe_hot[:, 1, :, :], ALU.add), [t])
            t = dv.do(lambda e: e.tensor_tensor(moe_hot[:, 0, :, :], moe_hot[:, 0, :, :], moe_p[:, :, :], ALU.mult), [t])
            t = dv.do(lambda e: e.tensor_tensor(moe_s[:, 0, :], moe_s[:, 0, :], moe_s[:, 1, :], ALU.add), [t])
            t = dv.do(lambda e: e.reciprocal(moe_s[:, 0, :], moe_s[:, 0, :]), [t])
            t = dv.do(lambda e: e.tensor_tensor(moe_w[:, :, 0:EXPERTS], moe_hot[:, 0, :, :],
                                                moe_s[:, 0, :].unsqueeze(2).to_broadcast([P, NT, EXPERTS]),
                                                ALU.mult), [t])
            t = split_small(moe_w[:, :, :], moe_rows, NG, moe_tmp[:, :, :], moe_bf[:, :, :], [t, s1, free])
            g, tt = turn_rows(moe_rows, [(moe_T, 1.0)], t, free)
            for a, c in blocks(T):
                acc = psum.take()
                for f in range(MOE_TILES):
                    ps = psum.take()
                    pw = psum.take()
                    mg = pe.do(lambda e, f=f, a=a, c=c, ps=ps: e.matmul(ps.ap[:, 0:c - a], w("d_gate", f * P, (f + 1) * P),
                                                                        src.ap[:, a:c], start=True, stop=True),
                               [src_ready, ps.after])
                    mu = pe.do(lambda e, f=f, a=a, c=c, ps=ps: e.matmul(
                        ps.ap[:, BANK:BANK + c - a], w("d_up", f * P, (f + 1) * P), src.ap[:, a:c], start=True, stop=True),
                        [src_ready])
                    s = min(f, EXPERTS // 2)
                    mw = pe.do(lambda e, s=s, a=a, c=c, pw=pw: e.matmul(
                        pw.ap[:, 0:c - a], w3["moe_bcast"][:, s * P:(s + 1) * P], moe_T[:, a:c], start=True, stop=True),
                        [g, pw.after])
                    ag, hd = act.take(), hid.take()
                    t = ac.do(lambda e, a=a, c=c, ps=ps, ag=ag: e.activation(ag.ap[:, 0:c - a], ps.ap[:, 0:c - a], ACT.Silu),
                              [mg, ag.after])
                    t = dv.do(lambda e, a=a, c=c, ps=ps, ag=ag: e.tensor_tensor(
                        ag.ap[:, 0:c - a], ag.ap[:, 0:c - a], ps.ap[:, BANK:BANK + c - a], ALU.mult), [t, mu])
                    ps.done(t)
                    t = dv.do(lambda e, a=a, c=c, pw=pw, ag=ag, hd=hd: e.tensor_tensor(
                        hd.ap[:, 0:c - a], ag.ap[:, 0:c - a], pw.ap[:, 0:c - a], ALU.mult), [t, mw, hd.after])
                    pw.done(t)
                    ag.done(t)
                    for n in range((c - a) // P):
                        m = pe.do(lambda e, f=f, n=n, hd=hd, acc=acc: e.matmul(
                            acc.ap[:, n * P:(n + 1) * P], hd.ap[:, n * P:(n + 1) * P], w("d_down", f * P, (f + 1) * P),
                            start=(f == 0 and n == 0), stop=(f == MOE_TILES - 1), skip_group_check=True),
                            [t, acc.after])
                    hd.done(m)
                n0, n1 = b * NT + a // P, b * NT + c // P
                t = dv.do(lambda e, a=a, c=c, n0=n0, n1=n1, acc=acc: e.tensor_tensor(
                    x[:, n0:n1, :], x[:, n0:n1, :], acc.ap[:, 0:c - a].rearrange("p (n d) -> p n d", d=P), ALU.add),
                    [m, x_ready[n0:n1], last_norm[0]])
                acc.done(t)
                stored.append(dma(out_dram[:, n0:n1, :], x[:, n0:n1, :], [t]))
            src.done((pe, pe.count))
            moe_free[0] = [(pe, pe.count), (dv, dv.count), (ac, ac.count)]

        stored = []
        layers = ((window_attention, (clear_attention,), load_b, "c"), (gla_layer, (clear_gla,), (), "d"),
                  (causal_mixed, (clear_attention, clear_recurrence), (), None), (moe_layer, (clear_moe,), (), None))
        next_loaded = []
        for layer, clears, _, next_weights in layers:
            ready += next_loaded
            for clear in clears:
                ready += clear()
            for b in range(batches):
                layer(b)
            end_of_layer()
            next_loaded = load(next_weights) if next_weights else []
        sp.wait(stored)


def pack(parts):
    place, width = {}, {}
    for name, a in parts.items():
        layer = "s" if name in BF_CONSTANTS else "l" if name[-1] in "ab" and name[0] == "b" else name[0] if name[1] == "_" else "k"
        place[name] = (layer, width.get(layer, 0), a.shape[0], a.shape[1])
        width[layer] = width.get(layer, 0) + a.shape[1]
    out = {layer: np.zeros((P, n), np.float32) for layer, n in width.items()}
    for name, a in parts.items():
        layer, first, rows, cols = place[name]
        out[layer][:rows, first:first + cols] = a
    return out, place


def weight_columns(i):
    rows = lambda a: a.reshape(-1, P, a.shape[1]).transpose(1, 0, 2).reshape(P, -1)
    every = lambda v: np.tile(v.reshape(1, -1), (P, 1))
    col = lambda v: v.reshape(-1, 1)
    qkv, bias = i["L1_attn_Wqkv_w"], i["L1_attn_Wqkv_b"]
    per_head = lambda a: a.reshape(P, HD)
    e_rows = lambda a: a.reshape(EXPERTS * EXPERT_HID, P)
    down = np.concatenate([i["L1_ffn_We_down"].transpose(0, 2, 1).reshape(-1, P), i["L1_ffn_Ws_down"].T], 0)
    return {
        "a_wq": i["L0_attn_Wq"].T, "a_wk": i["L0_attn_Wk"].T, "a_wv": i["L0_attn_Wv"].T, "a_wo": i["L0_attn_Wo"].T,
        "b_wq": i["L0_ffn_Wq"], "b_wk": i["L0_ffn_Wk"], "b_wv": i["L0_ffn_Wv"],
        "b_q2a": i["L0_ffn_Wqa"].T, "b_q2b": i["L0_ffn_Wqb"], "b_k2a": i["L0_ffn_Wka"].T, "b_k2b": i["L0_ffn_Wkb"],
        "b_g1a": i["L0_ffn_Wg1a"].T, "b_g1b": i["L0_ffn_Wg1b"], "b_g2a": i["L0_ffn_Wg2a"].T, "b_g2b": i["L0_ffn_Wg2b"],
        "b_ga": i["L0_ffn_Wga"].T, "b_gb": i["L0_ffn_Wgb"],
        "b_bg1": every(i["L0_ffn_bg1"]), "b_bg2": every(i["L0_ffn_bg2"]),
        "b_we": i["L0_ffn_We"], "b_norm": col(np.tile(i["L0_ffn_norm_w"], 2)), "b_wo": rows(i["L0_ffn_Wo"]),
        "c_wq": qkv[:, 0:P], "c_wk": qkv[:, P:2 * P], "c_wv": qkv[:, 2 * P:],
        "c_bq": col(bias[0:P]), "c_bk": col(bias[P:2 * P]), "c_bv": col(bias[2 * P:]), "c_bv_row": every(bias[2 * P:]),
        "c_lambda": per_head(i["L1_attn_Lambda_raw"]), "c_gamma": per_head(i["L1_attn_Gamma"]),
        "c_static": per_head(i["L1_attn_W_static"]),
        "c_gw1": i["L1_attn_gate_w1"], "c_gb1": col(i["L1_attn_gate_b1"]),
        "c_gw2": np.concatenate([i["L1_attn_gate_w2"], i["L1_attn_gate_b2"].reshape(1, -1)], 0),
        "c_wo": i["L1_attn_out_w"], "c_bo_row": every(i["L1_attn_out_b"]),
        "d_wg": np.concatenate([i["L1_ffn_Wg"], i["L1_ffn_Wsg"]], 0).T,
        "d_gate": np.concatenate([e_rows(i["L1_ffn_We_gate"]), i["L1_ffn_Ws_gate"]], 0).T,
        "d_up": np.concatenate([e_rows(i["L1_ffn_We_up"]), i["L1_ffn_Ws_up"]], 0).T,
        "d_down": rows(down),
    }


def kernel(**inputs):
    import concourse.bacc as _bacc
    from concourse.bass_utils import run_bass_kernel_spmd as _run

    i = {k: np.asarray(v) for k, v in inputs.items()}
    x = np.ascontiguousarray(i["L0_attn_x"])
    packed, place = pack({**constant_columns(), **weight_columns(i)})
    nc = _bacc.Bacc("TRN2", target_bir_lowering=False, num_devices=1)
    x_in = nc.dram_tensor("x_in", x.shape, F32, kind="ExternalInput").ap()
    w_in = {k: nc.dram_tensor(f"w_{k}", a.shape, F32, kind="ExternalInput").ap() for k, a in packed.items()}
    x_out = nc.dram_tensor("x_out", x.shape, F32, kind="ExternalOutput").ap()
    build(nc, x_in, w_in, x_out, place, x.shape[0], x.shape[1])
    r = _run(nc, [{"x_in": x, **{f"w_{k}": a for k, a in packed.items()}}], core_ids=[0])
    return r.results[0]["x_out"]
```

```python
from contextlib import ExitStack

import numpy as np

import concourse.bass as bass
from concourse import mybir

ALU = mybir.AluOpType
ACT = mybir.ActivationFunctionType
AX = mybir.AxisListType
F32 = mybir.dt.float32
BF16 = mybir.dt.bfloat16

P = 128
BANK = 512
EPS = 1e-5
HEADS, HD = 16, 8
GROUP = 4
WINDOW = 64
GLA_HEADS, GLA_D = 8, 64
PAIRS = GLA_HEADS // 2
GLA_CHUNK = 64
ROUTES = 4
EXPERTS, EXPERT_HID, SHARED_HID = 16, 64, 256
MOE_TILES = (EXPERTS * EXPERT_HID + SHARED_HID) // P
NORMALIZER = 16.0
SPLIT = 3
NEG_ROW = 96
ATT_SCALE = float(1.0 / np.sqrt(HD))


def flat(tokens):
    for t in tokens:
        if isinstance(t, list):
            yield from flat(t)
        elif t is not None:
            yield t


class Lane:

    def __init__(self, eng, sem, one_by_one=False):
        self.eng, self.sem, self.count, self.seen, self.held = eng, sem, 0, {}, []
        self.one_by_one = one_by_one

    def wait(self, after):
        need = {}
        held, self.held = self.held, []
        for lane, value in flat([list(after), held]):
            if value > self.seen.get(lane, 0):
                need[lane] = max(need.get(lane, 0), value)
        self.seen.update(need)
        for lane, value in need.items():
            self.eng.wait_ge(lane.sem, value)

    def do(self, op, after=()):
        if self.one_by_one:
            after = [list(after), [(self, self.count)]]
        self.wait(after)
        op(self.eng).then_inc(self.sem, 1)
        self.count += 1
        return (self, self.count)


class Channel:

    def __init__(self, sem):
        self.sem, self.count = sem, 0


class Slot:

    def __init__(self, ring, ap, after):
        self.ring, self.ap, self.after = ring, ap, after

    def done(self, *tokens):
        self.ring.free.append((self.ap, list(tokens)))


class Ring:
    def __init__(self, buffers):
        self.free = [(b, []) for b in buffers]

    def take(self):
        ap, after = self.free.pop(0)
        return Slot(self, ap, after)


def weave(streams, beside=()):
    left, extra = list(streams), list(beside)
    done = object()
    while left:
        for stream in left[:]:
            if next(stream, done) is done:
                left.remove(stream)
        for stream in extra[:]:
            if next(stream, done) is done:
                extra.remove(stream)


def all_of(stream):
    while True:
        try:
            next(stream)
        except StopIteration as end:
            return end.value


def constant_columns():
    r = np.arange(P)[:, None]
    c = np.arange(P)[None, :]
    w = np.arange(P + WINDOW)[None, :]
    mid = (r < GLA_CHUNK) * np.ones((1, 1))
    out = {
        "ident": r == c,
        "eps": np.full((P, 1), EPS),
        "win_row": ~((w > r) & (w <= r + WINDOW)) * -(2.0 ** 60),
        "win_col": ~((w >= r) & (w < r + WINDOW)) * -(2.0 ** 60),
        "causal_row": (c > r) * -100.0,
        "causal_col": (r > c) * -100.0,
        "tril": (r <= c) * 1.0,
        "gate_sum": np.concatenate([(r <= c) * 1.0 - mid, 1 - mid, mid], 1) / NORMALIZER,
        "half": np.concatenate([1 - mid, mid], 1) / NORMALIZER,
        "head_mean": (r // GLA_D == c // GLA_D) / GLA_D,
        "route_first": (r < ROUTES) * 1.0,
        "ones": np.ones((P, 1)),
    }
    part_rows = SPLIT * ROUTES
    sel = [((r % ROUTES == e) & (r < part_rows)) * np.ones((1, P)) for e in range(ROUTES)]
    out["route_bcast"] = np.concatenate(sel, 1)
    n = EXPERTS + 1
    sel = [((r % n == np.minimum(2 * f + c // EXPERT_HID, EXPERTS)) & (r < SPLIT * n)) * 1.0
           for f in range(EXPERTS // 2 + 1)]
    sel[-1] = ((r % n == EXPERTS) & (r < SPLIT * n)) * np.ones((1, P))
    out["moe_bcast"] = np.concatenate(sel, 1)
    return {k: np.asarray(v, np.float32) for k, v in out.items()}


REGION_OF = {"k": "constants", "a": "small", "b": "large", "c": "small", "d": "large"}
ARENA = 40500

BF_CONSTANTS = ("win_row", "win_col", "causal_row", "causal_col", "route_bcast", "moe_bcast")


def build(nc, x_in, packed, x_out, place, batches, T):
    sizes = {k: a.shape[1] for k, a in packed.items()}
    region_of = REGION_OF
    NT = T // P
    HALF = min(BANK, T)
    ctx = ExitStack()
    with ctx:
        def sb(name, shape, dt=F32):
            return ctx.enter_context(nc.sbuf_tensor(name, shape, dt))

        def sem(name):
            return ctx.enter_context(nc.semaphore(name))

        pe, dv, ac = (Lane(eng, sem(f"count_{n}")) for n, eng in
                      (("tensor", nc.tensor), ("vector", nc.vector), ("scalar", nc.scalar)))
        gp = Lane(nc.gpsimd, sem("count_gpsimd"), one_by_one=True)
        sp = Lane(nc.sync, None)
        channels = [Channel(sem(f"dma_{i}")) for i in range(24)]
        turn = [0]

        def dma(out, in_, after=()):
            ch = channels[turn[0] % len(channels)]
            turn[0] += 1
            sp.wait([list(after), [(ch, ch.count)]])
            nc.sync.dma_start(out, in_).then_inc(ch.sem, 16)
            ch.count += 16
            return (ch, ch.count)

        def exp_set(lane):
            lane.eng.preload_act_table_set("natural_log_exp_and_others")

        def end_of_layer():
            every = [(lane, lane.count) for lane in (pe, dv, ac, gp)] + [(ch, ch.count) for ch in channels]
            for lane in (pe, dv, ac, gp, sp):
                lane.held = every

        regions = {r: sb(f"weights_{r}", [P, max(n for k, n in sizes.items() if region_of.get(k) == r)])
                   for r in sorted(set(region_of.values()))}

        def w(name, a=0, b=None):
            layer, first, rows, cols = place[name]
            t = low_rank if layer == "l" else regions[region_of[layer]]
            return t[0:rows, first + a:first + (cols if b is None else b)]

        arena = sb("arena", [P, ARENA])
        used = [0]

        def carve(shape, dt=F32):
            n = int(np.prod(shape[1:]))
            words = n if dt == F32 else (n + 1) // 2
            ap = arena[0:shape[0], used[0]:used[0] + words]
            used[0] += words
            assert used[0] <= ARENA, used[0]
            if dt != F32:
                ap = ap.bitcast(dt)
            if len(shape) > 2:
                names = "abcdef"[:len(shape) - 1]
                ap = ap.rearrange(f"p ({' '.join(names)}) -> p {' '.join(names)}", **dict(zip(names, shape[1:])))
            return ap

        x = sb("x", [P, batches * NT, P])
        x_ready = [None] * (batches * NT)
        psum = Ring([ctx.enter_context(nc.psum_tensor(f"psum{i}", [P, 2 * BANK], F32)) for i in range(4)])

        stats = sb("stats", [P, NT, 6])
        moments = sb("moments", [P, NT, 2])
        rstd = sb("rstd", [P, 4, NT])
        xn = Ring([sb(f"xn{i}", [P, P]) for i in range(4)])
        xnT = Ring([sb("xnT0", [P, T])])

        w3 = {n: sb(f"bf_{n}", [P, place[n][3]], BF16) for n in BF_CONSTANTS}
        ident = w("ident")
        ident_bf = {v: sb(f"ident_{i}", [P, P], BF16) for i, v in enumerate((100.0, 2.0 ** 60))}

        q_stack = carve([P, HEADS, T], BF16)
        k_stack = carve([P, HEADS, T], BF16)
        full = {s: carve([P, T]) for s in "qkv"}
        rest = carve([P, T])
        parts = Ring([carve([P, SPLIT, T], BF16) for i in range(1)])
        v_nat = carve([P, NT, HEADS, 32])
        neg_max = carve([P, NT, 2, HEADS])
        neg_parts = carve([P, NT, SPLIT, GROUP])
        neg_rest = carve([P, NT, GROUP])
        neg_bf = carve([P, NT, GROUP], BF16)
        neg_T = carve([SPLIT * GROUP, T], BF16)
        probs = Ring([carve([P, 2 * BANK]) for i in range(2)])
        o_T = carve([P, HEADS // GROUP, T])
        att = Ring([carve([P, P]) for i in range(2)])
        attT = Ring([carve([P, P]) for i in range(2)])
        inv_den = Ring([carve([P, HEADS]) for i in range(2)])

        def load(layer, after=()):
            n = sizes[layer]
            return [dma(regions[REGION_OF[layer]][:, a:min(n, a + 2048)], packed[layer][:, a:min(n, a + 2048)], after)
                    for a in range(0, n, 2048)]

        staged = arena[:, 0:sizes["s"]]
        loaded = load("k") + [dma(staged, packed["s"])] + load("a")
        x_dram = x_in.rearrange("b (n p) d -> p (b n) d", p=P)
        out_dram = x_out.rearrange("b (n p) d -> p (b n) d", p=P)
        for b in range(batches):
            t = dma(x[:, b * NT:(b + 1) * NT, :], x_dram[:, b * NT:(b + 1) * NT, :])
            for n in range(NT):
                x_ready[b * NT + n] = t

        load_b = load("b")

        ready = []
        for n in BF_CONSTANTS:
            ready.append(ac.do(lambda e, n=n: e.activation(w3[n][:, :], staged[:, place[n][1]:place[n][1] + place[n][3]], ACT.Copy), loaded))
        for v, t in ident_bf.items():
            ready.append(ac.do(lambda e, v=v, t=t: e.activation(t[:, :], ident, ACT.Copy, scale=v), loaded))
        ready += loaded
        end_of_layer()

        last_norm = [[]]
        normed = {}

        def layer_norm(b):
            got = []
            norm_free = last_norm[0]
            exp_set(ac)
            for n in range(NT):
                t = dv.do(lambda e, n=n: e.bn_stats(stats[:, n, :], x[:, b * NT + n, :]),
                          [x_ready[b * NT + n], norm_free])
                got.append(dv.do(lambda e, n=n: e.bn_aggr(moments[:, n, :], stats[:, n, :]), [t, norm_free]))
            t = ac.do(lambda e: e.activation(rstd[:, 0, :], moments[:, :, 1], ACT.Ln, bias=w("eps")),
                      [got, norm_free, ready])
            t = ac.do(lambda e: e.activation(rstd[:, 1, :], rstd[:, 0, :], ACT.Exp, scale=-0.5), [t])
            t = dv.do(lambda e: e.tensor_tensor(rstd[:, 2, :], rstd[:, 1, :], rstd[:, 1, :], ALU.mult), [t])
            t = dv.do(lambda e: e.scalar_tensor_tensor(rstd[:, 0, :], moments[:, :, 1], EPS, rstd[:, 2, :],
                                                       ALU.add, ALU.mult), [t])
            t = dv.do(lambda e: e.tensor_scalar(rstd[:, 2, :], rstd[:, 0, :], -0.5, 1.5, ALU.mult, ALU.add), [t])
            t_r = dv.do(lambda e: e.tensor_tensor(rstd[:, 3, :], rstd[:, 1, :], rstd[:, 2, :], ALU.mult), [t])
            yield
            out = xnT.take()
            ends, norms = [], []
            for n0 in range(0, NT, 4):
                ps = psum.take()
                k = min(4, NT - n0)
                turned = []
                for n in range(n0, n0 + k):
                    s = xn.take()
                    t = dv.do(lambda e, n=n, s=s: e.tensor_scalar(
                        s.ap[:, :], x[:, b * NT + n, :], moments[:, n, 0:1], rstd[:, 3, n:n + 1],
                        ALU.subtract, ALU.mult), [t_r, s.after])
                    norms.append(t)
                    t = pe.do(lambda e, n=n, s=s, ps=ps, n0=n0: e.transpose(
                        ps.ap[:, (n - n0) * P:(n - n0 + 1) * P], s.ap[:, :], ident), [t, ps.after, ready])
                    s.done(t)
                    turned.append(t)
                t = ac.do(lambda e, ps=ps, n0=n0, k=k: e.activation(
                    out.ap[:, n0 * P:(n0 + k) * P], ps.ap[:, 0:k * P], ACT.Copy), [turned, out.after])
                ps.done(t)
                ends.append(t)
                yield
            last_norm[0] = normed[b] = norms
            return out, ends

        def blocks(n):
            return [(a, min(a + BANK, n)) for a in range(0, n, BANK)]

        scratch = {s: nc.dram_tensor(f"scratch_{s}", (SPLIT, P, T), BF16, kind="Internal").ap() for s in "qk"}
        whole = {s: nc.dram_tensor(f"whole_{s}", (P, T), F32, kind="Internal").ap() for s in "qk"}
        ones_bf = rest[0:SPLIT, 0:T // 2].bitcast(BF16)
        stacks = {"q": q_stack, "k": k_stack}
        GROUPS = HEADS // GROUP

        def clear_attention():
            got = [gp.do(lambda e: e.memset(s[64:P, :, :], 0.0)) for s in (q_stack, k_stack)]
            t = gp.do(lambda e: e.memset(ones_bf[:, :], 1.0))
            for h in range(HEADS):
                got.append(dma(k_stack[NEG_ROW:NEG_ROW + SPLIT, h, :], ones_bf[:, :], [t] + got[0:2]))
            t = gp.do(lambda e: e.memset(v_nat[:, :, :, :], 0.0))
            got.append(gp.do(lambda e: e.memset(v_nat[:, :, :, HD:HD + 1], 1.0), [t]))
            return got

        free = {"full_q": [], "full_k": [], "full_v": [], "rest": [], "scratch_q": [], "scratch_k": [],
                "stack": {g: [] for g in range(GROUPS)}, "v_nat": [], "neg": [], "neg_T": [], "o_T": [],
                "whole": [], "alpha": []}
        there = {}
        stacked = {}
        shifted = {}
        vals_ready = {}
        weighed = {}

        def split_to_scratch(W, src, src_ready, side, bias, b):
            ps = psum.take()
            mm = [pe.do(lambda e: e.matmul(ps.ap[:, a:c], W, src.ap[:, a:c], start=True, stop=True),
                        [src_ready, ps.after, ready]) for a, c in blocks(T)]
            scale = ATT_SCALE if side == "k" else 1.0
            dst = full[side]
            if bias is None:
                t = ac.do(lambda e: e.activation(dst[:, :], ps.ap[:, 0:T], ACT.Copy, scale=scale),
                          [mm, free["full_" + side]])
            else:
                t = dv.do(lambda e: e.tensor_scalar(dst[:, :], ps.ap[:, 0:T], bias, scale, ALU.add, ALU.mult),
                          [mm, free["full_" + side]])
            ps.done(t)
            full_ready = t
            yield
            pt = parts.take()
            hi = ac.do(lambda e: e.activation(pt.ap[:, 0, :], dst[:, :], ACT.Copy), [t, pt.after])
            t = dv.do(lambda e: e.tensor_tensor(rest[:, :], dst[:, :], pt.ap[:, 0, :], ALU.subtract), [hi, free["rest"]])
            yield
            mid = ac.do(lambda e: e.activation(pt.ap[:, 1, :], rest[:, :], ACT.Copy), [t, pt.after])
            lo = dv.do(lambda e: e.tensor_tensor(pt.ap[:, 2, :], rest[:, :], pt.ap[:, 1, :], ALU.subtract),
                       [mid, pt.after])
            free["rest"] = [lo]
            free["full_" + side] = [t]
            there[side, b] = dma(scratch[side].rearrange("a (h d) t -> (h d) a t", d=HD), pt.ap[:, :, :],
                                 [hi, mid, lo, free["scratch_" + side]])
            free["scratch_" + side] = []
            pt.done(there[side, b])
            there["full_" + side, b] = full_ready
            yield

        def load_stacks(b, g):
            heads = slice(g * GROUP, (g + 1) * GROUP)
            got = []
            for side in "qk":
                for row in range(SPLIT * SPLIT):
                    part = row // SPLIT if side == "q" else row % SPLIT
                    rows = scratch[side][part, g * GROUP * HD:(g + 1) * GROUP * HD, :].rearrange("(h d) t -> d h t", d=HD)
                    t = dma(stacks[side][row * HD:(row + 1) * HD, heads, :], rows,
                            [there[side, b], free["stack"][g], ready])
                    got.append(t)
                    free["scratch_" + side].append(t)
            stacked[b, g] = got

        def values(W, src, src_ready, bias_row, b):
            got = []
            for n0 in range(0, NT, 4):
                ps = psum.take()
                k = min(4, NT - n0)
                mm = [pe.do(lambda e: e.matmul(ps.ap[:, (n - n0) * P:(n - n0 + 1) * P], src.ap[:, n * P:(n + 1) * P],
                                               W, start=True, stop=True), [src_ready, ps.after, ready])
                      for n in range(n0, n0 + k)]
                cols = []
                for n in range(n0, n0 + k):
                    o = v_nat[:, n, :, 0:HD]
                    i = ps.ap[:, (n - n0) * P:(n - n0 + 1) * P].rearrange("p (h d) -> p h d", d=HD)
                    if bias_row is None:
                        t = ac.do(lambda e: e.activation(o, i, ACT.Copy), [mm, free["v_nat"], ready])
                    else:
                        t = dv.do(lambda e: e.tensor_tensor(o, i, bias_row.rearrange("p (h d) -> p h d", d=HD),
                                                            ALU.add), [mm, free["v_nat"], ready])
                    cols.append(t)
                ps.done(*cols)
                got += cols
            vals_ready[b] = got
            src.done(*[(pe, pe.count)])

        def spread_maxima(b, g, maxima):
            view = neg_max[:, :, 0, g * GROUP:(g + 1) * GROUP]
            t = [dv.do(lambda e: e.tensor_copy(neg_bf[:, :, :], view), [maxima, free["neg"]])]
            t = dv.do(lambda e: e.tensor_copy(neg_parts[:, :, 0, :], neg_bf[:, :, :]), [t, free["neg"]])
            t = dv.do(lambda e: e.tensor_tensor(neg_rest[:, :, :], view, neg_parts[:, :, 0, :], ALU.subtract), [t])
            t = dv.do(lambda e: e.tensor_copy(neg_bf[:, :, :], neg_rest[:, :, :]), [t])
            t = dv.do(lambda e: e.tensor_copy(neg_parts[:, :, 1, :], neg_bf[:, :, :]), [t])
            t = dv.do(lambda e: e.tensor_tensor(neg_parts[:, :, 2, :], neg_rest[:, :, :], neg_parts[:, :, 1, :],
                                                ALU.subtract), [t])
            rows = SPLIT * GROUP
            ps = psum.take()
            tt = [pe.do(lambda e: e.transpose(ps.ap[0:rows, n * P:(n + 1) * P],
                                              neg_parts[:, n, :, :].rearrange("p a h -> p (a h)"), ident),
                        [t, ps.after]) for n in range(NT)]
            free["neg"] = [tt[-1], t]
            t = ac.do(lambda e: e.activation(neg_T[:, :], ps.ap[0:rows, 0:T], ACT.Copy), [tt, free["neg_T"]])
            ps.done(t)
            sent = [dma(q_stack[NEG_ROW + a:NEG_ROW + a + 1, g * GROUP:(g + 1) * GROUP, :],
                        neg_T[a * GROUP:(a + 1) * GROUP, :], [t, free["stack"][g]]) for a in range(SPLIT)]
            free["neg_T"] = sent
            shifted[b, g] = sent

        def maxima_window(b, g):
            got = []
            for n in range(NT):
                lo = max(0, n * P - WINDOW)
                cut = lo - (n * P - WINDOW)
                cols = P + WINDOW - cut
                ps = psum.take()
                mm = []
                for i in range(GROUP):
                    o = ps.ap[:, i * 256:i * 256 + cols]
                    h = g * GROUP + i
                    pe.do(lambda e: e.matmul(o, q_stack[0:NEG_ROW, h, n * P:(n + 1) * P],
                                             k_stack[0:NEG_ROW, h, lo:(n + 1) * P], start=True, stop=False),
                          [stacked[b, g], ps.after])
                    mm.append(pe.do(lambda e: e.matmul(o, ident_bf[2.0 ** 60][:, :],
                                                       w3["win_row"][:, cut:P + WINDOW], start=False, stop=True),
                                    [ready]))
                t = dv.do(lambda e: e.tensor_reduce(
                    neg_max[:, n, 0, g * GROUP:(g + 1) * GROUP],
                    ps.ap[:, :].rearrange("p (i c) -> p i c", i=GROUP)[:, :, 0:cols], AX.X, ALU.max, negate=True), [mm])
                ps.done(t)
                got.append(t)
                yield
            spread_maxima(b, g, got)

        def maxima_causal(b, g):
            got = []
            for n in range(NT):
                pieces = []
                for half, (a, c) in enumerate(blocks((n + 1) * P)):
                    width = c - a
                    per = 2 if 2 * width <= BANK else 1
                    for h0 in range(g * GROUP, (g + 1) * GROUP, 2 * per):
                        ps = psum.take()
                        mm = []
                        for i in range(2 * per):
                            o = ps.ap[:, (i // per) * BANK + (i % per) * width:][:, 0:width]
                            h = h0 + i
                            diag = c == (n + 1) * P
                            t = pe.do(lambda e: e.matmul(o, q_stack[0:NEG_ROW, h, n * P:(n + 1) * P],
                                                         k_stack[0:NEG_ROW, h, a:c], start=True, stop=not diag),
                                      [stacked[b, g], ps.after])
                            if diag:
                                t = pe.do(lambda e: e.matmul(o[:, width - P:width], ident_bf[100.0][:, :],
                                                             w3["causal_row"][:, :], start=False, stop=True), [ready])
                            mm.append(t)
                        src = ps.ap[:, :].rearrange("p (k c) -> p k c", k=2)[:, :, 0:per * width]
                        if per > 1:
                            src = src.rearrange("p k (i c) -> p k i c", i=per)
                            dst = neg_max[:, n, half, h0:h0 + 2 * per].rearrange("p (k i) -> p k i", k=2)
                        else:
                            dst = neg_max[:, n, half, h0:h0 + 2]
                        t = dv.do(lambda e: e.tensor_reduce(dst, src, AX.X, ALU.max, negate=True), [mm])
                        ps.done(t)
                        pieces.append(t)
                        yield
                if (n + 1) * P > BANK:
                    both = neg_max[:, n, :, g * GROUP:(g + 1) * GROUP]
                    pieces = [dv.do(lambda e: e.tensor_tensor(both[:, 0, :], both[:, 0, :], both[:, 1, :], ALU.min),
                                    [pieces])]
                got += pieces
            spread_maxima(b, g, got)

        def weigh_window(b, g):
            acc = psum.take()
            operands = [stacked[b, g], shifted[b, g]]
            later = None
            crossed = False
            for j in range(NT):
                q0 = j * P
                cols = min(P + WINDOW, T - q0)
                ps = psum.take()
                mm = []
                for i in range(GROUP):
                    h = g * GROUP + i
                    o = ps.ap[:, i * 256:i * 256 + cols]
                    pe.do(lambda e: e.matmul(o, k_stack[:, h, q0:q0 + P], q_stack[:, h, q0:q0 + cols], start=True,
                                             stop=False), [operands, ps.after])
                    mm.append(pe.do(lambda e: e.matmul(o, ident_bf[2.0 ** 60][:, :], w3["win_col"][:, 0:cols],
                                                       start=False, stop=True), [ready]))
                pr = probs.take()
                view = lambda ap: ap[:, :].rearrange("p (i c) -> p i c", i=GROUP)[:, :, 0:cols]
                t = ac.do(lambda e: e.activation(view(pr.ap), view(ps.ap), ACT.Exp), [mm, pr.after])
                ps.done(t)

                def weigh(j, q0, cols, pr, t, crossed):
                    cuts = [(q0, BANK), (BANK, q0 + cols)] if q0 < BANK < q0 + cols else [(q0, q0 + cols)]
                    for a, c in cuts:
                        start = j == 0 or (a == BANK and not crossed)
                        for i in range(GROUP):
                            last = pe.do(lambda e: e.matmul(
                                acc.ap[32 * i:32 * i + 32, a:c], v_nat[:, j, g * GROUP + i, :],
                                pr.ap[:, i * 256 + a - q0:i * 256 + c - q0], start=start, stop=(j == NT - 1),
                                skip_group_check=True), [t, vals_ready[b], acc.after])
                    pr.done(last)
                    return last, crossed or len(cuts) == 2

                if later:
                    _, crossed = weigh(*later, crossed)
                later = (j, q0, cols, pr, t)
                yield
            last, _ = weigh(*later, crossed)
            t = ac.do(lambda e: e.activation(o_T[:, g, :], acc.ap[:, 0:T], ACT.Copy), [last, free["o_T"]])
            acc.done(t)
            weighed.setdefault(b, []).append(t)
            free["stack"][g] = [last]
            free["v_nat"] = [last]

        def weigh_causal(b, g):
            operands = [stacked[b, g], shifted[b, g]]
            for a0, c0 in blocks(T):
                acc = psum.take()
                keys = c0 // P
                later = None
                for j in range(keys):
                    a = max(a0, j * P)
                    n = c0 - a
                    for i0 in range(0, GROUP, 2):
                        ps = psum.take()
                        mm = []
                        for i in range(2):
                            h = g * GROUP + i0 + i
                            diag = a == j * P
                            t = pe.do(lambda e: e.matmul(ps.ap[:, i * BANK:i * BANK + n], k_stack[:, h, j * P:(j + 1) * P],
                                                         q_stack[:, h, a:c0], start=True, stop=not diag),
                                      [operands, ps.after])
                            if diag:
                                t = pe.do(lambda e: e.matmul(ps.ap[:, i * BANK:i * BANK + P], ident_bf[100.0][:, :],
                                                             w3["causal_col"][:, :], start=False, stop=True), [ready])
                            mm.append(t)
                        pr = probs.take()
                        view = lambda ap: ap[:, :].rearrange("p (i c) -> p i c", i=2)[:, :, 0:n]
                        t = ac.do(lambda e: e.activation(view(pr.ap), view(ps.ap), ACT.Exp), [mm, pr.after])
                        ps.done(t)

                        def weigh(j, a, n, i0, pr, t):
                            for i in range(i0, i0 + 2):
                                last = pe.do(lambda e: e.matmul(
                                    acc.ap[32 * i:32 * i + 32, a - a0:a - a0 + n], v_nat[:, j, g * GROUP + i, :],
                                    pr.ap[:, (i - i0) * BANK:(i - i0) * BANK + n], start=(j == 0),
                                    stop=(j == keys - 1), skip_group_check=True), [t, vals_ready[b], acc.after])
                            pr.done(last)
                            return last

                        if later:
                            weigh(*later)
                        later = (j, a, n, i0, pr, t)
                        yield
                last = weigh(*later)
                t = ac.do(lambda e: e.activation(o_T[:, g, a0:c0], acc.ap[:, 0:c0 - a0], ACT.Copy), [last, free["o_T"]])
                acc.done(t)
                weighed.setdefault(b, []).append(t)
            free["stack"][g] = [last]
            free["v_nat"] = [last]

        def attended(b, n):
            ps = psum.take()
            tt = [pe.do(lambda e: e.transpose(ps.ap[:, g * P:(g + 1) * P], o_T[:, g, n * P:(n + 1) * P], ident),
                        [weighed[b], ps.after]) for g in range(GROUPS)]
            view = ps.ap[:, 0:GROUPS * P].rearrange("p (h c) -> p h c", c=32)
            iv = inv_den.take()
            t = dv.do(lambda e: e.reciprocal(iv.ap[:, :], view[:, :, HD]), [tt, iv.after])
            at = att.take()
            t = dv.do(lambda e: e.tensor_tensor(
                at.ap[:, :].rearrange("p (h d) -> p h d", d=HD), view[:, :, 0:HD],
                iv.ap[:, :].unsqueeze(2).to_broadcast([P, HEADS, HD]), ALU.mult), [t, at.after])
            iv.done(t)
            ps.done(t)
            return at, t, tt

        def project_out(at, t, Wo, b, n, bias_row):
            ps = psum.take()
            t = pe.do(lambda e: e.transpose(ps.ap[:, 0:P], at.ap[:, :], ident), [t, ps.after])
            at.done(t)
            aT = attT.take()
            t = ac.do(lambda e: e.activation(aT.ap[:, :], ps.ap[:, 0:P], ACT.Copy), [t, aT.after])
            t = pe.do(lambda e: e.matmul(ps.ap[:, BANK:BANK + P], aT.ap[:, :], Wo, start=True, stop=True), [t, ready])
            aT.done(t)
            tile = x[:, b * NT + n, :]
            if bias_row is not None:
                x_ready[b * NT + n] = gp.do(lambda e: e.tensor_tensor(tile, tile, bias_row, ALU.add),
                                            [x_ready[b * NT + n], normed[b]])
            t = dv.do(lambda e: e.tensor_tensor(tile, tile, ps.ap[:, BANK:BANK + P], ALU.add),
                      [t, x_ready[b * NT + n], normed[b]])
            ps.done(t)
            x_ready[b * NT + n] = t

        def run_attention(prepare, open_row, finish, maxima, weigh):
            units = [(b, g) for b in range(batches) for g in range(GROUPS)]
            weave([prepare(0)])
            for g in range(GROUPS):
                load_stacks(0, g)
            open_row(0)
            for u in units[0:2]:
                weave([maxima(*u)])
            for i, (b, g) in enumerate(units):
                beside = [maxima(*units[i + 2])] if i + 2 < len(units) else []
                if g == 0:
                    preparing = [prepare(b + 1)] if b + 1 < batches else []
                if g <= 1:
                    weave([weigh(b, g)] + beside, preparing)
                if g == 1:
                    weave(preparing)
                if g > 1:
                    weave([weigh(b, g)] + beside)
                if b + 1 < batches:
                    for k in (() if g == 0 else (0, 1) if g == 1 else (g,)):
                        load_stacks(b + 1, k)
                if g == GROUPS - 1:
                    finish(b)
                    if b + 1 < batches:
                        open_row(b + 1)

        sources = {}

        def window_prepare(b):
            src, src_ready = yield from layer_norm(b)
            sources[b] = (src, src_ready)
            yield from split_to_scratch(w("a_wq"), src, src_ready, "q", None, b)
            yield from split_to_scratch(w("a_wk"), src, src_ready, "k", None, b)
            free["full_q"] = free["full_k"] = list(free["rest"])

        def window_open(b):
            values(w("a_wv"), *sources[b], None, b)

        def window_finish(b):
            turned = []
            for n in range(NT):
                at, t, tt = attended(b, n)
                turned += tt
                project_out(at, t, w("a_wo"), b, n, None)
            free["o_T"] = turned

        def window_attention():
            run_attention(window_prepare, window_open, window_finish, maxima_window, weigh_window)

        spread_k = Ring([carve([P, T]) for i in range(2)])
        spread_q = Ring([carve([P, T]) for i in range(2)])
        hebb = Ring([carve([P, T]) for i in range(1)])
        retain = carve([P, HD])
        alpha_T = carve([P // 2 + 1, T])
        alpha = carve([P, NT, HEADS])
        y_stp = full["v"]

        def clear_recurrence():
            t = ac.do(lambda e: e.activation(retain[:, :], w("c_lambda"), ACT.Exp), ready)
            t = dv.do(lambda e: e.tensor_scalar(retain[:, :], retain[:, :], 1.0, None, ALU.add), [t])
            return [dv.do(lambda e: e.reciprocal(retain[:, :], retain[:, :]), [t]),
                    gp.do(lambda e: e.memset(alpha_T[P // 2:P // 2 + 1, :], 1.0))]

        def recurrence(full_ready):
            acc = psum.take()
            sent = [dma(whole[s], full[s][:, :], [full_ready, free["whole"]]) for s in "qk"]
            free["whole"] = []
            for j in range(HD):
                sk, sq = spread_k.take(), spread_q.take()
                loads = []
                for s, side in ((sk, "k"), (sq, "q")):
                    row = whole[side].rearrange("(h j) t -> h j t", j=HD)[:, j, :]
                    loads.append(dma(s.ap[:, :], row.unsqueeze(1).to_broadcast([HEADS, HD, T]), [sent, s.after]))
                free["whole"] += loads
                t = dv.do(lambda e: e.scalar_tensor_tensor(
                    sk.ap[:, :], sk.ap[:, :], w("c_gamma", j, j + 1), full["v"][:, :], ALU.mult, ALU.mult),
                    [loads[0], full_ready, ready])
                hb = hebb.take()
                t = dv.do(lambda e: e.tensor_tensor_scan(
                    hb.ap[:, :], retain[:, j:j + 1].to_broadcast([P, T]), sk.ap[:, :], 0.0, ALU.mult, ALU.add),
                    [t, ready, hb.after])
                sk.done(t)
                t = dv.do(lambda e: e.scalar_tensor_tensor(
                    sq.ap[:, :], hb.ap[:, :], w("c_static", j, j + 1), sq.ap[:, :], ALU.add, ALU.mult), [t, loads[1]])
                hb.done(t)
                for n in range(NT):
                    m = pe.do(lambda e: e.matmul(
                        acc.ap[:, n * P:(n + 1) * P], sq.ap[:, n * P:(n + 1) * P], ident,
                        start=(j == 0 and n % 4 == 0), stop=(j == HD - 1), skip_group_check=True),
                        [t, acc.after])
                sq.done(m)
            free["full_q"] = free["full_k"] = [t] + sent
            t = ac.do(lambda e: e.activation(y_stp[:, :], acc.ap[:, 0:T], ACT.Copy), [m, t])
            acc.done(t)
            return t

        def causal_prepare(b):
            src, src_ready = yield from layer_norm(b)
            sources[b] = (src, src_ready)
            yield from split_to_scratch(w("c_wq"), src, src_ready, "q", w("c_bq"), b)
            yield from split_to_scratch(w("c_wk"), src, src_ready, "k", w("c_bk"), b)

        def causal_open(b):
            src, src_ready = sources[b]
            ps = psum.take()
            mm = [pe.do(lambda e: e.matmul(ps.ap[0:P // 2, a:c], w("c_gw1"), src.ap[:, a:c], start=True, stop=True),
                        [src_ready, ps.after, ready]) for a, c in blocks(T)]
            t = ac.do(lambda e: e.activation(alpha_T[0:P // 2, :], ps.ap[0:P // 2, 0:T], ACT.Gelu,
                                             bias=w("c_gb1")), [mm, free["alpha"]])
            ps.done(t)
            ps = psum.take()
            mm = [pe.do(lambda e: e.matmul(ps.ap[:, n * HEADS:(n + 1) * HEADS], alpha_T[:, n * P:(n + 1) * P],
                                           w("c_gw2"), start=True, stop=True), [t, ps.after, ready])
                  for n in range(NT)]
            exp_set(ac)
            av = alpha[:, :, :].rearrange("p n h -> p (n h)")
            t = ac.do(lambda e: e.activation(av, ps.ap[:, 0:NT * HEADS], ACT.Exp, scale=-1.0), [mm, free["alpha"]])
            ps.done(t)
            t = dv.do(lambda e: e.tensor_scalar(av, av, 1.0, None, ALU.add), [t])
            alpha_ready[0] = dv.do(lambda e: e.reciprocal(av, av), [t])
            ps = psum.take()
            mm = [pe.do(lambda e: e.matmul(ps.ap[:, a:c], w("c_wv"), src.ap[:, a:c], start=True, stop=True),
                        [src_ready, ps.after]) for a, c in blocks(T)]
            t = dv.do(lambda e: e.tensor_scalar(full["v"][:, :], ps.ap[:, 0:T], w("c_bv"), None, ALU.add),
                      [mm, free["full_v"]])
            ps.done(t)
            values(w("c_wv"), src, src_ready, w("c_bv_row"), b)
            y_ready[0] = recurrence([there["full_q", b], there["full_k", b], t])

        alpha_ready, y_ready = [None], [None]

        def causal_finish(b):
            turned, y_read = [], []
            for n in range(NT):
                at, t, tt = attended(b, n)
                turned += tt
                y = y_stp[:, n * P:(n + 1) * P]
                heads = at.ap[:, :].rearrange("p (h d) -> p h d", d=HD)
                t = dv.do(lambda e: e.tensor_tensor(at.ap[:, :], at.ap[:, :], y, ALU.subtract), [t, y_ready])
                t = dv.do(lambda e: e.tensor_tensor(
                    heads, heads, alpha[:, n, :].unsqueeze(2).to_broadcast([P, HEADS, HD]), ALU.mult), [t, alpha_ready])
                t = dv.do(lambda e: e.tensor_tensor(at.ap[:, :], at.ap[:, :], y, ALU.add), [t])
                project_out(at, t, w("c_wo"), b, n, w("c_bo_row"))
            free["full_v"], free["alpha"], free["o_T"] = [t], [t], turned

        def causal_mixed():
            run_attention(causal_prepare, causal_open, causal_finish, maxima_causal, weigh_causal)

        def first_largest(scores, eq, run, out, top, keep, after):
            n = scores.shape[2]
            f = lambda ap: ap.rearrange("p a b -> p (a b)")
            t = dv.do(lambda e: e.tensor_tensor(eq, scores, top.unsqueeze(2).to_broadcast([P, NT, n]),
                                                ALU.is_equal), after)
            t = dv.do(lambda e: e.tensor_tensor_scan(f(run), keep, f(eq), 0.0, ALU.mult, ALU.add), [t])
            return dv.do(lambda e: e.scalar_tensor_tensor(out, run, 1.0, eq, ALU.is_equal, ALU.mult), [t])

        def softmax_small(src, dst, small, n, after):
            bc = lambda ap: ap.unsqueeze(2).to_broadcast([P, NT, n])
            t = dv.do(lambda e: e.tensor_reduce(small[:, 0, :], src, AX.X, ALU.max), after)
            t = dv.do(lambda e: e.tensor_tensor(dst, src, bc(small[:, 0, :]), ALU.subtract), [t])
            done_src = t
            t = ac.do(lambda e: e.activation(dst, dst, ACT.Exp), [t])
            t = dv.do(lambda e: e.tensor_reduce(small[:, 1, :], dst, AX.X, ALU.add), [t])
            t = dv.do(lambda e: e.reciprocal(small[:, 1, :], small[:, 1, :]), [t])
            t = dv.do(lambda e: e.tensor_tensor(dst, dst, bc(small[:, 1, :]), ALU.mult), [t])
            return t, done_src

        def split_small(src, dst, n, tmp, tmp_bf, after):
            t = list(after)
            left = src
            for a in range(SPLIT):
                o = dst[:, :, a * n:(a + 1) * n]
                t = [dv.do(lambda e, left=left: e.tensor_copy(tmp_bf, left), t)]
                t = [dv.do(lambda e, o=o: e.tensor_copy(o, tmp_bf), t)]
                if a < SPLIT - 1:
                    t = [dv.do(lambda e, o=o, left=left: e.tensor_tensor(tmp, left, o, ALU.subtract), t)]
                    left = tmp
            return t

        def turn_rows(src, outs, after, free):
            ps = psum.take()
            tt = [pe.do(lambda e, n=n: e.transpose(ps.ap[:, n * P:(n + 1) * P], src[:, n, :], ident),
                        [after, ps.after, ready]) for n in range(NT)]
            got = [ac.do(lambda e, o=o, s=s: e.activation(o[:, :], ps.ap[:, 0:T], ACT.Copy, scale=s), [tt, free])
                   for o, s in outs]
            ps.done(*got)
            return got, tt

        DENSE = 1 + ROUTES
        used[0] = 0
        combined = {n: carve([P, GLA_HEADS * GLA_D]) for n in ("q2", "k2", "g1", "g2", "g")}
        route_p = carve([P, NT, ROUTES])
        route_s = carve([P, 2, NT])
        route_eq = carve([P, NT, ROUTES])
        route_run = carve([P, NT, ROUTES])
        route_hot = carve([P, NT, ROUTES])
        route_bf = carve([P, NT, ROUTES], BF16)
        route_top = carve([P, NT])
        rows_w = carve([P, NT, P])
        rows_h = rows_w
        w_T = carve([P, T], BF16)
        hot_T = carve([P, T], BF16)
        hot1_T = carve([P, T], BF16)
        gate_T = carve([P, PAIRS, T])
        gla = {n: Ring([carve([P, BANK]) for i in range(k)]) for n, k in
               (("gk", 2), ("e", 2), ("up", 2), ("dn", 2), ("q1", 2), ("q2", 2), ("k1", 2), ("k2", 2),
                ("k2n", 1), ("k1nat", 1), ("k2nat", 1), ("o", 1), ("rs", 1))}
        q_pad = [carve([P, PAIRS, 2, P]) for i in range(2)]
        q2m = Ring([carve([P, ROUTES, PAIRS * P]) for i in range(2)])
        hot_b = Ring([carve([P, ROUTES * P])])
        v5 = Ring([carve([P, DENSE, BANK]) for i in range(2)])
        masked1 = Ring([carve([P, GLA_HEADS * P])])
        masked2 = Ring([carve([P, GLA_HEADS * P])])
        mix = Ring([carve([P, P + 2 * ROUTES]) for i in range(2)])
        mix_tril = Ring([carve([P, P]) for i in range(2)])
        kmax = Ring([carve([P, 2, GLA_HEADS]) for i in range(2)])
        decay = Ring([carve([P, PAIRS, 2, DENSE]) for i in range(3)])
        factor = carve([P, PAIRS, DENSE])
        state = carve([P, PAIRS, DENSE, GLA_D])
        state_mid = carve([P, PAIRS, DENSE, GLA_D])
        state_dg = carve([P, PAIRS, DENSE, 2, GLA_D])
        low_rank = gate_T[:, :, :].rearrange("p a t -> p (a t)")[:, 0:sizes["l"]] if PAIRS * T >= sizes["l"] \
            else carve([P, sizes["l"]])
        keep4 = carve([P, NT, ROUTES])
        gla_free = {"route": [], "rows": [], "gate": [], "mid": [], "dg": [], "pad": [[], []]}

        def clear_gla():
            got = [gp.do(lambda e: e.memset(t, 0.0)) for t in (state_dg[:, :, :, :, :], q_pad[0], q_pad[1])]
            got += [
                gp.do(lambda e: e.memset(rows_w[:, :, :], 0.0))]
            t = gp.do(lambda e: e.memset(keep4[:, :, :], 1.0))
            got.append(gp.do(lambda e: e.memset(keep4[:, :, 0:1], 0.0), [t]))
            low = dma(low_rank, packed["l"])
            for n in combined:
                ps = psum.take()
                t = pe.do(lambda e, n=n, ps=ps: e.matmul(ps.ap[:, 0:BANK], w(f"b_{n}a"), w(f"b_{n}b"), start=True,
                                                         stop=True), [ready, low, ps.after])
                t = ac.do(lambda e, n=n, ps=ps: e.activation(combined[n][:, :], ps.ap[:, 0:BANK], ACT.Copy,
                                                             scale=GLA_D ** -0.5 if n == "q2" else 1.0), [t])
                ps.done(t)
                got.append(t)
            return got

        def gla_layer(b):
            src, src_ready = all_of(layer_norm(b))
            base = [src_ready, ready]
            for p in range(PAIRS):
                ps = psum.take()
                mm = [pe.do(lambda e, p=p, a=a, c=c, ps=ps: e.matmul(
                    ps.ap[:, a:c], combined["g"][:, p * P:(p + 1) * P], src.ap[:, a:c], start=True, stop=True),
                    [base, ps.after]) for a, c in blocks(T)]
                gated = ac.do(lambda e, p=p, ps=ps: e.activation(gate_T[:, p, :], ps.ap[:, 0:T], ACT.Silu),
                              [mm, gla_free["gate"]])
                ps.done(gated)
            exp_set(ac)
            ps = psum.take()
            mm = [pe.do(lambda e, n=n: e.matmul(ps.ap[:, n * ROUTES:(n + 1) * ROUTES], src.ap[:, n * P:(n + 1) * P],
                                                w("b_we"), start=True, stop=True), [base, ps.after])
                  for n in range(NT)]
            t, used = softmax_small(ps.ap[:, 0:NT * ROUTES].rearrange("p (n e) -> p n e", e=ROUTES),
                                    route_p[:, :, :], route_s, ROUTES, [mm, gla_free["route"]])
            ps.done(used)
            t_top = dv.do(lambda e: e.tensor_reduce(route_top[:, :], route_p[:, :, :], AX.X, ALU.max), [t])
            hot = first_largest(route_p[:, :, :], route_eq[:, :, :], route_run[:, :, :], route_hot[:, :, :],
                                route_top[:, :], keep4[:, :, :].rearrange("p a b -> p (a b)"),
                                [t_top, ready, gla_free["rows"]])
            t = [dv.do(lambda e, a=a: e.tensor_copy(rows_h[:, :, a * ROUTES:(a + 1) * ROUTES], route_hot[:, :, :]),
                       [hot, gla_free["rows"]]) for a in range(SPLIT)]
            g1, tt = turn_rows(rows_h, [(hot_T, 1.0), (hot1_T, w("route_first"))], t, gla_free["rows"])
            t = dv.do(lambda e: e.tensor_tensor(route_eq[:, :, :], route_p[:, :, :], route_hot[:, :, :], ALU.mult), [hot])
            t = split_small(route_eq[:, :, :], rows_w, ROUTES, route_run[:, :, :], route_bf[:, :, :], [t, tt])
            g2, tt = turn_rows(rows_w, [(w_T, 1.0)], t, gla_free["rows"])
            routed = g1 + g2

            state_of[b] = {}
            weave([produce(b, 0, src, base, routed, hot, t_top)])
            for n in range(NT):
                beside = [produce(b, n + 1, src, base, routed, hot, t_top)] if n + 1 < NT else []
                if n:
                    beside.append(finish(b, n - 1, gated))
                weave([consume(b, n)] + beside)
            weave([finish(b, NT - 1, gated)])
            state_of[b]["decay"].done((dv, dv.count))
            src.done((pe, pe.count))
            gla_free["gate"] = [(dv, dv.count)]
            gla_free["route"] = gla_free["rows"] = [(pe, pe.count), (dv, dv.count), (ac, ac.count)]

        made, state_of, summed = {}, {}, {}
        head_cols = lambda ap: ap.rearrange("p (h d) -> p h d", d=GLA_D)
        pair_cols = lambda ap: ap.rearrange("p (a c) -> p a c", a=PAIRS)
        over_head = lambda ap: ap.unsqueeze(2).to_broadcast([P, GLA_HEADS, GLA_D])

        def produce(b, n, src, base, routed, hot, t_top):
            tok = slice(n * P, (n + 1) * P)
            xt = src.ap[:, tok]
            gk, gk_ready = [], []
            ps = psum.take()
            mm = [pe.do(lambda e: e.matmul(ps.ap[:, i * BANK:(i + 1) * BANK], xt, combined[f"g{i + 1}"][:, :],
                                           start=True, stop=True), [base, ps.after]) for i in range(2)]
            zs = []
            for i in range(2):
                z = gla["gk"].take()
                zs.append((z, dv.do(lambda e: e.tensor_tensor(z.ap[:, :], ps.ap[:, i * BANK:(i + 1) * BANK],
                                                              w(f"b_bg{i + 1}"), ALU.add), [mm, z.after])))
            ps.done(zs[0][1], zs[1][1])
            yield
            for z, tz in zs:
                el = gla["e"].take()
                t = dv.do(lambda e: e.scalar_tensor_tensor(el.ap[:, :], z.ap[:, :], -1.0, z.ap[:, :], ALU.mult,
                                                           ALU.min), [tz, el.after])
                t = ac.do(lambda e: e.activation(el.ap[:, :], el.ap[:, :], ACT.Exp), [t])
                t = ac.do(lambda e: e.activation(el.ap[:, :], el.ap[:, :], ACT.Ln, bias=w("ones")), [t])
                t = dv.do(lambda e: e.scalar_tensor_tensor(z.ap[:, :], z.ap[:, :], 0.0, el.ap[:, :], ALU.min,
                                                           ALU.subtract), [t])
                el.done(t)
                gk.append(z)
                gk_ready.append(t)
            ps = psum.take()
            m1 = pe.do(lambda e: e.matmul(ps.ap[:, 0:P], hot_T[:, tok], hot1_T[:, tok], start=True, stop=True),
                       [routed, ps.after])
            m2 = pe.do(lambda e: e.matmul(ps.ap[:, P:2 * P], hot_T[:, tok], w_T[:, tok], start=True, stop=True),
                       [routed])
            m3 = [pe.do(lambda e: e.matmul(ps.ap[:, BANK + r * P:BANK + (r + 1) * P],
                                           w3["route_bcast"][:, r * P:(r + 1) * P], w_T[:, tok],
                                           start=True, stop=True), [routed]) for r in range(ROUTES)]
            mx, mt, hb = mix.take(), mix_tril.take(), hot_b.take()
            u1 = dv.do(lambda e: e.tensor_tensor(mx.ap[:, 0:P], ps.ap[:, 0:P], w("gate_sum", 0, P), ALU.mult),
                       [m1, m2, mx.after])
            u2 = dv.do(lambda e: e.tensor_tensor(
                mx.ap[:, P:P + 2 * ROUTES].rearrange("p (k r) -> p k r", k=2),
                route_hot[:, n, :].unsqueeze(1).to_broadcast([P, 2, ROUTES]),
                w("half").unsqueeze(2).to_broadcast([P, 2, ROUTES]), ALU.mult), [hot, mx.after])
            u3 = dv.do(lambda e: e.tensor_tensor(mt.ap[:, :], ps.ap[:, P:2 * P], w("tril"), ALU.mult), [m2, mt.after])
            u4 = ac.do(lambda e: e.activation(hb.ap[:, :], ps.ap[:, BANK:2 * BANK], ACT.Copy), [m3, hb.after])
            ps.done(u1, u3, u4)
            yield
            ps = psum.take()
            t = pe.do(lambda e: e.matmul(ps.ap[:, 0:BANK], xt, w("b_wv"), start=True, stop=True), [base, ps.after])
            vv = v5.take()
            tv = [ac.do(lambda e: e.activation(vv.ap[:, 0, :], ps.ap[:, 0:BANK], ACT.Copy), [t, vv.after])]
            for r in range(ROUTES):
                if r % 4 == 3:
                    tv.append(ac.do(lambda e: e.activation(vv.ap[:, 1 + r, :], ps.ap[:, 0:BANK], ACT.Copy,
                                                           scale=route_hot[:, n, r:r + 1]), [t, vv.after, hot]))
                else:
                    tv.append(dv.do(lambda e: e.tensor_scalar(vv.ap[:, 1 + r, :], vv.ap[:, 0, :],
                                                              route_hot[:, n, r:r + 1], None, ALU.mult),
                                    [tv[0], vv.after, hot]))
            ps.done(*tv)
            yield
            ps = psum.take()
            mq = [pe.do(lambda e: e.matmul(ps.ap[:, p * P:(p + 1) * P], combined["q2"][:, p * P:(p + 1) * P], xt,
                                           start=True, stop=True), [base, ps.after]) for p in range(PAIRS)]
            mk = pe.do(lambda e: e.matmul(ps.ap[:, BANK:2 * BANK], xt, combined["k2"][:, :], start=True, stop=True),
                       [base])
            km, kn = kmax.take(), gla["k2n"].take()
            t = dv.do(lambda e: e.tensor_reduce(km.ap[:, 0, :], head_cols(ps.ap[:, BANK:2 * BANK]), AX.X, ALU.max),
                      [mk, km.after])
            t = dv.do(lambda e: e.tensor_tensor(head_cols(kn.ap[:, :]), head_cols(ps.ap[:, BANK:2 * BANK]),
                                                over_head(km.ap[:, 0, :]), ALU.subtract), [t, kn.after])
            sub = t
            t = ac.do(lambda e: e.activation(kn.ap[:, :], kn.ap[:, :], ACT.Exp), [t])
            t = dv.do(lambda e: e.tensor_reduce(km.ap[:, 0, :], head_cols(kn.ap[:, :]), AX.X, ALU.add), [t])
            t = dv.do(lambda e: e.reciprocal(km.ap[:, 1, :], km.ap[:, 0, :]), [t])
            t = dv.do(lambda e: e.tensor_scalar(km.ap[:, 0, :], km.ap[:, 1, :], route_top[:, n:n + 1], None,
                                                ALU.mult), [t, t_top])
            k_soft = dv.do(lambda e: e.tensor_tensor(head_cols(kn.ap[:, :]), head_cols(kn.ap[:, :]),
                                                     over_head(km.ap[:, 0, :]), ALU.mult), [t])
            km.done(k_soft)
            q2_proj = ps
            up, dn, dc = [], [], decay.take()
            sums_ready, dcs = [[], []], []
            for i in range(2):
                cols = P + (2 if i == 0 else 2 * ROUTES)
                rhs = w("gate_sum") if i == 0 else mx.ap[:, 0:cols]
                ps = psum.take()
                mm = [pe.do(lambda e: e.matmul(ps.ap[:, p * 256:p * 256 + cols], gk[i].ap[:, p * P:(p + 1) * P], rhs,
                                               start=True, stop=True), [gk_ready[i], u1, u2, ps.after])
                      for p in range(PAIRS)]
                gk[i].done(mm[-1])
                v4 = pair_cols(ps.ap[:, :])
                for lst, name, sc in ((up, "up", 1.0), (dn, "dn", -1.0)):
                    s = gla[name].take()
                    t1 = ac.do(lambda e: e.activation(pair_cols(s.ap[:, :]), v4[:, :, 0:P], ACT.Exp, scale=sc),
                               [mm, s.after])
                    lst.append(s)
                    sums_ready[i].append(t1)
                d = 1 if i == 0 else ROUTES
                first = 0 if i == 0 else 1
                t1 = ac.do(lambda e: e.activation(
                    dc.ap[:, :, :, first:first + d],
                    v4[:, :, P:P + 2 * d].rearrange("p a (k d) -> p a k d", k=2), ACT.Exp), [mm, dc.after])
                dcs.append(t1)
                ps.done(t1)
            mx.done(mm[-1])
            q1, k1, q2, k2 = (gla[s].take() for s in ("q1", "k1", "q2", "k2"))
            tq2 = dv.do(lambda e: e.tensor_tensor(q2.ap[:, :], q2_proj.ap[:, 0:BANK], up[1].ap[:, :], ALU.mult),
                        [mq, sums_ready[1], q2.after])
            up[1].done(tq2)
            q2_proj.done(tq2, sub)
            yield
            ps = psum.take()
            mq = [pe.do(lambda e: e.matmul(ps.ap[:, p * P:(p + 1) * P], w("b_wq", p * P, (p + 1) * P), xt,
                                           start=True, stop=True), [base, ps.after]) for p in range(PAIRS)]
            mk = [pe.do(lambda e: e.matmul(ps.ap[:, BANK + p * P:BANK + (p + 1) * P], w("b_wk", p * P, (p + 1) * P),
                                           xt, start=True, stop=True), [base]) for p in range(PAIRS)]
            tq1 = dv.do(lambda e: e.scalar_tensor_tensor(q1.ap[:, :], ps.ap[:, 0:BANK], GLA_D ** -0.5,
                                                         up[0].ap[:, :], ALU.mult, ALU.mult),
                        [mq, sums_ready[0], q1.after])
            tk1 = dv.do(lambda e: e.tensor_tensor(k1.ap[:, :], ps.ap[:, BANK:2 * BANK], dn[0].ap[:, :], ALU.mult),
                        [mk, sums_ready[0], k1.after])
            ps.done(tq1, tk1)
            up[0].done(tq1)
            dn[0].done(tk1)
            qm = q2m.take()
            tm = [gp.do(lambda e: e.tensor_tensor(
                pair_cols(qm.ap[:, r, :]), pair_cols(q2.ap[:, :]),
                hb.ap[:, r * P:(r + 1) * P].unsqueeze(1).to_broadcast([P, PAIRS, P]), ALU.mult),
                [tq2, u4, qm.after]) for r in range(ROUTES)]
            hb.done(tm[-1])
            yield
            ps = psum.take()
            tt = [pe.do(lambda e: e.transpose(ps.ap[:, p * P:(p + 1) * P], kn.ap[:, p * P:(p + 1) * P], ident),
                        [k_soft, ps.after]) for p in range(PAIRS)]
            kn.done(tt[-1])
            tk2 = dv.do(lambda e: e.tensor_tensor(k2.ap[:, :], ps.ap[:, 0:BANK], dn[1].ap[:, :], ALU.mult),
                        [tt, k2.after])
            dn[1].done(tk2)
            ps.done(tk2)
            made[b, n] = dict(q=(q1, q2), k=(k1, k2), tq=(tq1, tq2), tk=(tk1, tk2), qm=qm, tm=tm, vv=vv, tv=tv,
                              mt=mt, u3=u3, dc=dc, dcs=dcs)
            yield

        def consume(b, n):
            m = made.pop((b, n))
            st = state_of[b]
            vv, tv, qm, mt = m["vv"], m["tv"], m["qm"], m["mt"]
            pads = []
            for i in range(2):
                for r in range(2):
                    rows = slice(r * GLA_D, (r + 1) * GLA_D)
                    t = ac.do(lambda e: e.activation(q_pad[i][rows, :, r, :], pair_cols(m["q"][i].ap[rows, :]), ACT.Copy),
                              [m["tq"][i], gla_free["pad"][i], ready])
                    pads.append(t)
            if n:
                prev = st["decay"]
                tf = dv.do(lambda e: e.tensor_tensor(factor[:, :, :], prev.ap[:, :, 0, :], m["dc"].ap[:, :, 1, :],
                                                     ALU.mult), [m["dcs"], gla_free["mid"]])
                prev.done(tf)
                t_mid = gp.do(lambda e: e.tensor_tensor(
                    state_mid[:, :, :, :].rearrange("p a r d -> p (a r) d"),
                    state[:, :, :, :].rearrange("p a r d -> p (a r) d"),
                    factor[:, :, :].rearrange("p a r -> p (a r)").unsqueeze(2).to_broadcast([P, PAIRS * DENSE, GLA_D]),
                    ALU.mult), [tf, st["ready"], gla_free["mid"]])
                t_dg = [ac.do(lambda e: e.activation(
                    state_dg[r * GLA_D:(r + 1) * GLA_D, :, :, r, :], state_mid[r * GLA_D:(r + 1) * GLA_D, :, :, :],
                    ACT.Copy), [t_mid, gla_free["dg"], ready]) for r in range(2)]
            st["decay"] = m["dc"]
            yield
            masked = []
            for i, ring, mask in ((0, masked1, w("tril")), (1, masked2, mt.ap[:, :])):
                ps = psum.take()
                k_ = m["k"][i]
                mm = [pe.do(lambda e: e.matmul(ps.ap[:, p * 256:(p + 1) * 256], k_.ap[:, p * P:(p + 1) * P],
                                               q_pad[i][:, p, :, :].rearrange("p r c -> p (r c)"), start=True,
                                               stop=True), [pads, m["tk"][i], ps.after]) for p in range(PAIRS)]
                gla_free["pad"][i] = [mm[-1]]
                mk_ = ring.take()
                t = dv.do(lambda e: e.tensor_tensor(
                    mk_.ap[:, :].rearrange("p (h c) -> p h c", c=P), ps.ap[:, :].rearrange("p (h c) -> p h c", c=P),
                    mask.unsqueeze(1).to_broadcast([P, GLA_HEADS, P]), ALU.mult), [mm, mk_.after, m["u3"]])
                ps.done(t)
                masked.append((mk_, t, mm[-1]))
                yield
            mt.done(masked[1][1])
            nats = []
            for i, name in ((0, "k1nat"), (1, "k2nat")):
                ps = psum.take()
                k_ = m["k"][i]
                tt = [pe.do(lambda e: e.transpose(ps.ap[:, p * P:(p + 1) * P], k_.ap[:, p * P:(p + 1) * P], ident),
                            [m["tk"][i], ps.after]) for p in range(PAIRS)]
                k_.done(tt[-1], masked[i][2])
                kn = gla[name].take()
                t = ac.do(lambda e: e.activation(kn.ap[:, :], ps.ap[:, 0:BANK], ACT.Copy), [tt, kn.after])
                ps.done(t)
                nats.append((kn, t))
            yield
            acc = psum.take()
            for mk_, t, _ in masked:
                first = mk_ is masked[0][0]
                for h in range(GLA_HEADS):
                    r0 = (h % 2) * GLA_D
                    last = pe.do(lambda e: e.matmul(
                        acc.ap[r0:r0 + GLA_D, (h // 2) * P:(h // 2 + 1) * P], vv.ap[:, 0, h * GLA_D:(h + 1) * GLA_D],
                        mk_.ap[:, h * P:(h + 1) * P], start=first and h < 2, stop=not first and n == 0,
                        skip_group_check=True), [t, tv, acc.after])
                mk_.done(last)
                yield
            ups = []
            for p0 in range(0, PAIRS, 2):
                ps = psum.take()
                for p in (p0, p0 + 1):
                    o = (p - p0) * BANK
                    for r in range(2):
                        h = 2 * p + r
                        cols = slice(h * GLA_D, (h + 1) * GLA_D)
                        pe.do(lambda e: e.matmul(
                            ps.ap[r * GLA_D:(r + 1) * GLA_D, o:o + GLA_D], nats[0][0].ap[:, cols], vv.ap[:, 0, cols],
                            start=True, stop=True, skip_group_check=True), [nats[0][1], tv, ps.after])
                        kv = pe.do(lambda e: e.matmul(
                            ps.ap[r * GLA_D:(r + 1) * GLA_D, o + GLA_D:o + DENSE * GLA_D], nats[1][0].ap[:, cols],
                            vv.ap[:, 1:DENSE, cols], start=True, stop=True, skip_group_check=True),
                            [nats[1][1], tv])
                src_ps = ps.ap[:, :].rearrange("p (a c) -> p a c", a=2)[:, :, 0:DENSE * GLA_D]
                dst = state[:, p0:p0 + 2, :, :].rearrange("p a r d -> p a (r d)")
                if n:
                    mid = state_mid[:, p0:p0 + 2, :, :].rearrange("p a r d -> p a (r d)")
                    t = dv.do(lambda e: e.tensor_tensor(dst, src_ps, mid, ALU.add), [kv, t_mid])
                else:
                    t = dv.do(lambda e: e.tensor_copy(dst, src_ps), [kv, gla_free["mid"]])
                ps.done(t)
                ups.append(t)
                yield
            for kn, _ in nats:
                kn.done(kv)
            vv.done(kv, last)
            st["ready"] = ups
            gla_free["mid"] = ups + (t_dg if n else [])
            if n:
                for p in range(PAIRS):
                    for r in range(DENSE):
                        rhs = m["q"][0].ap[:, p * P:(p + 1) * P] if r == 0 else qm.ap[:, r - 1, p * P:(p + 1) * P]
                        last = pe.do(lambda e: e.matmul(
                            acc.ap[:, p * P:(p + 1) * P], state_dg[:, p, r, :, :].rearrange("p a b -> p (a b)"),
                            rhs, start=False, stop=(r == DENSE - 1), skip_group_check=True), [t_dg, m["tm"]])
                    yield
                gla_free["dg"] = [last]
            m["q"][0].done(last, pads)
            m["q"][1].done(m["tm"][-1], pads)
            qm.done(last)
            o = gla["o"].take()
            t = ac.do(lambda e: e.activation(o.ap[:, :], acc.ap[:, 0:BANK], ACT.Copy), [last, o.after])
            acc.done(t)
            summed[b, n] = (o, t)

        def finish(b, n, gated):
            o, t_o = summed.pop((b, n))
            rs = gla["rs"].take()
            t = ac.do(lambda e: e.activation(rs.ap[:, :], o.ap[:, :], ACT.Square), [t_o, rs.after])
            yield
            ps = psum.take()
            t = pe.do(lambda e: e.matmul(ps.ap[:, 0:BANK], w("head_mean"), rs.ap[:, :], start=True, stop=True),
                      [t, ps.after])
            t = ac.do(lambda e: e.activation(rs.ap[:, :], ps.ap[:, 0:BANK], ACT.Ln, bias=w("eps")), [t])
            ps.done(t)
            t = ac.do(lambda e: e.activation(rs.ap[:, :], rs.ap[:, :], ACT.Exp, scale=-0.5), [t])
            t = dv.do(lambda e: e.scalar_tensor_tensor(rs.ap[:, :], o.ap[:, :], w("b_norm"), rs.ap[:, :], ALU.mult,
                                                       ALU.mult), [t])
            o.done(t)
            yield
            t = dv.do(lambda e: e.tensor_tensor(pair_cols(rs.ap[:, :]), pair_cols(rs.ap[:, :]),
                                                gate_T[:, :, n * P:(n + 1) * P], ALU.mult), [t, gated])
            t_gate = t
            yield
            yield
            ps = psum.take()
            for p in range(PAIRS):
                t = pe.do(lambda e: e.matmul(ps.ap[:, 0:P], rs.ap[:, p * P:(p + 1) * P], w("b_wo", p * P, (p + 1) * P),
                                             start=(p == 0), stop=(p == PAIRS - 1)), [t_gate, ps.after])
            rs.done(t)
            tile = x[:, b * NT + n, :]
            t = dv.do(lambda e: e.tensor_tensor(tile, tile, ps.ap[:, 0:P], ALU.add),
                      [t, x_ready[b * NT + n], normed[b]])
            ps.done(t)
            x_ready[b * NT + n] = t

        NG = EXPERTS + 1
        used[0] = 0
        moe_p = carve([P, NT, EXPERTS])
        moe_s = carve([P, 2, NT])
        moe_eq = carve([P, NT, EXPERTS])
        moe_run = carve([P, NT, EXPERTS])
        moe_hot = carve([P, 2, NT, EXPERTS])
        moe_w = carve([P, NT, NG])
        moe_tmp = carve([P, NT, NG])
        moe_bf = carve([P, NT, NG], BF16)
        keep16 = carve([P, NT, EXPERTS])
        moe_T = carve([P, T], BF16)
        moe_rows = carve([P, NT, P])
        act = Ring([carve([P, BANK]) for i in range(2)])
        hid = Ring([carve([P, BANK]) for i in range(2)])
        moe_free = [[]]

        def clear_moe():
            t = gp.do(lambda e: e.memset(keep16[:, :, :], 1.0))
            return [gp.do(lambda e: e.memset(keep16[:, :, 0:1], 0.0), [t]),
                    gp.do(lambda e: e.memset(moe_rows[:, :, :], 0.0))]

        def moe_layer(b):
            src, src_ready = all_of(layer_norm(b))
            ps = psum.take()
            mfree = moe_free[0]
            mm = [pe.do(lambda e, n=n: e.matmul(ps.ap[:, n * 32:n * 32 + NG], src.ap[:, n * P:(n + 1) * P], w("d_wg"),
                                                start=True, stop=True), [src_ready, ready, ps.after])
                  for n in range(NT)]
            lg = ps.ap[:, 0:NT * 32].rearrange("p (n e) -> p n e", e=32)
            t, used = softmax_small(lg[:, :, 0:EXPERTS], moe_p[:, :, :], moe_s, EXPERTS, [mm, mfree])
            s0 = ac.do(lambda e: e.activation(moe_w[:, :, EXPERTS], lg[:, :, EXPERTS], ACT.Exp, scale=-1.0), [mm, mfree])
            ps.done(used, s0)
            s1 = dv.do(lambda e: e.tensor_scalar(moe_w[:, :, EXPERTS], moe_w[:, :, EXPERTS], 1.0, None, ALU.add), [s0])
            s1 = dv.do(lambda e: e.reciprocal(moe_w[:, :, EXPERTS], moe_w[:, :, EXPERTS]), [s1])
            keep = keep16[:, :, :].rearrange("p a b -> p (a b)")
            t = dv.do(lambda e: e.tensor_reduce(moe_s[:, 0, :], moe_p[:, :, :], AX.X, ALU.max), [t])
            t = first_largest(moe_p[:, :, :], moe_eq[:, :, :], moe_run[:, :, :], moe_hot[:, 0, :, :], moe_s[:, 0, :],
                              keep, [t, ready])
            t = dv.do(lambda e: e.scalar_tensor_tensor(moe_tmp[:, :, 0:EXPERTS], moe_hot[:, 0, :, :], -2.0,
                                                       moe_p[:, :, :], ALU.mult, ALU.add), [t])
            t = dv.do(lambda e: e.tensor_reduce(moe_s[:, 1, :], moe_tmp[:, :, 0:EXPERTS], AX.X, ALU.max), [t])
            t = first_largest(moe_tmp[:, :, 0:EXPERTS], moe_eq[:, :, :], moe_run[:, :, :], moe_hot[:, 1, :, :],
                              moe_s[:, 1, :], keep, [t])
            t = dv.do(lambda e: e.tensor_tensor(moe_hot[:, 0, :, :], moe_hot[:, 0, :, :], moe_hot[:, 1, :, :], ALU.add), [t])
            t = dv.do(lambda e: e.tensor_tensor(moe_hot[:, 0, :, :], moe_hot[:, 0, :, :], moe_p[:, :, :], ALU.mult), [t])
            t = dv.do(lambda e: e.tensor_tensor(moe_s[:, 0, :], moe_s[:, 0, :], moe_s[:, 1, :], ALU.add), [t])
            t = dv.do(lambda e: e.reciprocal(moe_s[:, 0, :], moe_s[:, 0, :]), [t])
            t = dv.do(lambda e: e.tensor_tensor(moe_w[:, :, 0:EXPERTS], moe_hot[:, 0, :, :],
                                                moe_s[:, 0, :].unsqueeze(2).to_broadcast([P, NT, EXPERTS]),
                                                ALU.mult), [t])
            t = split_small(moe_w[:, :, :], moe_rows, NG, moe_tmp[:, :, :], moe_bf[:, :, :], [t, s1, mfree])
            g, tt = turn_rows(moe_rows, [(moe_T, 1.0)], t, mfree)
            for a, c in blocks(T):
                acc = psum.take()
                for f in range(MOE_TILES):
                    ps = psum.take()
                    pw = psum.take()
                    mg = pe.do(lambda e, f=f, a=a, c=c, ps=ps: e.matmul(ps.ap[:, 0:c - a], w("d_gate", f * P, (f + 1) * P),
                                                                        src.ap[:, a:c], start=True, stop=True),
                               [src_ready, ps.after])
                    mu = pe.do(lambda e, f=f, a=a, c=c, ps=ps: e.matmul(
                        ps.ap[:, BANK:BANK + c - a], w("d_up", f * P, (f + 1) * P), src.ap[:, a:c], start=True, stop=True),
                        [src_ready])
                    s = min(f, EXPERTS // 2)
                    mw = pe.do(lambda e, s=s, a=a, c=c, pw=pw: e.matmul(
                        pw.ap[:, 0:c - a], w3["moe_bcast"][:, s * P:(s + 1) * P], moe_T[:, a:c], start=True, stop=True),
                        [g, pw.after])
                    ag, hd = act.take(), hid.take()
                    t = ac.do(lambda e, a=a, c=c, ps=ps, ag=ag: e.activation(ag.ap[:, 0:c - a], ps.ap[:, 0:c - a], ACT.Silu),
                              [mg, ag.after])
                    t = dv.do(lambda e, a=a, c=c, ps=ps, ag=ag: e.tensor_tensor(
                        ag.ap[:, 0:c - a], ag.ap[:, 0:c - a], ps.ap[:, BANK:BANK + c - a], ALU.mult), [t, mu])
                    ps.done(t)
                    t = dv.do(lambda e, a=a, c=c, pw=pw, ag=ag, hd=hd: e.tensor_tensor(
                        hd.ap[:, 0:c - a], ag.ap[:, 0:c - a], pw.ap[:, 0:c - a], ALU.mult), [t, mw, hd.after])
                    pw.done(t)
                    ag.done(t)
                    for n in range((c - a) // P):
                        m = pe.do(lambda e, f=f, n=n, hd=hd, acc=acc: e.matmul(
                            acc.ap[:, n * P:(n + 1) * P], hd.ap[:, n * P:(n + 1) * P], w("d_down", f * P, (f + 1) * P),
                            start=(f == 0 and n == 0), stop=(f == MOE_TILES - 1), skip_group_check=True),
                            [t, acc.after])
                    hd.done(m)
                n0, n1 = b * NT + a // P, b * NT + c // P
                t = dv.do(lambda e, a=a, c=c, n0=n0, n1=n1, acc=acc: e.tensor_tensor(
                    x[:, n0:n1, :], x[:, n0:n1, :], acc.ap[:, 0:c - a].rearrange("p (n d) -> p n d", d=P), ALU.add),
                    [m, x_ready[n0:n1], normed[b]])
                acc.done(t)
                stored.append(dma(out_dram[:, n0:n1, :], x[:, n0:n1, :], [t]))
            src.done((pe, pe.count))
            moe_free[0] = [(pe, pe.count), (dv, dv.count), (ac, ac.count)]

        stored = []
        def all_gla():
            for b in range(batches):
                gla_layer(b)

        def all_moe():
            for b in range(batches):
                moe_layer(b)

        layers = ((window_attention, (clear_attention,), load_b, "c"), (all_gla, (clear_gla,), (), "d"),
                  (causal_mixed, (clear_attention, clear_recurrence), (), None), (all_moe, (clear_moe,), (), None))
        next_loaded = []
        for layer, clears, _, next_weights in layers:
            ready += next_loaded
            for clear in clears:
                ready += clear()
            layer()
            end_of_layer()
            next_loaded = load(next_weights) if next_weights else []
        sp.wait(stored)


def pack(parts):
    place, width = {}, {}
    for name, a in parts.items():
        layer = "s" if name in BF_CONSTANTS else "l" if name[-1] in "ab" and name[0] == "b" else name[0] if name[1] == "_" else "k"
        place[name] = (layer, width.get(layer, 0), a.shape[0], a.shape[1])
        width[layer] = width.get(layer, 0) + a.shape[1]
    out = {layer: np.zeros((P, n), np.float32) for layer, n in width.items()}
    for name, a in parts.items():
        layer, first, rows, cols = place[name]
        out[layer][:rows, first:first + cols] = a
    return out, place


def weight_columns(i):
    rows = lambda a: a.reshape(-1, P, a.shape[1]).transpose(1, 0, 2).reshape(P, -1)
    every = lambda v: np.tile(v.reshape(1, -1), (P, 1))
    col = lambda v: v.reshape(-1, 1)
    qkv, bias = i["L1_attn_Wqkv_w"], i["L1_attn_Wqkv_b"]
    per_head = lambda a: a.reshape(P, HD)
    e_rows = lambda a: a.reshape(EXPERTS * EXPERT_HID, P)
    down = np.concatenate([i["L1_ffn_We_down"].transpose(0, 2, 1).reshape(-1, P), i["L1_ffn_Ws_down"].T], 0)
    return {
        "a_wq": i["L0_attn_Wq"].T, "a_wk": i["L0_attn_Wk"].T, "a_wv": i["L0_attn_Wv"].T, "a_wo": i["L0_attn_Wo"].T,
        "b_wq": i["L0_ffn_Wq"], "b_wk": i["L0_ffn_Wk"], "b_wv": i["L0_ffn_Wv"],
        "b_q2a": i["L0_ffn_Wqa"].T, "b_q2b": i["L0_ffn_Wqb"], "b_k2a": i["L0_ffn_Wka"].T, "b_k2b": i["L0_ffn_Wkb"],
        "b_g1a": i["L0_ffn_Wg1a"].T, "b_g1b": i["L0_ffn_Wg1b"], "b_g2a": i["L0_ffn_Wg2a"].T, "b_g2b": i["L0_ffn_Wg2b"],
        "b_ga": i["L0_ffn_Wga"].T, "b_gb": i["L0_ffn_Wgb"],
        "b_bg1": every(i["L0_ffn_bg1"]), "b_bg2": every(i["L0_ffn_bg2"]),
        "b_we": i["L0_ffn_We"], "b_norm": col(np.tile(i["L0_ffn_norm_w"], 2)), "b_wo": rows(i["L0_ffn_Wo"]),
        "c_wq": qkv[:, 0:P], "c_wk": qkv[:, P:2 * P], "c_wv": qkv[:, 2 * P:],
        "c_bq": col(bias[0:P]), "c_bk": col(bias[P:2 * P]), "c_bv": col(bias[2 * P:]), "c_bv_row": every(bias[2 * P:]),
        "c_lambda": per_head(i["L1_attn_Lambda_raw"]), "c_gamma": per_head(i["L1_attn_Gamma"]),
        "c_static": per_head(i["L1_attn_W_static"]),
        "c_gw1": i["L1_attn_gate_w1"], "c_gb1": col(i["L1_attn_gate_b1"]),
        "c_gw2": np.concatenate([i["L1_attn_gate_w2"], i["L1_attn_gate_b2"].reshape(1, -1)], 0),
        "c_wo": i["L1_attn_out_w"], "c_bo_row": every(i["L1_attn_out_b"]),
        "d_wg": np.concatenate([i["L1_ffn_Wg"], i["L1_ffn_Wsg"]], 0).T,
        "d_gate": np.concatenate([e_rows(i["L1_ffn_We_gate"]), i["L1_ffn_Ws_gate"]], 0).T,
        "d_up": np.concatenate([e_rows(i["L1_ffn_We_up"]), i["L1_ffn_Ws_up"]], 0).T,
        "d_down": rows(down),
    }


def kernel(**inputs):
    import concourse.bacc as _bacc
    from concourse.bass_utils import run_bass_kernel_spmd as _run

    i = {k: np.asarray(v) for k, v in inputs.items()}
    x = np.ascontiguousarray(i["L0_attn_x"])
    packed, place = pack({**constant_columns(), **weight_columns(i)})
    nc = _bacc.Bacc("TRN2", target_bir_lowering=False, num_devices=1)
    x_in = nc.dram_tensor("x_in", x.shape, F32, kind="ExternalInput").ap()
    w_in = {k: nc.dram_tensor(f"w_{k}", a.shape, F32, kind="ExternalInput").ap() for k, a in packed.items()}
    x_out = nc.dram_tensor("x_out", x.shape, F32, kind="ExternalOutput").ap()
    build(nc, x_in, w_in, x_out, place, x.shape[0], x.shape[1])
    r = _run(nc, [{"x_in": x, **{f"w_{k}": a for k, a in packed.items()}}], core_ids=[0])
    return r.results[0]["x_out"]
```

```python
from contextlib import ExitStack

import numpy as np

import concourse.bass as bass
from concourse import mybir

ALU = mybir.AluOpType
ACT = mybir.ActivationFunctionType
AX = mybir.AxisListType
F32 = mybir.dt.float32
BF16 = mybir.dt.bfloat16

P = 128
BANK = 512
EPS = 1e-5
HEADS, HD = 16, 8
GROUP = 4
WINDOW = 64
GLA_HEADS, GLA_D = 8, 64
PAIRS = GLA_HEADS // 2
GLA_CHUNK = 64
ROUTES = 4
EXPERTS, EXPERT_HID, SHARED_HID = 16, 64, 256
MOE_TILES = (EXPERTS * EXPERT_HID + SHARED_HID) // P
NORMALIZER = 16.0
SPLIT = 3
NEG_ROW = 96
TWO_ONES = 1.0 + 127 * 2.0 ** -16
ATT_SCALE = float(1.0 / np.sqrt(HD))


def flat(tokens):
    for t in tokens:
        if isinstance(t, list):
            yield from flat(t)
        elif t is not None:
            yield t


class Lane:

    def __init__(self, eng, sem, one_by_one=False):
        self.eng, self.sem, self.count, self.seen, self.held = eng, sem, 0, {}, []
        self.one_by_one = one_by_one

    def wait(self, after):
        need = {}
        held, self.held = self.held, []
        for lane, value in flat([list(after), held]):
            if value > self.seen.get(lane, 0):
                need[lane] = max(need.get(lane, 0), value)
        self.seen.update(need)
        for lane, value in need.items():
            self.eng.wait_ge(lane.sem, value)

    def do(self, op, after=()):
        if self.one_by_one:
            after = [list(after), [(self, self.count)]]
        self.wait(after)
        op(self.eng).then_inc(self.sem, 1)
        self.count += 1
        return (self, self.count)


class Channel:

    def __init__(self, sem):
        self.sem, self.count = sem, 0


class Slot:

    def __init__(self, ring, ap, after):
        self.ring, self.ap, self.after = ring, ap, after

    def done(self, *tokens):
        self.ring.free.append((self.ap, list(tokens)))


class Ring:
    def __init__(self, buffers):
        self.free = [(b, []) for b in buffers]

    def take(self):
        ap, after = self.free.pop(0)
        return Slot(self, ap, after)


def weave(streams, beside=()):
    left, extra = list(streams), list(beside)
    done = object()
    while left:
        for stream in left[:]:
            if next(stream, done) is done:
                left.remove(stream)
        for stream in extra[:]:
            if next(stream, done) is done:
                extra.remove(stream)


def two_by_two(stream):
    for _ in stream:
        next(stream, None)
        yield


def all_of(stream):
    while True:
        try:
            next(stream)
        except StopIteration as end:
            return end.value


def constant_columns():
    r = np.arange(P)[:, None]
    c = np.arange(P)[None, :]
    w = np.arange(P + WINDOW)[None, :]
    mid = (r < GLA_CHUNK) * np.ones((1, 1))
    out = {
        "ident": r == c,
        "eps": np.full((P, 1), EPS),
        "win_row": ~((w > r) & (w <= r + WINDOW)) * -(2.0 ** 60),
        "win_col": ~((w >= r) & (w < r + WINDOW)) * -(2.0 ** 60),
        "causal_row": (c > r) * -100.0,
        "causal_col": (r > c) * -100.0,
        "tril": (r <= c) * 1.0,
        "gate_sum": np.concatenate([(r <= c) * 1.0 - mid, 1 - mid, mid], 1) / NORMALIZER,
        "half": np.concatenate([1 - mid, mid], 1) / NORMALIZER,
        "head_mean": (r // GLA_D == c // GLA_D) / GLA_D,
        "route_first": (r < ROUTES) * 1.0,
        "ones": np.ones((P, 1)),
    }
    part_rows = SPLIT * ROUTES
    sel = [((r % ROUTES == e) & (r < part_rows)) * np.ones((1, P)) for e in range(ROUTES)]
    out["route_bcast"] = np.concatenate(sel, 1)
    n = EXPERTS + 1
    sel = [((r % n == np.minimum(2 * f + c // EXPERT_HID, EXPERTS)) & (r < SPLIT * n)) * 1.0
           for f in range(EXPERTS // 2 + 1)]
    sel[-1] = ((r % n == EXPERTS) & (r < SPLIT * n)) * np.ones((1, P))
    out["moe_bcast"] = np.concatenate(sel, 1)
    return {k: np.asarray(v, np.float32) for k, v in out.items()}


REGION_OF = {"k": "constants", "a": "small", "b": "large", "c": "small", "d": "large"}
ARENA = 40500

BF_CONSTANTS = ("win_row", "win_col", "causal_row", "causal_col", "route_bcast", "moe_bcast")


def build(nc, x_in, packed, x_out, place, batches, T):
    sizes = {k: a.shape[1] for k, a in packed.items()}
    region_of = REGION_OF
    NT = T // P
    ctx = ExitStack()
    with ctx:
        def sb(name, shape, dt=F32):
            return ctx.enter_context(nc.sbuf_tensor(name, shape, dt))

        def sem(name):
            return ctx.enter_context(nc.semaphore(name))

        pe, dv, ac = (Lane(eng, sem(f"count_{n}")) for n, eng in
                      (("tensor", nc.tensor), ("vector", nc.vector), ("scalar", nc.scalar)))
        gp = Lane(nc.gpsimd, sem("count_gpsimd"), one_by_one=True)
        sp = Lane(nc.sync, None)
        channels = [Channel(sem(f"dma_{i}")) for i in range(24)]
        turn = [0]

        def dma(out, in_, after=()):
            ch = channels[turn[0] % len(channels)]
            turn[0] += 1
            sp.wait([list(after), [(ch, ch.count)]])
            nc.sync.dma_start(out, in_).then_inc(ch.sem, 16)
            ch.count += 16
            return (ch, ch.count)

        def exp_set(lane):
            lane.eng.preload_act_table_set("natural_log_exp_and_others")

        def end_of_layer():
            every = [(lane, lane.count) for lane in (pe, dv, ac, gp)] + [(ch, ch.count) for ch in channels]
            for lane in (pe, dv, ac, gp, sp):
                lane.held = every

        regions = {r: sb(f"weights_{r}", [P, max(n for k, n in sizes.items() if region_of.get(k) == r)])
                   for r in sorted(set(region_of.values()))}

        def w(name, a=0, b=None):
            layer, first, rows, cols = place[name]
            t = low_rank if layer == "l" else regions[region_of[layer]]
            return t[0:rows, first + a:first + (cols if b is None else b)]

        arena = sb("arena", [P, ARENA])
        used = [0]

        def carve(shape, dt=F32):
            n = int(np.prod(shape[1:]))
            words = n if dt == F32 else (n + 1) // 2
            ap = arena[0:shape[0], used[0]:used[0] + words]
            used[0] += words
            assert used[0] <= ARENA, used[0]
            if dt != F32:
                ap = ap.bitcast(dt)
            if len(shape) > 2:
                names = "abcdef"[:len(shape) - 1]
                ap = ap.rearrange(f"p ({' '.join(names)}) -> p {' '.join(names)}", **dict(zip(names, shape[1:])))
            return ap

        x = sb("x", [P, batches * NT, P])
        x_ready = [None] * (batches * NT)
        psum = Ring([ctx.enter_context(nc.psum_tensor(f"psum{i}", [P, 2 * BANK], F32)) for i in range(4)])

        stats = sb("stats", [P, NT, 6])
        moments = sb("moments", [P, NT, 2])
        rstd = sb("rstd", [P, 4, NT])
        xn = Ring([sb(f"xn{i}", [P, P]) for i in range(4)])
        xnT = Ring([sb("xnT0", [P, T])])

        w3 = {n: sb(f"bf_{n}", [P, place[n][3]], BF16) for n in BF_CONSTANTS}
        ident = w("ident")
        ident_bf = {v: sb(f"ident_{i}", [P, P], BF16) for i, v in enumerate((100.0, 2.0 ** 60))}

        q_stack = carve([P, HEADS, T], BF16)
        k_stack = carve([P, HEADS, T], BF16)
        full = {s: carve([P, T]) for s in "qkv"}
        rest = carve([P, T])
        parts = Ring([carve([P, SPLIT, T], BF16) for i in range(1)])
        v_nat = carve([P, NT, HEADS, 32])
        neg_max = carve([P, NT, 2, HEADS])
        neg_parts = carve([P, NT, SPLIT, GROUP])
        neg_rest = carve([P, NT, GROUP])
        neg_bf = carve([P, NT, GROUP], BF16)
        neg_T = carve([SPLIT * GROUP, T], BF16)
        probs = Ring([carve([P, 2 * BANK]) for i in range(2)])
        o_T = carve([P, HEADS // GROUP, T])
        att = Ring([carve([P, P]) for i in range(2)])
        attT = Ring([carve([P, P]) for i in range(2)])
        inv_den = Ring([carve([P, HEADS]) for i in range(2)])

        def load(layer, after=()):
            n = sizes[layer]
            return [dma(regions[REGION_OF[layer]][:, a:min(n, a + 2048)], packed[layer][:, a:min(n, a + 2048)], after)
                    for a in range(0, n, 2048)]

        x_dram = x_in.rearrange("b (n p) d -> p (b n) d", p=P)
        out_dram = x_out.rearrange("b (n p) d -> p (b n) d", p=P)

        def load_x(b):
            for n in range(0, NT, 4):
                tiles = slice(b * NT + n, b * NT + min(n + 4, NT))
                x_ready[tiles] = [dma(x[:, tiles, :], x_dram[:, tiles, :])] * (tiles.stop - tiles.start)

        load_x(0)
        ready = load("k")
        ready += load("a")
        staged = o_T[:, :, :].rearrange("p g t -> p (g t)")[:, 0:sizes["s"]] if HEADS // GROUP * T >= sizes["s"] \
            else arena[:, ARENA - sizes["s"]:ARENA]
        loaded = dma(staged, packed["s"])
        for b in range(1, batches):
            load_x(b)
        load_b = load("b")

        bf_ready = []

        def convert_constants():
            for v, t in ident_bf.items():
                bf_ready.append(ac.do(lambda e: e.activation(t[:, :], ident, ACT.Copy, scale=v), [ready]))
            for n in BF_CONSTANTS:
                first = place[n][1]
                bf_ready.append(ac.do(lambda e: e.activation(w3[n][:, :], staged[:, first:first + place[n][3]],
                                                             ACT.Copy), [loaded]))
            free["o_T"] = list(bf_ready)

        last_norm = [[]]
        normed = {}

        def layer_norm(b):
            got = []
            norm_free = last_norm[0]
            exp_set(ac)
            for n in range(NT):
                t = dv.do(lambda e, n=n: e.bn_stats(stats[:, n, :], x[:, b * NT + n, :]),
                          [x_ready[b * NT + n], norm_free])
                got.append(dv.do(lambda e, n=n: e.bn_aggr(moments[:, n, :], stats[:, n, :]), [t, norm_free]))
            t = ac.do(lambda e: e.activation(rstd[:, 0, :], moments[:, :, 1], ACT.Ln, bias=w("eps")),
                      [got, norm_free, ready])
            t = ac.do(lambda e: e.activation(rstd[:, 1, :], rstd[:, 0, :], ACT.Exp, scale=-0.5), [t])
            t = dv.do(lambda e: e.tensor_tensor(rstd[:, 2, :], rstd[:, 1, :], rstd[:, 1, :], ALU.mult), [t])
            t = dv.do(lambda e: e.scalar_tensor_tensor(rstd[:, 0, :], moments[:, :, 1], EPS, rstd[:, 2, :],
                                                       ALU.add, ALU.mult), [t])
            t = dv.do(lambda e: e.tensor_scalar(rstd[:, 2, :], rstd[:, 0, :], -0.5, 1.5, ALU.mult, ALU.add), [t])
            t_r = dv.do(lambda e: e.tensor_tensor(rstd[:, 3, :], rstd[:, 1, :], rstd[:, 2, :], ALU.mult), [t])
            yield
            out = xnT.take()
            ends, norms = [], []
            for n0 in range(0, NT, 4):
                ps = psum.take()
                k = min(4, NT - n0)
                turned = []
                for n in range(n0, n0 + k):
                    s = xn.take()
                    t = dv.do(lambda e, n=n, s=s: e.tensor_scalar(
                        s.ap[:, :], x[:, b * NT + n, :], moments[:, n, 0:1], rstd[:, 3, n:n + 1],
                        ALU.subtract, ALU.mult), [t_r, s.after])
                    norms.append(t)
                    t = pe.do(lambda e, n=n, s=s, ps=ps, n0=n0: e.transpose(
                        ps.ap[:, (n - n0) * P:(n - n0 + 1) * P], s.ap[:, :], ident), [t, ps.after, ready])
                    s.done(t)
                    turned.append(t)
                t = ac.do(lambda e, ps=ps, n0=n0, k=k: e.activation(
                    out.ap[:, n0 * P:(n0 + k) * P], ps.ap[:, 0:k * P], ACT.Copy), [turned, out.after])
                ps.done(t)
                ends.append(t)
                yield
            last_norm[0] = normed[b] = norms
            return out, ends

        early = {}

        def early_norm():
            early[0] = yield from layer_norm(0)

        def norm_of(b):
            return early.pop(0) if b == 0 and early else (yield from layer_norm(b))

        def blocks(n):
            return [(a, min(a + BANK, n)) for a in range(0, n, BANK)]

        scratch = {s: nc.dram_tensor(f"scratch_{s}", (SPLIT, P, T), BF16, kind="Internal").ap() for s in "qk"}
        whole = {s: nc.dram_tensor(f"whole_{s}", (batches, P, T), F32, kind="Internal").ap() for s in "qk"}
        stacks = {"q": q_stack, "k": k_stack}
        GROUPS = HEADS // GROUP

        def clear_attention():
            words = lambda ap: ap.rearrange("p h t -> p (h t)").bitcast(F32)
            for g in range(GROUPS):
                heads = slice(g * GROUP, (g + 1) * GROUP)
                cleared[g] = [gp.do(lambda e: e.memset(words(q_stack[64:P, heads, :]), 0.0)),
                              gp.do(lambda e: e.memset(words(k_stack[64:NEG_ROW, heads, :]), 0.0)),
                              gp.do(lambda e: e.memset(words(k_stack[NEG_ROW:P, heads, :]), TWO_ONES))]
                if g == 0:
                    t = gp.do(lambda e: e.memset(v_nat[:, :, :, :], 0.0))
                    cleared["v"] = gp.do(lambda e: e.memset(v_nat[:, :, :, HD:HD + 1], 1.0), [t])

        cleared = {}

        free = {"full_q": [], "full_k": [], "full_v": [], "rest": [], "scratch_q": [], "scratch_k": [],
                "stack": {g: [] for g in range(GROUPS)}, "v_nat": [], "neg": [], "neg_T": [], "o_T": [],
                "alpha": [], "y": []}
        there = {}
        stacked = {}
        shifted = {}
        vals_ready = {}
        weighed = {}

        def split_to_scratch(W, src, src_ready, side, bias, b):
            ps = psum.take()
            mm = [pe.do(lambda e: e.matmul(ps.ap[:, a:c], W, src.ap[:, a:c], start=True, stop=True),
                        [src_ready, ps.after, ready]) for a, c in blocks(T)]
            scale = ATT_SCALE if side == "k" else 1.0
            dst = full[side]
            if bias is None:
                t = ac.do(lambda e: e.activation(dst[:, :], ps.ap[:, 0:T], ACT.Copy, scale=scale),
                          [mm, free["full_" + side]])
            else:
                t = dv.do(lambda e: e.tensor_scalar(dst[:, :], ps.ap[:, 0:T], bias, scale, ALU.add, ALU.mult),
                          [mm, free["full_" + side]])
            ps.done(t)
            full_ready = t
            yield
            pt = parts.take()
            hi = ac.do(lambda e: e.activation(pt.ap[:, 0, :], dst[:, :], ACT.Copy), [t, pt.after])
            t = dv.do(lambda e: e.tensor_tensor(rest[:, :], dst[:, :], pt.ap[:, 0, :], ALU.subtract), [hi, free["rest"]])
            yield
            mid = ac.do(lambda e: e.activation(pt.ap[:, 1, :], rest[:, :], ACT.Copy), [t, pt.after])
            lo = dv.do(lambda e: e.tensor_tensor(pt.ap[:, 2, :], rest[:, :], pt.ap[:, 1, :], ALU.subtract),
                       [mid, pt.after])
            free["rest"] = [lo]
            free["full_" + side] = [t]
            there[side, b] = dma(scratch[side].rearrange("a (h d) t -> (h d) a t", d=HD), pt.ap[:, :, :],
                                 [hi, mid, lo, free["scratch_" + side]])
            free["scratch_" + side] = []
            pt.done(there[side, b])
            if bias is not None:
                there["whole_" + side, b] = dma(whole[side][b], dst[:, :], [full_ready])
                free["full_" + side].append(there["whole_" + side, b])
            yield

        def load_stacks(b, g):
            heads = slice(g * GROUP, (g + 1) * GROUP)
            got = []
            for side in "qk":
                for row in range(SPLIT * SPLIT):
                    part = row // SPLIT if side == "q" else row % SPLIT
                    rows = scratch[side][part, g * GROUP * HD:(g + 1) * GROUP * HD, :].rearrange("(h d) t -> d h t", d=HD)
                    t = dma(stacks[side][row * HD:(row + 1) * HD, heads, :], rows,
                            [there[side, b], free["stack"][g], cleared[g]])
                    got.append(t)
                    free["scratch_" + side].append(t)
            stacked[b, g] = got

        def values(W, src, src_ready, bias_row, b):
            got = []
            for n0 in range(0, NT, 4):
                ps = psum.take()
                k = min(4, NT - n0)
                mm = [pe.do(lambda e: e.matmul(ps.ap[:, (n - n0) * P:(n - n0 + 1) * P], src.ap[:, n * P:(n + 1) * P],
                                               W, start=True, stop=True), [src_ready, ps.after, ready])
                      for n in range(n0, n0 + k)]
                cols = []
                for n in range(n0, n0 + k):
                    o = v_nat[:, n, :, 0:HD]
                    i = ps.ap[:, (n - n0) * P:(n - n0 + 1) * P].rearrange("p (h d) -> p h d", d=HD)
                    if bias_row is None:
                        t = ac.do(lambda e: e.activation(o, i, ACT.Copy), [mm, free["v_nat"], cleared["v"]])
                    else:
                        t = dv.do(lambda e: e.tensor_tensor(o, i, bias_row.rearrange("p (h d) -> p h d", d=HD),
                                                            ALU.add), [mm, free["v_nat"], cleared["v"]])
                    cols.append(t)
                ps.done(*cols)
                got += cols
            vals_ready[b] = got
            src.done(*[(pe, pe.count)])

        def spread_maxima(b, g, maxima):
            view = neg_max[:, :, 0, g * GROUP:(g + 1) * GROUP]
            t = [dv.do(lambda e: e.tensor_copy(neg_bf[:, :, :], view), [maxima, free["neg"]])]
            t = dv.do(lambda e: e.tensor_copy(neg_parts[:, :, 0, :], neg_bf[:, :, :]), [t, free["neg"]])
            t = dv.do(lambda e: e.tensor_tensor(neg_rest[:, :, :], view, neg_parts[:, :, 0, :], ALU.subtract), [t])
            t = dv.do(lambda e: e.tensor_copy(neg_bf[:, :, :], neg_rest[:, :, :]), [t])
            t = dv.do(lambda e: e.tensor_copy(neg_parts[:, :, 1, :], neg_bf[:, :, :]), [t])
            t = dv.do(lambda e: e.tensor_tensor(neg_parts[:, :, 2, :], neg_rest[:, :, :], neg_parts[:, :, 1, :],
                                                ALU.subtract), [t])
            yield
            yield
            rows = SPLIT * GROUP
            ps = psum.take()
            tt = [pe.do(lambda e: e.transpose(ps.ap[0:rows, n * P:(n + 1) * P],
                                              neg_parts[:, n, :, :].rearrange("p a h -> p (a h)"), ident),
                        [t, ps.after]) for n in range(NT)]
            free["neg"] = [tt[-1], t]
            yield
            t = ac.do(lambda e: e.activation(neg_T[:, :], ps.ap[0:rows, 0:T], ACT.Copy), [tt, free["neg_T"]])
            ps.done(t)
            sent = [dma(q_stack[NEG_ROW + a:NEG_ROW + a + 1, g * GROUP:(g + 1) * GROUP, :],
                        neg_T[a * GROUP:(a + 1) * GROUP, :], [t, free["stack"][g]]) for a in range(SPLIT)]
            free["neg_T"] = sent
            shifted[b, g] = sent

        def maxima_window(b, g):
            got = []
            for n in range(NT):
                lo = max(0, n * P - WINDOW)
                cut = lo - (n * P - WINDOW)
                cols = P + WINDOW - cut
                ps = psum.take()
                mm = []
                for i in range(GROUP):
                    o = ps.ap[:, i * 256:i * 256 + cols]
                    h = g * GROUP + i
                    pe.do(lambda e: e.matmul(o, q_stack[0:NEG_ROW, h, n * P:(n + 1) * P],
                                             k_stack[0:NEG_ROW, h, lo:(n + 1) * P], start=True, stop=False),
                          [stacked[b, g], ps.after])
                    mm.append(pe.do(lambda e: e.matmul(o, ident_bf[2.0 ** 60][:, :],
                                                       w3["win_row"][:, cut:P + WINDOW], start=False, stop=True),
                                    [bf_ready]))
                t = dv.do(lambda e: e.tensor_reduce(
                    neg_max[:, n, 0, g * GROUP:(g + 1) * GROUP],
                    ps.ap[:, :].rearrange("p (i c) -> p i c", i=GROUP)[:, :, 0:cols], AX.X, ALU.max, negate=True), [mm])
                ps.done(t)
                got.append(t)
                yield
            yield from spread_maxima(b, g, got)

        def maxima_causal(b, g):
            got = []
            for n in range(NT):
                pieces = []
                for half, (a, c) in enumerate(blocks((n + 1) * P)):
                    width = c - a
                    per = 2 if 2 * width <= BANK else 1
                    for h0 in range(g * GROUP, (g + 1) * GROUP, 2 * per):
                        ps = psum.take()
                        mm = []
                        for i in range(2 * per):
                            o = ps.ap[:, (i // per) * BANK + (i % per) * width:][:, 0:width]
                            h = h0 + i
                            diag = c == (n + 1) * P
                            t = pe.do(lambda e: e.matmul(o, q_stack[0:NEG_ROW, h, n * P:(n + 1) * P],
                                                         k_stack[0:NEG_ROW, h, a:c], start=True, stop=not diag),
                                      [stacked[b, g], ps.after])
                            if diag:
                                t = pe.do(lambda e: e.matmul(o[:, width - P:width], ident_bf[100.0][:, :],
                                                             w3["causal_row"][:, :], start=False, stop=True), [bf_ready])
                            mm.append(t)
                        src = ps.ap[:, :].rearrange("p (k c) -> p k c", k=2)[:, :, 0:per * width]
                        if per > 1:
                            src = src.rearrange("p k (i c) -> p k i c", i=per)
                            dst = neg_max[:, n, half, h0:h0 + 2 * per].rearrange("p (k i) -> p k i", k=2)
                        else:
                            dst = neg_max[:, n, half, h0:h0 + 2]
                        t = dv.do(lambda e: e.tensor_reduce(dst, src, AX.X, ALU.max, negate=True), [mm])
                        ps.done(t)
                        pieces.append(t)
                        yield
                if (n + 1) * P > BANK:
                    both = neg_max[:, n, :, g * GROUP:(g + 1) * GROUP]
                    pieces = [dv.do(lambda e: e.tensor_tensor(both[:, 0, :], both[:, 0, :], both[:, 1, :], ALU.min),
                                    [pieces])]
                got += pieces
            yield from spread_maxima(b, g, got)

        def weigh_window(b, g):
            acc = psum.take()
            operands = [stacked[b, g], shifted[b, g]]
            later = None
            crossed = False
            for j in range(NT):
                q0 = j * P
                cols = min(P + WINDOW, T - q0)
                ps = psum.take()
                mm = []
                for i in range(GROUP):
                    h = g * GROUP + i
                    o = ps.ap[:, i * 256:i * 256 + cols]
                    pe.do(lambda e: e.matmul(o, k_stack[:, h, q0:q0 + P], q_stack[:, h, q0:q0 + cols], start=True,
                                             stop=False), [operands, ps.after])
                    mm.append(pe.do(lambda e: e.matmul(o, ident_bf[2.0 ** 60][:, :], w3["win_col"][:, 0:cols],
                                                       start=False, stop=True), [bf_ready]))
                pr = probs.take()
                view = lambda ap: ap[:, :].rearrange("p (i c) -> p i c", i=GROUP)[:, :, 0:cols]
                t = ac.do(lambda e: e.activation(view(pr.ap), view(ps.ap), ACT.Exp), [mm, pr.after])
                ps.done(t)

                def weigh(j, q0, cols, pr, t, crossed):
                    cuts = [(q0, BANK), (BANK, q0 + cols)] if q0 < BANK < q0 + cols else [(q0, q0 + cols)]
                    for a, c in cuts:
                        start = j == 0 or (a == BANK and not crossed)
                        for i in range(GROUP):
                            last = pe.do(lambda e: e.matmul(
                                acc.ap[32 * i:32 * i + 32, a:c], v_nat[:, j, g * GROUP + i, :],
                                pr.ap[:, i * 256 + a - q0:i * 256 + c - q0], start=start, stop=(j == NT - 1),
                                skip_group_check=True), [t, vals_ready[b], acc.after])
                    pr.done(last)
                    return last, crossed or len(cuts) == 2

                if later:
                    _, crossed = weigh(*later, crossed)
                later = (j, q0, cols, pr, t)
                yield
            last, _ = weigh(*later, crossed)
            t = ac.do(lambda e: e.activation(o_T[:, g, :], acc.ap[:, 0:T], ACT.Copy), [last, free["o_T"]])
            acc.done(t)
            weighed.setdefault(b, []).append(t)
            free["stack"][g] = [last]
            free["v_nat"] = [last]

        def weigh_causal(b, g):
            operands = [stacked[b, g], shifted[b, g]]
            for a0, c0 in blocks(T):
                acc = psum.take()
                keys = c0 // P
                later = None
                for j in range(keys):
                    a = max(a0, j * P)
                    n = c0 - a
                    for i0 in range(0, GROUP, 2):
                        ps = psum.take()
                        mm = []
                        for i in range(2):
                            h = g * GROUP + i0 + i
                            diag = a == j * P
                            t = pe.do(lambda e: e.matmul(ps.ap[:, i * BANK:i * BANK + n], k_stack[:, h, j * P:(j + 1) * P],
                                                         q_stack[:, h, a:c0], start=True, stop=not diag),
                                      [operands, ps.after])
                            if diag:
                                t = pe.do(lambda e: e.matmul(ps.ap[:, i * BANK:i * BANK + P], ident_bf[100.0][:, :],
                                                             w3["causal_col"][:, :], start=False, stop=True), [bf_ready])
                            mm.append(t)
                        pr = probs.take()
                        view = lambda ap: ap[:, :].rearrange("p (i c) -> p i c", i=2)[:, :, 0:n]
                        t = ac.do(lambda e: e.activation(view(pr.ap), view(ps.ap), ACT.Exp), [mm, pr.after])
                        ps.done(t)

                        def weigh(j, a, n, i0, pr, t):
                            for i in range(i0, i0 + 2):
                                last = pe.do(lambda e: e.matmul(
                                    acc.ap[32 * i:32 * i + 32, a - a0:a - a0 + n], v_nat[:, j, g * GROUP + i, :],
                                    pr.ap[:, (i - i0) * BANK:(i - i0) * BANK + n], start=(j == 0),
                                    stop=(j == keys - 1), skip_group_check=True), [t, vals_ready[b], acc.after])
                            pr.done(last)
                            return last

                        if later:
                            weigh(*later)
                        later = (j, a, n, i0, pr, t)
                        yield
                last = weigh(*later)
                t = ac.do(lambda e: e.activation(o_T[:, g, a0:c0], acc.ap[:, 0:c0 - a0], ACT.Copy), [last, free["o_T"]])
                acc.done(t)
                weighed.setdefault(b, []).append(t)
            free["stack"][g] = [last]
            free["v_nat"] = [last]

        def attended(b, n):
            ps = psum.take()
            tt = [pe.do(lambda e: e.transpose(ps.ap[:, g * P:(g + 1) * P], o_T[:, g, n * P:(n + 1) * P], ident),
                        [weighed[b], ps.after]) for g in range(GROUPS)]
            view = ps.ap[:, 0:GROUPS * P].rearrange("p (h c) -> p h c", c=32)
            iv = inv_den.take()
            t = dv.do(lambda e: e.reciprocal(iv.ap[:, :], view[:, :, HD]), [tt, iv.after])
            at = att.take()
            t = dv.do(lambda e: e.tensor_tensor(
                at.ap[:, :].rearrange("p (h d) -> p h d", d=HD), view[:, :, 0:HD],
                iv.ap[:, :].unsqueeze(2).to_broadcast([P, HEADS, HD]), ALU.mult), [t, at.after])
            iv.done(t)
            ps.done(t)
            return at, t, tt

        def turn_attended(at, t):
            ps = psum.take()
            t = pe.do(lambda e: e.transpose(ps.ap[:, 0:P], at.ap[:, :], ident), [t, ps.after])
            at.done(t)
            aT = attT.take()
            t = ac.do(lambda e: e.activation(aT.ap[:, :], ps.ap[:, 0:P], ACT.Copy), [t, aT.after])
            ps.done(t)
            return aT, t

        def project_out(aT, t, Wo, b, n, bias_row):
            ps = psum.take()
            t = pe.do(lambda e: e.matmul(ps.ap[:, 0:P], aT.ap[:, :], Wo, start=True, stop=True), [t, ready, ps.after])
            aT.done(t)
            tile = x[:, b * NT + n, :]
            if bias_row is not None:
                x_ready[b * NT + n] = gp.do(lambda e: e.tensor_tensor(tile, tile, bias_row, ALU.add),
                                            [x_ready[b * NT + n], normed[b]])
            t = dv.do(lambda e: e.tensor_tensor(tile, tile, ps.ap[:, 0:P], ALU.add),
                      [t, x_ready[b * NT + n], normed[b]])
            ps.done(t)
            x_ready[b * NT + n] = t

        def finish_row(b, mixed_tile, Wo, bias_row):
            turned = free["o_T"] = []
            at, aT = {}, {}
            for n in range(NT + 2):
                if n - 2 in aT:
                    project_out(*aT.pop(n - 2), Wo, b, n - 2, bias_row)
                if n - 1 in at:
                    aT[n - 1] = turn_attended(*at.pop(n - 1))
                if n < NT:
                    tile, t, tt = attended(b, n)
                    turned += tt
                    at[n] = (tile, mixed_tile(tile, t, n))
                yield

        def run_attention(prepare, open_row, finish, maxima, weigh, following):
            units = [(b, g) for b in range(batches) for g in range(GROUPS)]
            weave([prepare(0)])
            if not bf_ready:
                convert_constants()
            for g in range(GROUPS):
                load_stacks(0, g)
            opened = open_row(0)
            next(opened, None)
            next(opened, None)
            weave([maxima(*units[0])])
            tail = [two_by_two(maxima(*units[1]))]
            finishing = []
            for i, (b, g) in enumerate(units):
                ahead = [maxima(*units[i + 2])] if i + 2 < len(units) else []
                if g == 0:
                    preparing = [prepare(b + 1)] if b + 1 < batches else []
                norming = [early_norm()] if i == len(units) - 1 and b else []
                weave([weigh(b, g)], tail + ahead + finishing + ([opened] if g or not b else []) + preparing + norming)
                weave(norming)
                weave(tail)
                tail = ahead
                if g == 0:
                    weave(finishing)
                    finishing = []
                if g == 1:
                    weave(preparing)
                    preparing = []
                if b + 1 < batches:
                    for k in (() if g == 0 else (0, 1) if g == 1 else (g,)):
                        load_stacks(b + 1, k)
                if g == GROUPS - 1:
                    weave([opened])
                    finishing = [finish(b)]
                    if b + 1 < batches:
                        opened = open_row(b + 1)
                        next(opened, None)
                        next(opened, None)
            end_of_layer()
            weave(finishing + [following()])

        sources = {}

        def window_prepare(b):
            src, src_ready = yield from layer_norm(b)
            sources[b] = (src, src_ready)
            yield from split_to_scratch(w("a_wq"), src, src_ready, "q", None, b)
            yield from split_to_scratch(w("a_wk"), src, src_ready, "k", None, b)
            free["full_q"] = free["full_k"] = list(free["rest"])

        def window_open(b):
            values(w("a_wv"), *sources[b], None, b)
            yield

        def window_finish(b):
            yield from finish_row(b, lambda at, t, n: t, w("a_wo"), None)

        def window_attention():
            run_attention(window_prepare, window_open, window_finish, maxima_window, weigh_window, gla_begin)

        spread_k = Ring([carve([P, T]) for i in range(2)])
        spread_q = Ring([carve([P, T]) for i in range(2)])
        retain = carve([P, HD])
        alpha_T = carve([P // 2 + 1, T])
        alphas = [carve([P, NT, HEADS]) for i in range(2)]
        y_stp = carve([P, T])

        def clear_recurrence():
            t = ac.do(lambda e: e.activation(retain[:, :], w("c_lambda"), ACT.Exp), ready)
            t = dv.do(lambda e: e.tensor_scalar(retain[:, :], retain[:, :], 1.0, None, ALU.add), [t])
            cleared["alpha"] = gp.do(lambda e: e.memset(alpha_T[P // 2:P // 2 + 1, :], 1.0))
            return [dv.do(lambda e: e.reciprocal(retain[:, :], retain[:, :]), [t])]

        def recurrence(b, full_ready):
            y_free = free["y"]
            rows = {}

            def fetch(j):
                sk, sq = spread_k.take(), spread_q.take()
                loads = []
                for s, side in ((sk, "k"), (sq, "q")):
                    row = whole[side][b].rearrange("(h j) t -> h j t", j=HD)[:, j, :]
                    loads.append(dma(s.ap[:, :], row.unsqueeze(1).to_broadcast([HEADS, HD, T]),
                                     [there["whole_" + side, b], s.after]))
                rows[j] = [sk, sq, loads, None]

            def times_value(j):
                sk, _, loads, _ = rows[j]
                rows[j][3] = gp.do(lambda e: e.tensor_tensor(sk.ap[:, :], sk.ap[:, :], full["v"][:, :], ALU.mult),
                                   [loads[0], full_ready])
                free["full_v"] = [rows[j][3]]

            fetch(0)
            yield
            yield
            times_value(0)
            yield
            for j in range(HD):
                sk, sq, loads, t = rows[j]
                if j + 1 < HD:
                    fetch(j + 1)
                yield
                t = ac.do(lambda e: e.activation(sk.ap[:, :], sk.ap[:, :], ACT.Copy, scale=w("c_gamma", j, j + 1)),
                          [t, ready])
                yield
                t = dv.do(lambda e: e.tensor_tensor_scan(
                    sk.ap[:, :], retain[:, j:j + 1].to_broadcast([P, T]), sk.ap[:, :], 0.0, ALU.mult, ALU.add),
                    [t, ready])
                yield
                if j + 1 < HD:
                    times_value(j + 1)
                out = y_stp if j == 0 else sq.ap
                t = dv.do(lambda e: e.scalar_tensor_tensor(
                    out[:, :], sk.ap[:, :], w("c_static", j, j + 1), sq.ap[:, :], ALU.add, ALU.mult),
                    [t, loads[1], y_free])
                sk.done(t)
                yield
                if j:
                    t = gp.do(lambda e: e.tensor_tensor(y_stp[:, :], y_stp[:, :], sq.ap[:, :], ALU.add), [t, first])
                else:
                    first = t
                sq.done(t)
                yield
            y_ready[b] = t

        def causal_prepare(b):
            src, src_ready = yield from norm_of(b)
            sources[b] = (src, src_ready)
            yield from split_to_scratch(w("c_wq"), src, src_ready, "q", w("c_bq"), b)
            yield from split_to_scratch(w("c_wk"), src, src_ready, "k", w("c_bk"), b)

        def causal_open(b):
            src, src_ready = sources[b]
            ps = psum.take()
            mm = [pe.do(lambda e: e.matmul(ps.ap[0:P // 2, a:c], w("c_gw1"), src.ap[:, a:c], start=True, stop=True),
                        [src_ready, ps.after, ready]) for a, c in blocks(T)]
            t = ac.do(lambda e: e.activation(alpha_T[0:P // 2, :], ps.ap[0:P // 2, 0:T], ACT.Gelu,
                                             bias=w("c_gb1")), [mm, free["alpha"]])
            ps.done(t)
            ps = psum.take()
            mm = [pe.do(lambda e: e.matmul(ps.ap[:, n * HEADS:(n + 1) * HEADS], alpha_T[:, n * P:(n + 1) * P],
                                           w("c_gw2"), start=True, stop=True), [t, ps.after, cleared["alpha"]])
                  for n in range(NT)]
            exp_set(ac)
            av = alphas[b % 2][:, :, :].rearrange("p n h -> p (n h)")
            t = ac.do(lambda e: e.activation(av, ps.ap[:, 0:NT * HEADS], ACT.Exp, scale=-1.0), [mm, free["alpha"]])
            ps.done(t)
            t = dv.do(lambda e: e.tensor_scalar(av, av, 1.0, None, ALU.add), [t])
            alpha_ready[b] = dv.do(lambda e: e.reciprocal(av, av), [t])
            ps = psum.take()
            mm = [pe.do(lambda e: e.matmul(ps.ap[:, a:c], w("c_wv"), src.ap[:, a:c], start=True, stop=True),
                        [src_ready, ps.after]) for a, c in blocks(T)]
            t = dv.do(lambda e: e.tensor_scalar(full["v"][:, :], ps.ap[:, 0:T], w("c_bv"), None, ALU.add),
                      [mm, free["full_v"]])
            ps.done(t)
            yield
            values(w("c_wv"), src, src_ready, w("c_bv_row"), b)
            yield
            yield from recurrence(b, t)

        alpha_ready, y_ready = {}, {}

        def causal_finish(b):
            def mix(at, t, n):
                ps = psum.take()
                y_nat = pe.do(lambda e: e.transpose(ps.ap[:, 0:P], y_stp[:, n * P:(n + 1) * P], ident),
                              [y_ready[b], ps.after])
                free["y"] = [y_nat]
                y = ps.ap[:, 0:P]
                heads = at.ap[:, :].rearrange("p (h d) -> p h d", d=HD)
                t = dv.do(lambda e: e.tensor_tensor(at.ap[:, :], at.ap[:, :], y, ALU.subtract), [t, y_nat])
                t = dv.do(lambda e: e.tensor_tensor(
                    heads, heads, alphas[b % 2][:, n, :].unsqueeze(2).to_broadcast([P, HEADS, HD]), ALU.mult),
                    [t, alpha_ready[b]])
                t = dv.do(lambda e: e.tensor_tensor(at.ap[:, :], at.ap[:, :], y, ALU.add), [t])
                free["alpha"] = [t]
                ps.done(t)
                return t

            yield from finish_row(b, mix, w("c_wo"), w("c_bo_row"))

        def causal_mixed():
            run_attention(causal_prepare, causal_open, causal_finish, maxima_causal, weigh_causal, moe_begin)

        def first_largest(scores, eq, run, out, top, keep, after):
            n = scores.shape[2]
            f = lambda ap: ap.rearrange("p a b -> p (a b)")
            t = dv.do(lambda e: e.tensor_tensor(eq, scores, top.unsqueeze(2).to_broadcast([P, NT, n]),
                                                ALU.is_equal), after)
            t = dv.do(lambda e: e.tensor_tensor_scan(f(run), keep, f(eq), 0.0, ALU.mult, ALU.add), [t])
            return dv.do(lambda e: e.scalar_tensor_tensor(out, run, 1.0, eq, ALU.is_equal, ALU.mult), [t])

        def softmax_small(src, dst, small, n, after):
            bc = lambda ap: ap.unsqueeze(2).to_broadcast([P, NT, n])
            t = dv.do(lambda e: e.tensor_reduce(small[:, 0, :], src, AX.X, ALU.max), after)
            t = dv.do(lambda e: e.tensor_tensor(dst, src, bc(small[:, 0, :]), ALU.subtract), [t])
            done_src = t
            t = ac.do(lambda e: e.activation(dst, dst, ACT.Exp), [t])
            t = dv.do(lambda e: e.tensor_reduce(small[:, 1, :], dst, AX.X, ALU.add), [t])
            t = dv.do(lambda e: e.reciprocal(small[:, 1, :], small[:, 1, :]), [t])
            t = dv.do(lambda e: e.tensor_tensor(dst, dst, bc(small[:, 1, :]), ALU.mult), [t])
            return t, done_src

        def split_small(src, dst, n, tmp, tmp_bf, after):
            t = list(after)
            left = src
            for a in range(SPLIT):
                o = dst[:, :, a * n:(a + 1) * n]
                t = [dv.do(lambda e, left=left: e.tensor_copy(tmp_bf, left), t)]
                t = [dv.do(lambda e, o=o: e.tensor_copy(o, tmp_bf), t)]
                if a < SPLIT - 1:
                    t = [dv.do(lambda e, o=o, left=left: e.tensor_tensor(tmp, left, o, ALU.subtract), t)]
                    left = tmp
            return t

        def turn_rows(src, outs, after, free):
            ps = psum.take()
            rows = src.shape[2]
            tt = [pe.do(lambda e: e.transpose(ps.ap[0:rows, n * P:(n + 1) * P], src[:, n, :], ident),
                        [after, ps.after, ready]) for n in range(NT)]
            got = [ac.do(lambda e: e.activation(o[0:rows, :], ps.ap[0:rows, 0:T], ACT.Copy, scale=s), [tt, free])
                   for o, s in outs]
            ps.done(*got)
            return got, tt

        DENSE = 1 + ROUTES
        stack_words = HEADS * T
        used[0] = 0
        combined = {n: carve([P, GLA_HEADS * GLA_D]) for n in ("q2", "k2", "g1", "g2", "g")}
        route_p = carve([P, NT, ROUTES])
        route_s = carve([P, 2, NT])
        route_eq = carve([P, NT, ROUTES])
        route_run = carve([P, NT, ROUTES])
        route_hot = carve([P, NT, ROUTES])
        route_bf = carve([P, NT, ROUTES], BF16)
        route_top = carve([P, NT])
        rows_w = carve([P, NT, SPLIT * ROUTES])
        rows_h = rows_w
        w_T = carve([P, T], BF16)
        hot_T = carve([P, T], BF16)
        hot1_T = carve([P, T], BF16)
        gate_T = carve([P, PAIRS, T])
        keep4 = carve([P, NT, ROUTES])
        low_rank = gate_T[:, :, :].rearrange("p a t -> p (a t)")[:, 0:sizes["l"]] if PAIRS * T >= sizes["l"] \
            else carve([P, sizes["l"]])
        assert used[0] <= stack_words
        gla = {n: Ring([carve([P, BANK]) for i in range(k)]) for n, k in
               (("gk", 2), ("e", 2), ("up", 2), ("dn", 2), ("q1", 2), ("q2", 2), ("k1", 2), ("k2", 2),
                ("k2n", 1), ("k1nat", 1), ("k2nat", 1), ("o", 1), ("rs", 1))}
        q_pad = [carve([P, PAIRS, 2, P]) for i in range(2)]
        q2m = Ring([carve([P, ROUTES, PAIRS * P]) for i in range(2)])
        hot_b = Ring([carve([P, ROUTES * P])])
        v5 = Ring([carve([P, DENSE, BANK]) for i in range(2)])
        masked1 = Ring([carve([P, GLA_HEADS * P])])
        masked2 = Ring([carve([P, GLA_HEADS * P])])
        mix = Ring([carve([P, P + 2 * ROUTES]) for i in range(2)])
        mix_tril = Ring([carve([P, P]) for i in range(2)])
        kmax = Ring([carve([P, 2, GLA_HEADS]) for i in range(2)])
        decay = Ring([carve([P, PAIRS, 2, DENSE]) for i in range(3)])
        factor = carve([P, PAIRS, DENSE])
        state = carve([P, PAIRS, DENSE, GLA_D])
        state_mid = carve([P, PAIRS, DENSE, GLA_D])
        state_dg = carve([P, PAIRS, DENSE, 2, GLA_D])
        second_xnT_b = carve([P, T])
        gla_free = {"route": [], "rows": [], "gate": [], "mid": [], "dg": [], "pad": [[], []]}

        def clear_gla():
            return [gp.do(lambda e: e.memset(t, 0.0)) for t in (state_dg[:, :, :, :, :], q_pad[0], q_pad[1])]

        def gla_begin():
            got = [gp.do(lambda e: e.memset(t, 0.0)) for t in (w_T[:, :], hot_T[:, :], hot1_T[:, :])]
            t = gp.do(lambda e: e.memset(keep4[:, :, :], 1.0))
            got.append(gp.do(lambda e: e.memset(keep4[:, :, 0:1], 0.0), [t]))
            low = dma(low_rank, packed["l"])
            for n in combined:
                ps = psum.take()
                t = pe.do(lambda e, n=n, ps=ps: e.matmul(ps.ap[:, 0:BANK], w(f"b_{n}a"), w(f"b_{n}b"), start=True,
                                                         stop=True), [ready, low, ps.after])
                t = ac.do(lambda e, n=n, ps=ps: e.activation(combined[n][:, :], ps.ap[:, 0:BANK], ACT.Copy,
                                                             scale=GLA_D ** -0.5 if n == "q2" else 1.0), [t])
                ps.done(t)
                got.append(t)
            ready.extend(got)
            yield
            yield from gla_route(0)

        routing = {}

        def gla_route(b):
            src, src_ready = yield from norm_of(b)
            base = [src_ready, ready]
            ps = psum.take()
            mm = [pe.do(lambda e: e.matmul(ps.ap[:, n * ROUTES:(n + 1) * ROUTES], src.ap[:, n * P:(n + 1) * P],
                                           w("b_we"), start=True, stop=True), [base, ps.after])
                  for n in range(NT)]
            t, used = softmax_small(ps.ap[:, 0:NT * ROUTES].rearrange("p (n e) -> p n e", e=ROUTES),
                                    route_p[:, :, :], route_s, ROUTES, [mm, gla_free["route"]])
            ps.done(used)
            t_top = dv.do(lambda e: e.tensor_reduce(route_top[:, :], route_p[:, :, :], AX.X, ALU.max), [t])
            yield
            hot = first_largest(route_p[:, :, :], route_eq[:, :, :], route_run[:, :, :], route_hot[:, :, :],
                                route_top[:, :], keep4[:, :, :].rearrange("p a b -> p (a b)"),
                                [t_top, ready, gla_free["rows"]])
            t = [dv.do(lambda e: e.tensor_copy(rows_h[:, :, a * ROUTES:(a + 1) * ROUTES], route_hot[:, :, :]),
                       [hot, gla_free["rows"]]) for a in range(SPLIT)]
            yield
            g1, tt = turn_rows(rows_h, [(hot_T, 1.0), (hot1_T, w("route_first", 0, 1)[0:SPLIT * ROUTES, :])], t,
                               gla_free["rows"])
            t = dv.do(lambda e: e.tensor_tensor(route_eq[:, :, :], route_p[:, :, :], route_hot[:, :, :], ALU.mult), [hot])
            yield
            t = split_small(route_eq[:, :, :], rows_w, ROUTES, route_run[:, :, :], route_bf[:, :, :], [t, tt])
            yield
            g2, tt = turn_rows(rows_w, [(w_T, 1.0)], t, gla_free["rows"])
            routing[b] = (src, base, g1 + g2, hot, t_top)
            yield

        def gla_gate(b):
            src, base = routing[b][0:2]
            for p in range(PAIRS):
                ps = psum.take()
                mm = [pe.do(lambda e: e.matmul(ps.ap[:, a:c], combined["g"][:, p * P:(p + 1) * P], src.ap[:, a:c],
                                               start=True, stop=True), [base, ps.after]) for a, c in blocks(T)]
                gated = ac.do(lambda e: e.activation(gate_T[:, p, :], ps.ap[:, 0:T], ACT.Silu),
                              [mm, gla_free["gate"]])
                ps.done(gated)
            exp_set(ac)
            gates[b] = gated

        def gla_row(b):
            gla_gate(b)
            weave([produce(b, 0)])
            for n in range(NT):
                others = []
                if n:
                    others.append(finish(b, n - 1))
                if n + 1 < NT:
                    others.append(produce(b, n + 1))
                elif b + 1 < batches:
                    gla_free["route"] = gla_free["rows"] = [(pe, pe.count), (dv, dv.count), (ac, ac.count), (gp, gp.count)]
                    others.append(gla_route(b + 1))
                elif xnT.free[0][0] is not second_xnT_b:
                    others.append(early_norm())
                weave([consume(b, n)] + others)
            weave([finish(b, NT - 1)])
            state_of[b]["decay"].done((dv, dv.count))
            routing[b][0].done((pe, pe.count))
            gla_free["gate"] = [(dv, dv.count)]

        made, summed, gates = {}, {}, {}
        state_of = {b: {} for b in range(batches)}
        head_cols = lambda ap: ap.rearrange("p (h d) -> p h d", d=GLA_D)
        pair_cols = lambda ap: ap.rearrange("p (a c) -> p a c", a=PAIRS)
        over_head = lambda ap: ap.unsqueeze(2).to_broadcast([P, GLA_HEADS, GLA_D])

        def produce(b, n):
            src, base, routed, hot, t_top = routing[b]
            tok = slice(n * P, (n + 1) * P)
            xt = src.ap[:, tok]
            gk, gk_ready = [], []
            ps = psum.take()
            mm = [pe.do(lambda e: e.matmul(ps.ap[:, i * BANK:(i + 1) * BANK], xt, combined[f"g{i + 1}"][:, :],
                                           start=True, stop=True), [base, ps.after]) for i in range(2)]
            zs = []
            for i in range(2):
                z = gla["gk"].take()
                zs.append((z, dv.do(lambda e: e.tensor_tensor(z.ap[:, :], ps.ap[:, i * BANK:(i + 1) * BANK],
                                                              w(f"b_bg{i + 1}"), ALU.add), [mm, z.after])))
            ps.done(zs[0][1], zs[1][1])
            yield
            for z, tz in zs:
                el = gla["e"].take()
                t = dv.do(lambda e: e.scalar_tensor_tensor(el.ap[:, :], z.ap[:, :], -1.0, z.ap[:, :], ALU.mult,
                                                           ALU.min), [tz, el.after])
                t = ac.do(lambda e: e.activation(el.ap[:, :], el.ap[:, :], ACT.Exp), [t])
                t = ac.do(lambda e: e.activation(el.ap[:, :], el.ap[:, :], ACT.Ln, bias=w("ones")), [t])
                t = dv.do(lambda e: e.scalar_tensor_tensor(z.ap[:, :], z.ap[:, :], 0.0, el.ap[:, :], ALU.min,
                                                           ALU.subtract), [t])
                el.done(t)
                gk.append(z)
                gk_ready.append(t)
            ps = psum.take()
            m1 = pe.do(lambda e: e.matmul(ps.ap[:, 0:P], hot_T[:, tok], hot1_T[:, tok], start=True, stop=True),
                       [routed, ps.after])
            m2 = pe.do(lambda e: e.matmul(ps.ap[:, P:2 * P], hot_T[:, tok], w_T[:, tok], start=True, stop=True),
                       [routed])
            m3 = [pe.do(lambda e: e.matmul(ps.ap[:, BANK + r * P:BANK + (r + 1) * P],
                                           w3["route_bcast"][:, r * P:(r + 1) * P], w_T[:, tok],
                                           start=True, stop=True), [routed]) for r in range(ROUTES)]
            mx, mt, hb = mix.take(), mix_tril.take(), hot_b.take()
            u1 = dv.do(lambda e: e.tensor_tensor(mx.ap[:, 0:P], ps.ap[:, 0:P], w("gate_sum", 0, P), ALU.mult),
                       [m1, m2, mx.after])
            u2 = dv.do(lambda e: e.tensor_tensor(
                mx.ap[:, P:P + 2 * ROUTES].rearrange("p (k r) -> p k r", k=2),
                route_hot[:, n, :].unsqueeze(1).to_broadcast([P, 2, ROUTES]),
                w("half").unsqueeze(2).to_broadcast([P, 2, ROUTES]), ALU.mult), [hot, mx.after])
            u3 = dv.do(lambda e: e.tensor_tensor(mt.ap[:, :], ps.ap[:, P:2 * P], w("tril"), ALU.mult), [m2, mt.after])
            u4 = ac.do(lambda e: e.activation(hb.ap[:, :], ps.ap[:, BANK:2 * BANK], ACT.Copy), [m3, hb.after])
            ps.done(u1, u3, u4)
            yield
            ps = psum.take()
            t = pe.do(lambda e: e.matmul(ps.ap[:, 0:BANK], xt, w("b_wv"), start=True, stop=True), [base, ps.after])
            vv = v5.take()
            tv = [ac.do(lambda e: e.activation(vv.ap[:, 0, :], ps.ap[:, 0:BANK], ACT.Copy), [t, vv.after])]
            for r in range(ROUTES):
                if r % 4 == 3:
                    tv.append(ac.do(lambda e: e.activation(vv.ap[:, 1 + r, :], ps.ap[:, 0:BANK], ACT.Copy,
                                                           scale=route_hot[:, n, r:r + 1]), [t, vv.after, hot]))
                else:
                    tv.append(dv.do(lambda e: e.tensor_scalar(vv.ap[:, 1 + r, :], vv.ap[:, 0, :],
                                                              route_hot[:, n, r:r + 1], None, ALU.mult),
                                    [tv[0], vv.after, hot]))
            ps.done(*tv)
            yield
            ps = psum.take()
            mq = [pe.do(lambda e: e.matmul(ps.ap[:, p * P:(p + 1) * P], combined["q2"][:, p * P:(p + 1) * P], xt,
                                           start=True, stop=True), [base, ps.after]) for p in range(PAIRS)]
            mk = pe.do(lambda e: e.matmul(ps.ap[:, BANK:2 * BANK], xt, combined["k2"][:, :], start=True, stop=True),
                       [base])
            km, kn = kmax.take(), gla["k2n"].take()
            t = dv.do(lambda e: e.tensor_reduce(km.ap[:, 0, :], head_cols(ps.ap[:, BANK:2 * BANK]), AX.X, ALU.max),
                      [mk, km.after])
            t = dv.do(lambda e: e.tensor_tensor(head_cols(kn.ap[:, :]), head_cols(ps.ap[:, BANK:2 * BANK]),
                                                over_head(km.ap[:, 0, :]), ALU.subtract), [t, kn.after])
            sub = t
            t = ac.do(lambda e: e.activation(kn.ap[:, :], kn.ap[:, :], ACT.Exp), [t])
            t = dv.do(lambda e: e.tensor_reduce(km.ap[:, 0, :], head_cols(kn.ap[:, :]), AX.X, ALU.add), [t])
            t = dv.do(lambda e: e.reciprocal(km.ap[:, 1, :], km.ap[:, 0, :]), [t])
            t = dv.do(lambda e: e.tensor_scalar(km.ap[:, 0, :], km.ap[:, 1, :], route_top[:, n:n + 1], None,
                                                ALU.mult), [t, t_top])
            k_soft = dv.do(lambda e: e.tensor_tensor(head_cols(kn.ap[:, :]), head_cols(kn.ap[:, :]),
                                                     over_head(km.ap[:, 0, :]), ALU.mult), [t])
            km.done(k_soft)
            q2_proj = ps
            up, dn, dc = [], [], decay.take()
            sums_ready, dcs = [[], []], []
            for i in range(2):
                cols = P + (2 if i == 0 else 2 * ROUTES)
                rhs = w("gate_sum") if i == 0 else mx.ap[:, 0:cols]
                ps = psum.take()
                mm = [pe.do(lambda e: e.matmul(ps.ap[:, p * 256:p * 256 + cols], gk[i].ap[:, p * P:(p + 1) * P], rhs,
                                               start=True, stop=True), [gk_ready[i], u1, u2, ps.after])
                      for p in range(PAIRS)]
                gk[i].done(mm[-1])
                v4 = pair_cols(ps.ap[:, :])
                for lst, name, sc in ((up, "up", 1.0), (dn, "dn", -1.0)):
                    s = gla[name].take()
                    t1 = ac.do(lambda e: e.activation(pair_cols(s.ap[:, :]), v4[:, :, 0:P], ACT.Exp, scale=sc),
                               [mm, s.after])
                    lst.append(s)
                    sums_ready[i].append(t1)
                d = 1 if i == 0 else ROUTES
                first = 0 if i == 0 else 1
                t1 = ac.do(lambda e: e.activation(
                    dc.ap[:, :, :, first:first + d],
                    v4[:, :, P:P + 2 * d].rearrange("p a (k d) -> p a k d", k=2), ACT.Exp), [mm, dc.after])
                dcs.append(t1)
                ps.done(t1)
            mx.done(mm[-1])
            q1, k1, q2, k2 = (gla[s].take() for s in ("q1", "k1", "q2", "k2"))
            tq2 = dv.do(lambda e: e.tensor_tensor(q2.ap[:, :], q2_proj.ap[:, 0:BANK], up[1].ap[:, :], ALU.mult),
                        [mq, sums_ready[1], q2.after])
            up[1].done(tq2)
            q2_proj.done(tq2, sub)
            yield
            ps = psum.take()
            mq = [pe.do(lambda e: e.matmul(ps.ap[:, p * P:(p + 1) * P], w("b_wq", p * P, (p + 1) * P), xt,
                                           start=True, stop=True), [base, ps.after]) for p in range(PAIRS)]
            mk = [pe.do(lambda e: e.matmul(ps.ap[:, BANK + p * P:BANK + (p + 1) * P], w("b_wk", p * P, (p + 1) * P),
                                           xt, start=True, stop=True), [base]) for p in range(PAIRS)]
            tq1 = dv.do(lambda e: e.scalar_tensor_tensor(q1.ap[:, :], ps.ap[:, 0:BANK], GLA_D ** -0.5,
                                                         up[0].ap[:, :], ALU.mult, ALU.mult),
                        [mq, sums_ready[0], q1.after])
            tk1 = dv.do(lambda e: e.tensor_tensor(k1.ap[:, :], ps.ap[:, BANK:2 * BANK], dn[0].ap[:, :], ALU.mult),
                        [mk, sums_ready[0], k1.after])
            ps.done(tq1, tk1)
            up[0].done(tq1)
            dn[0].done(tk1)
            qm = q2m.take()
            tm = [gp.do(lambda e: e.tensor_tensor(
                pair_cols(qm.ap[:, r, :]), pair_cols(q2.ap[:, :]),
                hb.ap[:, r * P:(r + 1) * P].unsqueeze(1).to_broadcast([P, PAIRS, P]), ALU.mult),
                [tq2, u4, qm.after]) for r in range(ROUTES)]
            hb.done(tm[-1])
            yield
            ps = psum.take()
            tt = [pe.do(lambda e: e.transpose(ps.ap[:, p * P:(p + 1) * P], kn.ap[:, p * P:(p + 1) * P], ident),
                        [k_soft, ps.after]) for p in range(PAIRS)]
            kn.done(tt[-1])
            tk2 = dv.do(lambda e: e.tensor_tensor(k2.ap[:, :], ps.ap[:, 0:BANK], dn[1].ap[:, :], ALU.mult),
                        [tt, k2.after])
            dn[1].done(tk2)
            ps.done(tk2)
            pads = []
            for i, (q, tq) in enumerate(((q1, tq1), (q2, tq2))):
                for r in range(2):
                    rows = slice(r * GLA_D, (r + 1) * GLA_D)
                    pads.append(ac.do(lambda e: e.activation(q_pad[i][rows, :, r, :], pair_cols(q.ap[rows, :]),
                                                             ACT.Copy), [tq, gla_free["pad"][i], ready]))
            made[b, n] = dict(pads=pads, q=(q1, q2), k=(k1, k2), tq=(tq1, tq2), tk=(tk1, tk2), qm=qm, tm=tm, vv=vv, tv=tv,
                              mt=mt, u3=u3, dc=dc, dcs=dcs)
            yield

        def consume(b, n):
            m = made.pop((b, n))
            st = state_of[b]
            vv, tv, qm, mt = m["vv"], m["tv"], m["qm"], m["mt"]
            pads = m["pads"]
            if n:
                prev = st["decay"]
                tf = dv.do(lambda e: e.tensor_tensor(factor[:, :, :], prev.ap[:, :, 0, :], m["dc"].ap[:, :, 1, :],
                                                     ALU.mult), [m["dcs"], gla_free["mid"]])
                prev.done(tf)
                t_mid = gp.do(lambda e: e.tensor_tensor(
                    state_mid[:, :, :, :].rearrange("p a r d -> p (a r) d"),
                    state[:, :, :, :].rearrange("p a r d -> p (a r) d"),
                    factor[:, :, :].rearrange("p a r -> p (a r)").unsqueeze(2).to_broadcast([P, PAIRS * DENSE, GLA_D]),
                    ALU.mult), [tf, st["ready"], gla_free["mid"]])
            st["decay"] = m["dc"]
            yield
            nats, k_turned = [], []
            ps = psum.take()
            for i, name in ((0, "k1nat"), (1, "k2nat")):
                k_ = m["k"][i]
                o = i * BANK
                tt = [pe.do(lambda e: e.transpose(ps.ap[:, o + p * P:o + (p + 1) * P], k_.ap[:, p * P:(p + 1) * P],
                                                  ident), [m["tk"][i], ps.after]) for p in range(PAIRS)]
                k_turned.append(tt[-1])
                kn = gla[name].take()
                t = ac.do(lambda e: e.activation(kn.ap[:, :], ps.ap[:, o:o + BANK], ACT.Copy), [tt, kn.after])
                nats.append((kn, t))
            ps.done(nats[0][1], nats[1][1])
            yield
            masked = []
            for i, ring, mask in ((0, masked1, w("tril")), (1, masked2, mt.ap[:, :])):
                ps = psum.take()
                k_ = m["k"][i]
                mm = [pe.do(lambda e: e.matmul(ps.ap[:, p * 256:(p + 1) * 256], k_.ap[:, p * P:(p + 1) * P],
                                               q_pad[i][:, p, :, :].rearrange("p r c -> p (r c)"), start=True,
                                               stop=True), [pads, m["tk"][i], ps.after]) for p in range(PAIRS)]
                gla_free["pad"][i] = [mm[-1]]
                mk_ = ring.take()
                t = dv.do(lambda e: e.tensor_tensor(
                    mk_.ap[:, :].rearrange("p (h c) -> p h c", c=P), ps.ap[:, :].rearrange("p (h c) -> p h c", c=P),
                    mask.unsqueeze(1).to_broadcast([P, GLA_HEADS, P]), ALU.mult), [mm, mk_.after, m["u3"]])
                ps.done(t)
                k_.done(k_turned[i], mm[-1])
                masked.append((mk_, t))
                yield
            mt.done(masked[1][1])
            if n:
                t_dg = [ac.do(lambda e: e.activation(
                    state_dg[r * GLA_D:(r + 1) * GLA_D, :, :, r, :], state_mid[r * GLA_D:(r + 1) * GLA_D, :, :, :],
                    ACT.Copy), [t_mid, gla_free["dg"], ready]) for r in range(2)]
            ups = []
            for p0 in range(0, PAIRS, 2):
                ps = psum.take()
                for p in (p0, p0 + 1):
                    o = (p - p0) * BANK
                    for r in range(2):
                        h = 2 * p + r
                        cols = slice(h * GLA_D, (h + 1) * GLA_D)
                        pe.do(lambda e: e.matmul(
                            ps.ap[r * GLA_D:(r + 1) * GLA_D, o:o + GLA_D], nats[0][0].ap[:, cols], vv.ap[:, 0, cols],
                            start=True, stop=True, skip_group_check=True), [nats[0][1], tv, ps.after])
                        kv = pe.do(lambda e: e.matmul(
                            ps.ap[r * GLA_D:(r + 1) * GLA_D, o + GLA_D:o + DENSE * GLA_D], nats[1][0].ap[:, cols],
                            vv.ap[:, 1:DENSE, cols], start=True, stop=True, skip_group_check=True),
                            [nats[1][1], tv])
                src_ps = ps.ap[:, :].rearrange("p (a c) -> p a c", a=2)[:, :, 0:DENSE * GLA_D]
                dst = state[:, p0:p0 + 2, :, :].rearrange("p a r d -> p a (r d)")
                if n:
                    mid = state_mid[:, p0:p0 + 2, :, :].rearrange("p a r d -> p a (r d)")
                    t = dv.do(lambda e: e.tensor_tensor(dst, src_ps, mid, ALU.add), [kv, t_mid])
                else:
                    t = dv.do(lambda e: e.tensor_copy(dst, src_ps), [kv, gla_free["mid"]])
                ps.done(t)
                ups.append(t)
                yield
            acc = psum.take()
            for mk_, t in masked:
                first = mk_ is masked[0][0]
                for h in range(GLA_HEADS):
                    r0 = (h % 2) * GLA_D
                    last = pe.do(lambda e: e.matmul(
                        acc.ap[r0:r0 + GLA_D, (h // 2) * P:(h // 2 + 1) * P], vv.ap[:, 0, h * GLA_D:(h + 1) * GLA_D],
                        mk_.ap[:, h * P:(h + 1) * P], start=first and h < 2, stop=not first and n == 0,
                        skip_group_check=True), [t, tv, acc.after])
                mk_.done(last)
                yield
            for kn, _ in nats:
                kn.done(kv)
            vv.done(kv, last)
            st["ready"] = ups
            gla_free["mid"] = ups + (t_dg if n else [])
            if n:
                for p in range(PAIRS):
                    for r in range(DENSE):
                        rhs = m["q"][0].ap[:, p * P:(p + 1) * P] if r == 0 else qm.ap[:, r - 1, p * P:(p + 1) * P]
                        last = pe.do(lambda e: e.matmul(
                            acc.ap[:, p * P:(p + 1) * P], state_dg[:, p, r, :, :].rearrange("p a b -> p (a b)"),
                            rhs, start=False, stop=(r == DENSE - 1), skip_group_check=True), [t_dg, m["tm"]])
                    yield
                gla_free["dg"] = [last]
            m["q"][0].done(last, pads)
            m["q"][1].done(m["tm"][-1], pads)
            qm.done(last)
            o = gla["o"].take()
            t = ac.do(lambda e: e.activation(o.ap[:, :], acc.ap[:, 0:BANK], ACT.Copy), [last, o.after])
            acc.done(t)
            summed[b, n] = (o, t)

        def finish(b, n):
            o, t_o = summed.pop((b, n))
            rs = gla["rs"].take()
            t = ac.do(lambda e: e.activation(rs.ap[:, :], o.ap[:, :], ACT.Square), [t_o, rs.after])
            yield
            yield
            yield
            ps = psum.take()
            t = pe.do(lambda e: e.matmul(ps.ap[:, 0:BANK], w("head_mean"), rs.ap[:, :], start=True, stop=True),
                      [t, ps.after])
            t = ac.do(lambda e: e.activation(rs.ap[:, :], ps.ap[:, 0:BANK], ACT.Ln, bias=w("eps")), [t])
            ps.done(t)
            t = ac.do(lambda e: e.activation(rs.ap[:, :], rs.ap[:, :], ACT.Exp, scale=-0.5), [t])
            t = dv.do(lambda e: e.scalar_tensor_tensor(rs.ap[:, :], o.ap[:, :], w("b_norm"), rs.ap[:, :], ALU.mult,
                                                       ALU.mult), [t])
            o.done(t)
            yield
            t = dv.do(lambda e: e.tensor_tensor(pair_cols(rs.ap[:, :]), pair_cols(rs.ap[:, :]),
                                                gate_T[:, :, n * P:(n + 1) * P], ALU.mult), [t, gates[b]])
            t_gate = t
            yield
            yield
            ps = psum.take()
            for p in range(PAIRS):
                t = pe.do(lambda e: e.matmul(ps.ap[:, 0:P], rs.ap[:, p * P:(p + 1) * P], w("b_wo", p * P, (p + 1) * P),
                                             start=(p == 0), stop=(p == PAIRS - 1)), [t_gate, ps.after])
            rs.done(t)
            tile = x[:, b * NT + n, :]
            t = dv.do(lambda e: e.tensor_tensor(tile, tile, ps.ap[:, 0:P], ALU.add),
                      [t, x_ready[b * NT + n], normed[b]])
            ps.done(t)
            x_ready[b * NT + n] = t

        NG = EXPERTS + 1
        used[0] = 0
        moe_p = carve([P, NT, EXPERTS])
        moe_s = carve([P, 2, NT])
        moe_eq = carve([P, NT, EXPERTS])
        moe_run = carve([P, NT, EXPERTS])
        moe_hot = carve([P, 2, NT, EXPERTS])
        moe_w = carve([P, NT, NG])
        moe_tmp = carve([P, NT, NG])
        moe_bf = carve([P, NT, NG], BF16)
        keep16 = carve([P, NT, EXPERTS])
        moe_T = Ring([carve([P, T], BF16) for i in range(2)])
        moe_rows = carve([P, NT, P])
        act = Ring([carve([P, BANK]) for i in range(2)])
        hid = Ring([carve([P, BANK]) for i in range(3)])
        second_xnT = carve([P, T])
        assert used[0] <= stack_words
        moe_free = [[]]
        mixed = {}

        def moe_begin():
            ready.extend(loaded_d)
            xnT.free.append((second_xnT, []))
            t = gp.do(lambda e: e.memset(keep16[:, :, :], 1.0))
            ready.extend([gp.do(lambda e: e.memset(keep16[:, :, 0:1], 0.0), [t]),
                          gp.do(lambda e: e.memset(moe_rows[:, :, :], 0.0))])
            yield from route(0)

        def route(b):
            src, src_ready = yield from norm_of(b)
            ps = psum.take()
            mfree = moe_free[0]
            mm = [pe.do(lambda e: e.matmul(ps.ap[:, n * 32:n * 32 + NG], src.ap[:, n * P:(n + 1) * P], w("d_wg"),
                                           start=True, stop=True), [src_ready, ready, ps.after])
                  for n in range(NT)]
            lg = ps.ap[:, 0:NT * 32].rearrange("p (n e) -> p n e", e=32)
            t, used = softmax_small(lg[:, :, 0:EXPERTS], moe_p[:, :, :], moe_s, EXPERTS, [mm, mfree])
            s0 = ac.do(lambda e: e.activation(moe_w[:, :, EXPERTS], lg[:, :, EXPERTS], ACT.Exp, scale=-1.0), [mm, mfree])
            ps.done(used, s0)
            s1 = dv.do(lambda e: e.tensor_scalar(moe_w[:, :, EXPERTS], moe_w[:, :, EXPERTS], 1.0, None, ALU.add), [s0])
            s1 = dv.do(lambda e: e.reciprocal(moe_w[:, :, EXPERTS], moe_w[:, :, EXPERTS]), [s1])
            keep = keep16[:, :, :].rearrange("p a b -> p (a b)")
            t = dv.do(lambda e: e.tensor_reduce(moe_s[:, 0, :], moe_p[:, :, :], AX.X, ALU.max), [t])
            yield
            t = first_largest(moe_p[:, :, :], moe_eq[:, :, :], moe_run[:, :, :], moe_hot[:, 0, :, :], moe_s[:, 0, :],
                              keep, [t, ready])
            t = dv.do(lambda e: e.scalar_tensor_tensor(moe_tmp[:, :, 0:EXPERTS], moe_hot[:, 0, :, :], -2.0,
                                                       moe_p[:, :, :], ALU.mult, ALU.add), [t])
            t = dv.do(lambda e: e.tensor_reduce(moe_s[:, 1, :], moe_tmp[:, :, 0:EXPERTS], AX.X, ALU.max), [t])
            yield
            t = first_largest(moe_tmp[:, :, 0:EXPERTS], moe_eq[:, :, :], moe_run[:, :, :], moe_hot[:, 1, :, :],
                              moe_s[:, 1, :], keep, [t])
            t = dv.do(lambda e: e.tensor_tensor(moe_hot[:, 0, :, :], moe_hot[:, 0, :, :], moe_hot[:, 1, :, :], ALU.add), [t])
            t = dv.do(lambda e: e.tensor_tensor(moe_hot[:, 0, :, :], moe_hot[:, 0, :, :], moe_p[:, :, :], ALU.mult), [t])
            yield
            t = dv.do(lambda e: e.tensor_tensor(moe_s[:, 0, :], moe_s[:, 0, :], moe_s[:, 1, :], ALU.add), [t])
            t = dv.do(lambda e: e.reciprocal(moe_s[:, 0, :], moe_s[:, 0, :]), [t])
            t = dv.do(lambda e: e.tensor_tensor(moe_w[:, :, 0:EXPERTS], moe_hot[:, 0, :, :],
                                                moe_s[:, 0, :].unsqueeze(2).to_broadcast([P, NT, EXPERTS]),
                                                ALU.mult), [t])
            yield
            t = split_small(moe_w[:, :, :], moe_rows, NG, moe_tmp[:, :, :], moe_bf[:, :, :], [t, s1, mfree])
            rows = moe_T.take()
            g, tt = turn_rows(moe_rows, [(rows.ap, 1.0)], t, rows.after)
            moe_free[0] = [tt, t, (ac, ac.count)]
            mixed[b] = (src, src_ready, rows, g)
            yield

        def experts(b):
            src, src_ready, rows, rows_ready = mixed.pop(b)
            both = psum.take()
            total, spread = both.ap[:, 0:BANK], both.ap[:, BANK:2 * BANK]
            total_free = spread_free = both.after

            def down(f, hd, t, n_tiles):
                for n in range(n_tiles):
                    m = pe.do(lambda e: e.matmul(
                        total[:, n * P:(n + 1) * P], hd.ap[:, n * P:(n + 1) * P], w("d_down", f * P, (f + 1) * P),
                        start=(f == 0 and n == 0), stop=(f == MOE_TILES - 1), skip_group_check=True),
                        [t, total_free])
                hd.done(m)
                return m

            later = None
            for a, c in blocks(T):
                n0, n1, cols = b * NT + a // P, b * NT + c // P, c - a
                for f in range(MOE_TILES):
                    ps = psum.take()
                    mg = pe.do(lambda e: e.matmul(ps.ap[:, 0:cols], w("d_gate", f * P, (f + 1) * P), src.ap[:, a:c],
                                                  start=True, stop=True), [src_ready, ps.after])
                    mu = pe.do(lambda e: e.matmul(ps.ap[:, BANK:BANK + cols], w("d_up", f * P, (f + 1) * P),
                                                  src.ap[:, a:c], start=True, stop=True), [src_ready])
                    s = min(f, EXPERTS // 2)
                    mw = pe.do(lambda e: e.matmul(spread[:, 0:cols], w3["moe_bcast"][:, s * P:(s + 1) * P],
                                                  rows.ap[:, a:c], start=True, stop=True), [rows_ready, spread_free])
                    ag, hd = act.take(), hid.take()
                    t = ac.do(lambda e: e.activation(ag.ap[:, 0:cols], ps.ap[:, 0:cols], ACT.Silu), [mg, ag.after])
                    t = dv.do(lambda e: e.tensor_tensor(ag.ap[:, 0:cols], ag.ap[:, 0:cols],
                                                        ps.ap[:, BANK:BANK + cols], ALU.mult), [t, mu])
                    ps.done(t)
                    t = dv.do(lambda e: e.tensor_tensor(hd.ap[:, 0:cols], ag.ap[:, 0:cols], spread[:, 0:cols],
                                                        ALU.mult), [t, mw, hd.after])
                    spread_free = [t]
                    ag.done(t)
                    if f:
                        down(*later)
                    later = (f, hd, t, cols // P)
                    yield
                m = down(*later)
                t = dv.do(lambda e: e.tensor_tensor(
                    x[:, n0:n1, :], x[:, n0:n1, :], total[:, 0:cols].rearrange("p (n d) -> p n d", d=P), ALU.add),
                    [m, x_ready[n0:n1], normed[b]])
                total_free = [t]
                stored.append(dma(out_dram[:, n0:n1, :], x[:, n0:n1, :], [t]))
            both.done(t, spread_free)
            rows.done((pe, pe.count))
            src.done((pe, pe.count))

        stored = []
        def all_gla():
            ready.extend(clear_gla())
            xnT.free.append((second_xnT_b, []))
            for b in range(batches):
                gla_row(b)
            xnT.free = [f for f in xnT.free if f[0] is not second_xnT_b]

        def all_moe():
            for b in range(batches):
                weave([experts(b)] + ([route(b + 1)] if b + 1 < batches else []))

        clear_attention()
        window_attention()
        end_of_layer()
        loaded_c = load("c")
        ready += load_b
        all_gla()
        end_of_layer()
        loaded_d = load("d")
        ready += loaded_c
        clear_attention()
        ready += clear_recurrence()
        causal_mixed()
        end_of_layer()
        all_moe()
        sp.wait(stored)


def pack(parts):
    place, width = {}, {}
    for name, a in parts.items():
        layer = "s" if name in BF_CONSTANTS else "l" if name[-1] in "ab" and name[0] == "b" else name[0] if name[1] == "_" else "k"
        place[name] = (layer, width.get(layer, 0), a.shape[0], a.shape[1])
        width[layer] = width.get(layer, 0) + a.shape[1]
    out = {layer: np.zeros((P, n), np.float32) for layer, n in width.items()}
    for name, a in parts.items():
        layer, first, rows, cols = place[name]
        out[layer][:rows, first:first + cols] = a
    return out, place


def weight_columns(i):
    rows = lambda a: a.reshape(-1, P, a.shape[1]).transpose(1, 0, 2).reshape(P, -1)
    every = lambda v: np.tile(v.reshape(1, -1), (P, 1))
    col = lambda v: v.reshape(-1, 1)
    qkv, bias = i["L1_attn_Wqkv_w"], i["L1_attn_Wqkv_b"]
    per_head = lambda a: a.reshape(P, HD)
    e_rows = lambda a: a.reshape(EXPERTS * EXPERT_HID, P)
    down = np.concatenate([i["L1_ffn_We_down"].transpose(0, 2, 1).reshape(-1, P), i["L1_ffn_Ws_down"].T], 0)
    return {
        "a_wq": i["L0_attn_Wq"].T, "a_wk": i["L0_attn_Wk"].T, "a_wv": i["L0_attn_Wv"].T, "a_wo": i["L0_attn_Wo"].T,
        "b_wq": i["L0_ffn_Wq"], "b_wk": i["L0_ffn_Wk"], "b_wv": i["L0_ffn_Wv"],
        "b_q2a": i["L0_ffn_Wqa"].T, "b_q2b": i["L0_ffn_Wqb"], "b_k2a": i["L0_ffn_Wka"].T, "b_k2b": i["L0_ffn_Wkb"],
        "b_g1a": i["L0_ffn_Wg1a"].T, "b_g1b": i["L0_ffn_Wg1b"], "b_g2a": i["L0_ffn_Wg2a"].T, "b_g2b": i["L0_ffn_Wg2b"],
        "b_ga": i["L0_ffn_Wga"].T, "b_gb": i["L0_ffn_Wgb"],
        "b_bg1": every(i["L0_ffn_bg1"]), "b_bg2": every(i["L0_ffn_bg2"]),
        "b_we": i["L0_ffn_We"], "b_norm": col(np.tile(i["L0_ffn_norm_w"], 2)), "b_wo": rows(i["L0_ffn_Wo"]),
        "c_wq": qkv[:, 0:P], "c_wk": qkv[:, P:2 * P], "c_wv": qkv[:, 2 * P:],
        "c_bq": col(bias[0:P]), "c_bk": col(bias[P:2 * P]), "c_bv": col(bias[2 * P:]), "c_bv_row": every(bias[2 * P:]),
        "c_lambda": per_head(i["L1_attn_Lambda_raw"]), "c_gamma": per_head(i["L1_attn_Gamma"]),
        "c_static": per_head(i["L1_attn_W_static"]),
        "c_gw1": i["L1_attn_gate_w1"], "c_gb1": col(i["L1_attn_gate_b1"]),
        "c_gw2": np.concatenate([i["L1_attn_gate_w2"], i["L1_attn_gate_b2"].reshape(1, -1)], 0),
        "c_wo": i["L1_attn_out_w"], "c_bo_row": every(i["L1_attn_out_b"]),
        "d_wg": np.concatenate([i["L1_ffn_Wg"], i["L1_ffn_Wsg"]], 0).T,
        "d_gate": np.concatenate([e_rows(i["L1_ffn_We_gate"]), i["L1_ffn_Ws_gate"]], 0).T,
        "d_up": np.concatenate([e_rows(i["L1_ffn_We_up"]), i["L1_ffn_Ws_up"]], 0).T,
        "d_down": rows(down),
    }


def kernel(**inputs):
    import concourse.bacc as _bacc
    from concourse.bass_utils import run_bass_kernel_spmd as _run

    i = {k: np.asarray(v) for k, v in inputs.items()}
    x = np.ascontiguousarray(i["L0_attn_x"])
    packed, place = pack({**constant_columns(), **weight_columns(i)})
    nc = _bacc.Bacc("TRN2", target_bir_lowering=False, num_devices=1)
    x_in = nc.dram_tensor("x_in", x.shape, F32, kind="ExternalInput").ap()
    w_in = {k: nc.dram_tensor(f"w_{k}", a.shape, F32, kind="ExternalInput").ap() for k, a in packed.items()}
    x_out = nc.dram_tensor("x_out", x.shape, F32, kind="ExternalOutput").ap()
    build(nc, x_in, w_in, x_out, place, x.shape[0], x.shape[1])
    r = _run(nc, [{"x_in": x, **{f"w_{k}": a for k, a in packed.items()}}], core_ids=[0])
    return r.results[0]["x_out"]
```
